# Optimizing a Trainium2 kernel written in Bass

```python
import numpy as np
import jax
import jax.numpy as jnp

def _softmax(x, axis=-1):
    return jax.nn.softmax(x, axis=axis)

def _gelu(x):
    return jax.nn.gelu(x, approximate=True)

def _silu(x):
    return jax.nn.silu(x)

def _sigmoid(x):
    return jax.nn.sigmoid(x)

def _layernorm(x, axis=-1, eps=1e-05):
    m = jnp.mean(x, axis=axis, keepdims=True)
    v = jnp.var(x, axis=axis, keepdims=True)
    return (x - m) / jnp.sqrt(v + eps)

def _scatter_add(tgt, idx, src, axis=0):
    return tgt.at[idx].add(src)

def _segment_sum(src, seg, n):
    return jax.ops.segment_sum(src, seg, n)
kernel_name = 'mk_adaln_d1_jaxref_r4_db4fb5'

def setup_inputs(seed: int=0):
    np.random.seed(seed)
    _w = jnp.asarray

    def _L0_attn_setup():
        import jax, jax.numpy as jnp
        import numpy as np
        from jax import lax
        D_MODEL = 256
        N_HEADS = 4
        D_STATE = 64
        D_CONV = 4
        EXPAND = 2
        D_INNER = EXPAND * D_MODEL
        DT_RANK = 64
        H_DIN = D_INNER // N_HEADS
        H_DT = DT_RANK // N_HEADS
        H_DS = D_STATE // N_HEADS
        BATCH, SEQ = (2, 256)
        key = jax.random.key(seed)
        ks = jax.random.split(key, 8)
        hidden_states = jax.random.normal(ks[0], (BATCH, SEQ, D_MODEL), dtype=jnp.float32)
        s_in = 1.0 / np.sqrt(D_MODEL)
        in_proj_w = jax.random.uniform(ks[1], (2 * D_INNER, D_MODEL), minval=-s_in, maxval=s_in)
        s_c = 1.0 / np.sqrt(D_CONV)
        conv_w = jax.random.uniform(ks[2], (D_INNER, 1, D_CONV), minval=-s_c, maxval=s_c)
        conv_b = jax.random.uniform(ks[3], (D_INNER,), minval=-s_c, maxval=s_c)
        s_x = 1.0 / np.sqrt(H_DIN)
        x_proj_w = jax.random.uniform(ks[4], ((2 * H_DS + H_DT) * N_HEADS, H_DIN), minval=-s_x, maxval=s_x)
        s_dt = H_DT ** (-0.5)
        dt_proj_w = jax.random.uniform(ks[5], (D_INNER, H_DT), minval=-s_dt, maxval=s_dt)
        dt = jnp.exp(jax.random.uniform(ks[6], (D_INNER,)) * (np.log(0.1) - np.log(0.001)) + np.log(0.001))
        dt = jnp.clip(dt, 0.0001, None)
        dt_proj_b = dt + jnp.log(-jnp.expm1(-dt))
        A_log = jnp.log(jnp.tile(jnp.arange(1, H_DS + 1, dtype=jnp.float32), (D_INNER, 1)))
        Dskip = jnp.ones((D_INNER,), dtype=jnp.float32)
        out_proj_w = jax.random.uniform(ks[7], (D_MODEL, D_INNER), minval=-s_x, maxval=s_x)
        return {'hidden_states': hidden_states, 'in_proj_w': in_proj_w, 'conv_w': conv_w, 'conv_b': conv_b, 'x_proj_w': x_proj_w, 'dt_proj_w': dt_proj_w, 'dt_proj_b': dt_proj_b, 'A_log': A_log, 'Dskip': Dskip, 'out_proj_w': out_proj_w}
    _L0_attn_in = _L0_attn_setup()

    def _L0_ffn_setup():
        import jax, jax.numpy as jnp
        import numpy as np
        B, S, D, E = (4, 512, 256, 8)
        key = jax.random.key(seed)
        ks = jax.random.split(key, 5)
        s = 0.02
        return {'hidden_states': jax.random.normal(ks[0], (B, S, D), dtype=jnp.float32), 'Wr': jax.random.normal(ks[1], (D, E), dtype=jnp.float32) * s, 'br': jnp.zeros((E,), dtype=jnp.float32), 'W1': jax.random.normal(ks[2], (E, D, 4 * D), dtype=jnp.float32) * s, 'b1': jnp.zeros((E, 4 * D), dtype=jnp.float32), 'W2': jax.random.normal(ks[3], (E, 4 * D, 2 * D), dtype=jnp.float32) * s, 'b2': jnp.zeros((E, 2 * D), dtype=jnp.float32), 'W3': jax.random.normal(ks[4], (E, 2 * D, D), dtype=jnp.float32) * s, 'b3': jnp.zeros((E, D), dtype=jnp.float32)}
    _L0_ffn_in = _L0_ffn_setup()
    _L0_c = _w((lambda *s: np.random.randn(*s).astype(np.float32) * 0.05)(8, 256))
    _L0_wmod = _w((lambda *s: np.random.randn(*s).astype(np.float32) * 0.05)(256, 6 * 256) * 256 ** (-0.5))
    _d = {'L0_attn_hidden_states': _L0_attn_in['hidden_states'], 'L0_attn_in_proj_w': _L0_attn_in['in_proj_w'], 'L0_attn_conv_w': _L0_attn_in['conv_w'], 'L0_attn_conv_b': _L0_attn_in['conv_b'], 'L0_attn_x_proj_w': _L0_attn_in['x_proj_w'], 'L0_attn_dt_proj_w': _L0_attn_in['dt_proj_w'], 'L0_attn_dt_proj_b': _L0_attn_in['dt_proj_b'], 'L0_attn_A_log': _L0_attn_in['A_log'], 'L0_attn_Dskip': _L0_attn_in['Dskip'], 'L0_attn_out_proj_w': _L0_attn_in['out_proj_w'], 'L0_ffn_Wr': _L0_ffn_in['Wr'], 'L0_ffn_br': _L0_ffn_in['br'], 'L0_ffn_W1': _L0_ffn_in['W1'], 'L0_ffn_b1': _L0_ffn_in['b1'], 'L0_ffn_W2': _L0_ffn_in['W2'], 'L0_ffn_b2': _L0_ffn_in['b2'], 'L0_ffn_W3': _L0_ffn_in['W3'], 'L0_ffn_b3': _L0_ffn_in['b3'], 'L0_c': _L0_c, 'L0_wmod': _L0_wmod}
    _x0 = _d['L0_attn_hidden_states']
    _d['L0_attn_hidden_states'] = jax.random.normal(jax.random.fold_in(jax.random.key(seed), 1), (8, 512, 256), dtype=_x0.dtype)
    del _x0
    return _d

def reference(L0_attn_hidden_states, L0_attn_in_proj_w, L0_attn_conv_w, L0_attn_conv_b, L0_attn_x_proj_w, L0_attn_dt_proj_w, L0_attn_dt_proj_b, L0_attn_A_log, L0_attn_Dskip, L0_attn_out_proj_w, L0_ffn_Wr, L0_ffn_br, L0_ffn_W1, L0_ffn_b1, L0_ffn_W2, L0_ffn_b2, L0_ffn_W3, L0_ffn_b3, L0_c, L0_wmod):

    def _L0_attn_ref(hidden_states, in_proj_w, conv_w, conv_b, x_proj_w, dt_proj_w, dt_proj_b, A_log, Dskip, out_proj_w):
        import jax, jax.numpy as jnp
        import numpy as np
        from jax import lax
        D_MODEL = 256
        N_HEADS = 4
        D_STATE = 64
        D_CONV = 4
        EXPAND = 2
        D_INNER = EXPAND * D_MODEL
        DT_RANK = 64
        H_DIN = D_INNER // N_HEADS
        H_DT = DT_RANK // N_HEADS
        H_DS = D_STATE // N_HEADS
        BATCH, SEQ = (2, 256)
        b, L, _ = hidden_states.shape
        xz = hidden_states @ in_proj_w.T
        x, z = jnp.split(xz, 2, axis=-1)
        xp = jnp.pad(x, ((0, 0), (D_CONV - 1, 0), (0, 0)))
        w = conv_w[:, 0, :]
        xc = conv_b
        for k in range(D_CONV):
            xc = xc + xp[:, k:k + L, :] * w[:, k]
        x = jax.nn.silu(xc)
        xh = x.reshape(b, L, N_HEADS, H_DIN)
        xw = x_proj_w.reshape(N_HEADS, 2 * H_DS + H_DT, H_DIN)
        x_dbl = jnp.einsum('hod,blhd->blho', xw, xh)
        dt_r, Bm, Cm = jnp.split(x_dbl, [H_DT, H_DT + H_DS], axis=-1)
        dtw = dt_proj_w.reshape(N_HEADS, H_DIN, H_DT)
        delta = jnp.einsum('hdr,blhr->blhd', dtw, dt_r)
        delta = jax.nn.softplus(delta + dt_proj_b.reshape(N_HEADS, H_DIN))
        A = -jnp.exp(A_log).reshape(N_HEADS, H_DIN, H_DS)

        def step(s, inp):
            d_t, u_t, B_t, C_t = inp
            dA = jnp.exp(d_t[..., None] * A)
            s = s * dA + (d_t * u_t)[..., None] * B_t[:, :, None, :]
            y_t = jnp.einsum('bhdn,bhn->bhd', s, C_t)
            return (s, y_t)
        s0 = jnp.zeros((b, N_HEADS, H_DIN, H_DS), dtype=x.dtype)
        scan_in = (delta.transpose(1, 0, 2, 3), xh.transpose(1, 0, 2, 3), Bm.transpose(1, 0, 2, 3), Cm.transpose(1, 0, 2, 3))
        _, ys = lax.scan(step, s0, scan_in)
        y = ys.transpose(1, 0, 2, 3).reshape(b, L, D_INNER)
        y = y + x * Dskip
        y = y * jax.nn.silu(z)
        out = y @ out_proj_w.T
        return out

    def _L0_ffn_ref(hidden_states, Wr, br, W1, b1, W2, b2, W3, b3):
        import jax, jax.numpy as jnp
        import numpy as np
        B, S, D, E = (4, 512, 256, 8)
        b, s, d = hidden_states.shape
        num_experts = Wr.shape[1]
        x = hidden_states.reshape(-1, d)
        router_logits = x @ Wr + br
        expert_mask = jax.nn.one_hot(jnp.argmax(router_logits, axis=-1), num_experts, dtype=x.dtype)
        out = jnp.zeros_like(x)
        for e in range(num_experts):
            h = jax.nn.gelu(x @ W1[e] + b1[e], approximate=False)
            h = jax.nn.gelu(h @ W2[e] + b2[e], approximate=False)
            y = h @ W3[e] + b3[e]
            out = out + expert_mask[:, e:e + 1] * y
        return out.reshape(b, s, d)
    x = L0_attn_hidden_states
    mod = (_silu(L0_c) @ L0_wmod).reshape(L0_c.shape[0], 6, 1, -1)
    sa, ca, ga, sb, cb, gb = (mod[:, 0], mod[:, 1], mod[:, 2], mod[:, 3], mod[:, 4], mod[:, 5])
    ga = (2 * (ga >= 0) - 1) * jnp.maximum(jnp.abs(ga), 0.25)
    gb = (2 * (gb >= 0) - 1) * jnp.maximum(jnp.abs(gb), 0.25)
    h = _layernorm(x, axis=-1) * (1 + ca) + sa
    x = x + ga * _L0_attn_ref(h, L0_attn_in_proj_w, L0_attn_conv_w, L0_attn_conv_b, L0_attn_x_proj_w, L0_attn_dt_proj_w, L0_attn_dt_proj_b, L0_attn_A_log, L0_attn_Dskip, L0_attn_out_proj_w)
    h = _layernorm(x, axis=-1) * (1 + cb) + sb
    x = x + gb * _L0_ffn_ref(h, L0_ffn_Wr, L0_ffn_br, L0_ffn_W1, L0_ffn_b1, L0_ffn_W2, L0_ffn_b2, L0_ffn_W3, L0_ffn_b3)
    return x

_drawn_inputs = setup_inputs


def setup_inputs(seed=0):
    import zlib

    import numpy as np

    out = dict(_drawn_inputs(seed))
    spreads = {'L0_attn_Dskip': (1.0, 0.6),
     'L0_ffn_br': (0.0, 0.359),
     'L0_ffn_b1': (0.0, 2.0),
     'L0_ffn_b2': (0.0, 2.0),
     'L0_ffn_b3': (0.0, 2.0)}
    factors = {'L0_attn_conv_w': 2.939,
     'L0_attn_conv_b': 3.797,
     'L0_attn_x_proj_w': 8.0,
     'L0_attn_dt_proj_w': 8.0,
     'L0_attn_dt_proj_b': 8.0,
     'L0_attn_A_log': 8.0,
     'L0_ffn_W1': 8.0,
     'L0_ffn_W2': 8.0,
     'L0_ffn_W3': 6.293}
    for name, (base, spread) in spreads.items():
        noise = np.random.default_rng([zlib.crc32(name.encode()), seed]).standard_normal(out[name].shape)
        drawn = base * np.exp(spread * noise) if base else spread * noise
        out[name] = jnp.asarray(drawn.astype(out[name].dtype))
    for name, factor in factors.items():
        out[name] = (out[name] * factor).astype(out[name].dtype)
    return out
```

```python
from contextlib import ExitStack

import concourse.bass as bass
from concourse import mybir

F32 = mybir.dt.float32
BF16 = mybir.dt.bfloat16
I32 = mybir.dt.int32
U32 = mybir.dt.uint32
ALU = mybir.AluOpType
ACT = mybir.ActivationFunctionType
AX_X = mybir.AxisListType.X

P = 128
EPS = 1e-5
EXP_LN = "natural_log_exp_and_others"


def build(nc, x_in, in_wT, conv_w, conv_b, xp_wT, dt_wT, dt_b, a_log, d_skip, out_wT,
          wr, br, w1, b12, w2, w3, b3, cT, wmod, out):
    B, L, D = x_in.shape
    H = 4
    NS = a_log.shape[2]
    TT = L // P
    DC = D // P
    KC = conv_w.shape[2]
    CS = KC - 1
    NP = NS // 2
    DTR = dt_wT.shape[0]
    E = wr.shape[2]
    DT0 = 32
    MID, LOW = 64, 96
    NT = B * TT
    BLK_BITS = 8
    BLK = 1 << BLK_BITS
    NB = (NT * P + E * (BLK - 1)) // BLK

    mod_d = nc.dram_tensor("mod_rows", (B, 4, D), F32).ap()
    x2_d = nc.dram_tensor("x2_rows", (NT * P, D), F32).ap()
    h2_d = nc.dram_tensor("h2_rows", (NT * P, D), F32).ap()
    hs_d = nc.dram_tensor("h2_slots", (NB * BLK, D), F32).ap()
    ys_d = nc.dram_tensor("y_slots", (NB * BLK, D), F32).ap()

    with ExitStack() as outer:
        def keep(name, shape, dt):
            return outer.enter_context(nc.sbuf_tensor(name, shape, dt))

        def sem(name):
            return outer.enter_context(nc.semaphore(name))

        def wait(eng, s, v):
            if not (isinstance(v, int) and v <= 0):
                eng.wait_ge(s, v)

        logits = keep("logits", [P, NT, E], F32)
        ident = keep("ident", [P, P], F32)

        with ExitStack() as ctx:
            def sb(name, shape, dt):
                return ctx.enter_context(nc.sbuf_tensor(name, shape, dt))

            def ps(name, shape, dt=F32):
                return ctx.enter_context(nc.psum_tensor(name, shape, dt))

            in_w = sb("in_w", [P, DC, 2 * H * P], F32)
            xp_w = sb("xp_w", [P, H, P], F32)
            dt_w = sb("dt_w", [P, H * P], F32)
            out_w = sb("out_w", [P, H, D], F32)
            cw = sb("cw", [P, H, KC], F32)
            cb = sb("cb", [P, H], F32)
            dtb = sb("dtb", [P, H], F32)
            dsk = sb("dsk", [P, H], F32)
            a_neg = sb("a_neg", [P, H, NS], F32)
            wr_sb = sb("wr_sb", [P, DC, E], F32)
            br_bc = sb("br_bc", [P, E], F32)
            sel = sb("sel", [P, 2 * NS, P], BF16)
            c_sb = sb("c_sb", [P, DC, B], F32)
            sh_pp = sb("sh_pp", [P, DC, B], F32)
            sc_pp = sb("sc_pp", [P, DC, B], F32)
            psB = ps("psB", [P, 2, L])
            psC = ps("psC", [P, 2, L])
            psY = ps("psY", [P, 2, L])
            psG = ps("psG", [P, 2, L])

            s_par = sem("s_par")
            s_small = sem("s_small")
            s_wload = sem("s_wload")
            s_zero = sem("s_zero")
            s_const = sem("s_const")
            s_cact = sem("s_cact")
            s_aexp = sem("s_aexp")
            s_aneg = sem("s_aneg")
            s_modps = sem("s_modps")
            s_modrow = sem("s_modrow")
            s_guard = sem("s_guard")
            s_modst = sem("s_modst")
            s_zrow = sem("s_zrow")
            s_zst = sem("s_zst")

            with nc.sbuf_tensor("wm", [P, DC, 6 * D], F32) as wm, \
                    nc.sbuf_tensor("modr", [B, 4, D], F32) as modr, \
                    nc.sbuf_tensor("sgn", [B, 2, D], F32) as sgn, \
                    nc.sbuf_tensor("mag", [B, 2, D], F32) as mag, \
                    nc.sbuf_tensor("zrow", [P, D], F32) as zrow, \
                    nc.sbuf_tensor("aex", [P, H, NS], F32) as aex, \
                    nc.Block() as block:
                small = [(c_sb[:], cT), (aex[:], a_log), (cw[:], conv_w), (cb[:], conv_b), (dtb[:], dt_b),
                         (dsk[:], d_skip), (wr_sb[:], wr), (br_bc[:], br.partition_broadcast(P))]

                @block.sync
                def _(sp):
                    sp.dma_start(wm[:], wmod.rearrange("(c p) n -> p c n", p=P)).then_inc(s_wload, 16)
                    for dst, src in small:
                        sp.dma_start(dst, src).then_inc(s_small, 16)
                    sp.dma_start(in_w[:], in_wT.rearrange("(c p) n -> p c n", p=P)).then_inc(s_par, 16)
                    sp.dma_start(dt_w[DT0:DT0 + DTR, :], dt_wT).then_inc(s_par, 16)
                    sp.dma_start(out_w[:], out_wT.rearrange("(h p) n -> p h n", p=P)).then_inc(s_par, 16)
                    sp.wait_ge(s_zero, 1)
                    for at in (0, MID, LOW):
                        sp.dma_start(xp_w[:, :, at:at + 2 * NS], xp_wT[:, :, DTR:]).then_inc(s_par, 16)
                    sp.dma_start(xp_w[:, :, DT0:DT0 + DTR], xp_wT[:, :, 0:DTR]).then_inc(s_par, 16)
                    sp.wait_ge(s_modrow, 6)
                    sp.dma_start(mod_d, modr[:]).then_inc(s_modst, 16)
                    sp.wait_ge(s_modst, 16)
                    sp.wait_ge(s_zrow, 1)
                    sp.dma_start(hs_d.rearrange("(n p) d -> p n d", p=P),
                                 zrow[:].rearrange("p (a d) -> p a d", a=1).broadcast_to([P, NB * BLK // P, D])
                                 ).then_inc(s_zst, 16)
                    sp.wait_ge(s_zst, 16)
                    sp.wait_ge(s_par, 16 * 7)
                    sp.wait_ge(s_small, 16 * len(small))

                @block.gpsimd
                def _(pool):
                    pool.memset(xp_w[:], 0.0).then_inc(s_zero, 1)
                    pool.memset(zrow[:], 0.0).then_inc(s_zrow, 1)
                    pool.memset(ident[:], 0.0).then_inc(s_const, 1)
                    pool.memset(sel[:], 0.0).then_inc(s_const, 1)
                    pool.wait_ge(s_const, 2)
                    pool.affine_select(out=ident[:], in_=ident[:], compare_op=ALU.not_equal, fill=1.0, base=0,
                                       pattern=[[-1, P]], channel_multiplier=1).then_inc(s_const, 1)
                    for k, at in enumerate((0, MID, LOW)):
                        pool.affine_select(out=sel[:], in_=sel[:], compare_op=ALU.not_equal, fill=1.0, base=-at,
                                           pattern=[[-1, 2 * NS], [0, P]], channel_multiplier=1).then_inc(s_const, 1)
                        pool.wait_ge(s_const, 4 + k)

                @block.scalar
                def _(act):
                    act.wait_ge(s_small, 16 * len(small))
                    act.activation(c_sb[:], c_sb[:], ACT.Silu).then_inc(s_cact, 1)
                    act.activation(aex[:], aex[:], ACT.Exp).then_inc(s_aexp, 1)

                @block.tensor
                def _(pe):
                    pe.wait_ge(s_wload, 16)
                    pe.wait_ge(s_cact, 1)
                    for j in range(2 * DC):
                        for c in range(DC):
                            mm = pe.matmul(psG[:, 0, j * B:(j + 1) * B], wm[:, c, j * P:(j + 1) * P], c_sb[:, c, :],
                                           start=(c == 0), stop=(c == DC - 1))
                    mm.then_inc(s_modps, 1)
                    for j in range(2):
                        for c in range(DC):
                            mm = pe.matmul(psY[0:B, j, :], c_sb[:, c, :], wm[:, c, (2 + 2 * j) * D:(4 + 2 * j) * D],
                                           start=(c == 0), stop=(c == DC - 1))
                    mm.then_inc(s_modps, 1)

                @block.vector
                def _(dve):
                    dve.wait_ge(s_aexp, 1)
                    dve.tensor_scalar(a_neg[:], aex[:], -1.0, None, ALU.mult).then_inc(s_aneg, 1)
                    dve.wait_ge(s_modps, 2)
                    pp = psG[:, 0, 0:2 * DC * B].rearrange("p (k c b) -> p k c b", k=2, c=DC)
                    dve.tensor_copy(sh_pp[:], pp[:, 0]).then_inc(s_modrow, 1)
                    dve.tensor_scalar(sc_pp[:], pp[:, 1], 1.0, None, ALU.add).then_inc(s_modrow, 1)
                    gates = [psY[0:B, 0, 0:D], psY[0:B, 1, D:2 * D]]
                    for k in range(2):
                        dve.tensor_copy(mag[:, k, :], gates[k]).then_inc(s_guard, 1)
                        dve.tensor_scalar(sgn[:, k, :], gates[k], 0.0, 2.0, ALU.is_ge, ALU.mult).then_inc(s_guard, 1)
                        dve.wait_ge(s_guard, 4 * k + 2)
                        dve.tensor_scalar(sgn[:, k, :], sgn[:, k, :], 1.0, None, ALU.subtract).then_inc(s_guard, 1)
                        dve.scalar_tensor_tensor(out=mag[:, k, :], in0=mag[:, k, :], scalar=-1.0, in1=mag[:, k, :],
                                                 op0=ALU.mult, op1=ALU.max).then_inc(s_guard, 1)
                        dve.wait_ge(s_guard, 4 * k + 4)
                        dve.scalar_tensor_tensor(out=modr[:, 3 * k, :], in0=mag[:, k, :], scalar=0.25,
                                                 in1=sgn[:, k, :], op0=ALU.max, op1=ALU.mult).then_inc(s_modrow, 1)
                    dve.tensor_copy(modr[:, 1, :], psY[0:B, 0, D:2 * D]).then_inc(s_modrow, 1)
                    dve.tensor_scalar(modr[:, 2, :], psY[0:B, 1, 0:D], 1.0, None, ALU.add).then_inc(s_modrow, 1)

            xa = sb("xa", [P, TT, D], F32)
            xr = sb("xr", [P, TT, D], F32)
            mbc = sb("mbc", [P, 4, D], F32)
            xn = sb("xn", [P, TT, D], F32)
            xn2 = sb("xn2", [P, TT, D], F32)
            x2b = sb("x2b", [P, TT, D], F32)
            h2n = sb("h2n", [P, TT, D], F32)
            st1 = sb("st1", [P, TT, 6], F32)
            mv1 = sb("mv1", [P, TT, 2], F32)
            rs1 = sb("rs1", [P, 4, TT], F32)
            st2 = sb("st2", [P, TT, 6], F32)
            mv2 = sb("mv2", [P, TT, 2], F32)
            rs2 = sb("rs2", [P, 4, TT], F32)
            hT = sb("hT", [P, DC, L], F32)
            h2T = sb("h2T", [P, DC, L], F32)
            cv = sb("cv", [P, L], F32)
            tap = sb("tap", [P, KC, KC - 1 + L], F32)
            u = sb("u", [P, 2, L], F32)
            zs = sb("zs", [P, 2, L], F32)
            xds = sb("xds", [P, L], F32)
            bc3 = sb("bc3", [P, 2, L], BF16)
            bcr = sb("bcr", [P, L], F32)
            sp_a = sb("sp_a", [P, L], F32)
            sp_r = sb("sp_r", [P, L], F32)
            sp_e = sb("sp_e", [P, L], F32)
            sp_l = sb("sp_l", [P, L], F32)
            sp_w = sb("sp_w", [P, L], F32)
            delta = sb("delta", [P, 2, L], F32)
            du = sb("du", [P, 2, L], F32)
            dA = sb("dA", [P, 4, L], F32)
            dBu = sb("dBu", [P, 2, 2, L], F32)
            st = sb("st", [P, 2, 2, L], F32)
            cbr = sb("cbr", [P, 2, 2, L], F32)
            sc = sb("sc", [P, 2, 2, L], F32)
            ytmp = sb("ytmp", [P, L], F32)
            yT = sb("yT", [P, H, L], F32)

            d_xa = sem("d_xa")
            d_xr = sem("d_xr")
            d_mbc = sem("d_mbc")
            d_x2 = sem("d_x2")
            d_h2 = sem("d_h2")
            s_st1 = sem("s_st1")
            s_mv1 = sem("s_mv1")
            s_ve1 = sem("s_ve1")
            s_rg1 = sem("s_rg1")
            s_rs1 = sem("s_rs1")
            s_xn1 = sem("s_xn1")
            s_t1 = sem("s_t1")
            s_hT = sem("s_hT")
            s_padz = sem("s_padz")
            s_xin = sem("s_xin")
            s_xpad = sem("s_xpad")
            s_conv = sem("s_conv")
            s_u = sem("s_u")
            s_zin = sem("s_zin")
            s_zs = sem("s_zs")
            s_xd = sem("s_xd")
            s_cast = sem("s_cast")
            s_xds = sem("s_xds")
            s_split = sem("s_split")
            s_dtp = sem("s_dtp")
            s_spa = sem("s_spa")
            s_spr = sem("s_spr")
            s_spe = sem("s_spe")
            s_spl = sem("s_spl")
            s_delta = sem("s_delta")
            s_w = sem("s_w")
            s_ln = sem("s_ln")
            s_du = sem("s_du")
            s_B = sem("s_B")
            s_C = sem("s_C")
            s_cev = sem("s_cev")
            s_mulB = sem("s_mulB")
            s_scan = sem("s_scan")
            s_prod = sem("s_prod")
            s_sum = sem("s_sum")
            s_dA = sem("s_dA")
            s_ytmp = sem("s_ytmp")
            s_y = sem("s_y")
            s_out = sem("s_out")
            s_gated = sem("s_gated")
            s_x2 = sem("s_x2")
            s_st2 = sem("s_st2")
            s_mv2 = sem("s_mv2")
            s_ve2 = sem("s_ve2")
            s_rg2 = sem("s_rg2")
            s_rs2 = sem("s_rs2")
            s_xn2 = sem("s_xn2")
            s_mod2 = sem("s_mod2")
            s_h2 = sem("s_h2")
            s_t2 = sem("s_t2")
            s_h2T = sem("s_h2T")
            s_rt = sem("s_rt")
            s_lg = sem("s_lg")

            x_v = x_in.rearrange("b (t p) d -> b p t d", p=P)
            x2_v = x2_d.rearrange("(b t p) d -> b p t d", t=TT, p=P)
            h2_v = h2_d.rearrange("(b t p) d -> b p t d", t=TT, p=P)

            def batches(eng, body):
                body(0, True, False)
                with eng.Fori(1, B - 1) as b:
                    body(b, False, False)
                body(B - 1, False, True)

            def of_batch(view, b):
                return view[bass.ds(b, 1)].rearrange("a p t d -> (a p) t d")

            with nc.Block() as block:
                @block.sync
                def _(sp):
                    def load_tokens(b):
                        wait(sp, s_xn1, b * TT)
                        sp.dma_start(xa[:], of_batch(x_v, b)).then_inc(d_xa, 16)

                    def load_tail(b):
                        wait(sp, s_x2, b * 2)
                        sp.dma_start(xr[:], of_batch(x_v, b)).then_inc(d_xr, 16)
                        wait(sp, s_h2, b)
                        sp.dma_start(mbc[:].rearrange("p k d -> p (k d)"),
                                     mod_d[bass.ds(b, 1)].rearrange("a k d -> (a k d)").partition_broadcast(P)
                                     ).then_inc(d_mbc, 16)

                    def store_tail(b):
                        wait(sp, s_x2, (b + 1) * 2)
                        sp.dma_start(of_batch(x2_v, b), x2b[:]).then_inc(d_x2, 16)
                        wait(sp, s_h2, b + 1)
                        sp.dma_start(of_batch(h2_v, b), h2n[:]).then_inc(d_h2, 16)

                    def body(b, first, last):
                        if not first:
                            load_tail(b - 1)
                        if not last:
                            load_tokens(b + 1)
                        if not first:
                            store_tail(b - 1)
                    load_tokens(0)
                    batches(sp, body)
                    load_tail(B - 1)
                    store_tail(B - 1)
                    sp.wait_ge(d_x2, 16 * B)
                    sp.wait_ge(d_h2, 16 * B)

                @block.tensor
                def _(pe):
                    def xin_mm(v, h):
                        wait(pe, s_xds, v)
                        for c in range(DC):
                            mm = pe.matmul(psG[:, 0, :], in_w[:, c, h * P:(h + 1) * P], hT[:, c, :],
                                           start=(c == 0), stop=(c == DC - 1))
                        mm.then_inc(s_xin, 1)

                    def zin_mm(v, h):
                        wait(pe, s_spr, v)
                        for c in range(DC):
                            mm = pe.matmul(psG[:, 1, :], in_w[:, c, (H + h) * P:(H + h + 1) * P], hT[:, c, :],
                                           start=(c == 0), stop=(c == DC - 1))
                        mm.then_inc(s_zin, 1)

                    def xdbl_mm(v, h):
                        wait(pe, s_xpad, v + 1)
                        wait(pe, s_u, v + 1)
                        pe.matmul(psG[:, 0, :], xp_w[:, h, :], u[:, h % 2, :], start=True, stop=True).then_inc(s_xd, 1)

                    def dt_mm(v, h):
                        wait(pe, s_zs, v + 1)
                        wait(pe, s_xds, v + 1)
                        pe.matmul(psG[:, 1, :], dt_w[DT0:DT0 + DTR, h * P:(h + 1) * P], xds[DT0:DT0 + DTR, :],
                                  start=True, stop=True).then_inc(s_dtp, 1)

                    def out_mm(b, k):
                        for t in (2 * k, 2 * k + 1):
                            for h in range(H):
                                mm = pe.matmul(psG[:, 0, (t % 2) * D:(t % 2 + 1) * D], yT[:, h, t * P:(t + 1) * P],
                                               out_w[:, h, :], start=(h == 0), stop=(h == H - 1))
                        mm.then_inc(s_out, 1)

                    def turn(src, c, done):
                        for t in range(TT):
                            mm = pe.transpose(psG[:, 0, t * P:(t + 1) * P], src[:, t, c * P:(c + 1) * P], ident[:])
                        mm.then_inc(done, 1)

                    def router_mm(b):
                        wait(pe, s_h2T, (b + 1) * DC)
                        for t in range(TT):
                            for c in range(DC):
                                mm = pe.matmul(psG[:, 1, t * E:(t + 1) * E], h2T[:, c, t * P:(t + 1) * P],
                                               wr_sb[:, c, :], start=(c == 0), stop=(c == DC - 1))
                        mm.then_inc(s_rt, 1)

                    def broadcast(q, h, g):
                        p = q * NP + g
                        if g == 0:
                            wait(pe, s_split, (q + 1) * 3)
                        wait(pe, s_mulB, p)
                        for i in range(2):
                            mm = pe.matmul(psB[:, i, :], sel[:, 2 * g + i, :], bc3[:, h % 2, :], start=True, stop=True)
                        mm.then_inc(s_B, 1)
                        wait(pe, s_cev, p)
                        for i in range(2):
                            mm = pe.matmul(psC[:, i, :], sel[:, NS + 2 * g + i, :], bc3[:, h % 2, :],
                                           start=True, stop=True)
                        mm.then_inc(s_C, 1)

                    def sums(q, h, g):
                        if g == 0:
                            wait(pe, s_y, q - 1)
                        wait(pe, s_prod, q * NP + g + 1)
                        for i in range(2):
                            mm = pe.matmul(psY[:, h % 2, :], ident[:], sc[:, g % 2, i, :],
                                           start=(g == 0 and i == 0), stop=(g == NP - 1 and i == 1))
                        mm.then_inc(s_sum, 1)

                    def guest(b, h, k, first, last):
                        if h == 0 and not first:
                            if k == 0:
                                wait(pe, s_y, b * H)
                            wait(pe, s_gated, (b - 1) * 2 + k)
                            out_mm(b - 1, k)
                        if h == 1 and not first:
                            wait(pe, s_h2, b)
                            wait(pe, s_h2T, (b - 1) * DC + k)
                            turn(h2n, k, s_t2)
                        if h == 2 and not last:
                            wait(pe, s_xn1, (b + 2) * TT)
                            wait(pe, s_hT, (b + 1) * DC + k)
                            turn(xn, k, s_t1)

                    def unit(b, h, first, last):
                        q = b * H + h
                        v = q + 1
                        vh = (h + 1) % H
                        prep = not (last and h == H - 1)
                        guests = (h == 0 and not first) or (h == 1 and not first) or (h == 2 and not last)
                        for g in range(NP):
                            broadcast(q, h, g)
                            if g > 0:
                                sums(q, h, g - 1)
                            elif not (first and h == 0):
                                sums(q - 1, (h + 1) % 2, NP - 1)
                            if g == 0 and prep:
                                if h == H - 1:
                                    wait(pe, s_hT, (b + 2) * DC)
                                xin_mm(v, vh)
                            if g == 2 and prep:
                                if h == 2 and not first:
                                    wait(pe, s_lg, b)
                                zin_mm(v, vh)
                            if g in (2, 3) and guests:
                                if g == 2:
                                    wait(pe, s_xpad, v + 1)
                                guest(b, h, g - 2, first, last)
                            if g == 4 and prep:
                                if h == 0 and not first:
                                    wait(pe, s_gated, b * 2)
                                if h == 1 and not first:
                                    wait(pe, s_h2T, b * DC)
                                if h == 2 and not last:
                                    wait(pe, s_hT, (b + 2) * DC)
                                xdbl_mm(v, vh)
                                dt_mm(v, vh)
                            if g == 7 and h == 1 and not first:
                                wait(pe, s_spr, v + 1)
                                router_mm(b - 1)

                    for c in range(DC):
                        wait(pe, s_xn1, TT)
                        wait(pe, s_hT, c)
                        turn(xn, c, s_t1)
                    wait(pe, s_hT, DC)
                    xin_mm(0, 0)
                    zin_mm(0, 0)
                    xdbl_mm(0, 0)
                    dt_mm(0, 0)

                    def body(b, first, last):
                        for h in range(H):
                            unit(b, h, first, last)
                    batches(pe, body)
                    sums(B * H - 1, H - 1, NP - 1)
                    wait(pe, s_y, B * H)
                    for k in range(2):
                        wait(pe, s_gated, (B - 1) * 2 + k)
                        out_mm(B - 1, k)
                    wait(pe, s_h2, B)
                    wait(pe, s_gated, B * 2)
                    for k in range(2):
                        wait(pe, s_h2T, (B - 1) * DC + k)
                        turn(h2n, k, s_t2)
                    router_mm(B - 1)

                @block.scalar
                def _(act):
                    def x_copy(v, h):
                        wait(act, s_xin, v + 1)
                        wait(act, s_conv, v * CS)
                        for k in range(KC):
                            last = act.activation(tap[:, k, KC - 1:], psG[:, 0, :], ACT.Copy, scale=cw[:, h, k:k + 1])
                        last.then_inc(s_xpad, 1)

                    def silus(v, h):
                        wait(act, s_conv, (v + 1) * CS)
                        wait(act, s_y, v - 1)
                        act.activation(u[:, h % 2, :], cv[:], ACT.Silu, bias=cb[:, h:h + 1]).then_inc(s_u, 1)
                        wait(act, s_zin, v + 1)
                        act.activation(zs[:, h % 2, :], psG[:, 1, :], ACT.Silu).then_inc(s_zs, 1)
                        act.preload_act_table_set(EXP_LN)

                    def xd_copy(v, h):
                        wait(act, s_xd, v + 1)
                        wait(act, s_C, (v - 1) * NP)
                        act.activation(bc3[:, h % 2, :], psG[:, 0, :], ACT.Copy).then_inc(s_cast, 1)
                        wait(act, s_split, v * 3)
                        wait(act, s_dtp, v)
                        act.activation(xds[:], psG[:, 0, :], ACT.Copy).then_inc(s_xds, 1)

                    def softplus(v, h):
                        wait(act, s_dtp, v + 1)
                        wait(act, s_delta, v * 3)
                        act.activation(sp_a[:], psG[:, 1, :], ACT.Abs, bias=dtb[:, h:h + 1]).then_inc(s_spa, 1)
                        act.activation(sp_r[:], psG[:, 1, :], ACT.Relu, bias=dtb[:, h:h + 1]).then_inc(s_spr, 1)
                        wait(act, s_spa, v + 1)
                        act.activation(sp_e[:], sp_a[:], ACT.Exp, scale=-1.0).then_inc(s_spe, 1)
                        wait(act, s_spe, v + 1)
                        act.activation(sp_l[:], sp_e[:], ACT.Ln, bias=1.0).then_inc(s_spl, 1)

                    def decays(q, h, g):
                        p = q * NP + g
                        if g == 0:
                            wait(act, s_delta, (q + 1) * 3)
                        wait(act, s_scan, p - 1)
                        for i in range(2):
                            n = 2 * g + i
                            act.activation(dA[:, n % 4, :], delta[:, h % 2, :], ACT.Exp,
                                           scale=a_neg[:, h, n:n + 1]).then_inc(s_dA, 1)

                    def c_copy(q, g):
                        p = q * NP + g
                        wait(act, s_C, p + 1)
                        wait(act, s_prod, p - 1)
                        act.activation(cbr[:, g % 2], psC[:], ACT.Copy).then_inc(s_cev, 1)

                    def modulated(b, c):
                        wait(act, s_t1, b * DC + c + 1)
                        act.activation(hT[:, c, :], psG[:, 0, :], ACT.Identity, bias=sh_pp[:, c, bass.ds(b, 1)],
                                       scale=sc_pp[:, c, bass.ds(b, 1)]).then_inc(s_hT, 1)

                    def h2_copy(b, c):
                        wait(act, s_t2, b * DC + c + 1)
                        act.activation(h2T[:, c, :], psG[:, 0, :], ACT.Copy).then_inc(s_h2T, 1)

                    def guess_rstd(b, rs, before, done):
                        wait(act, before, b + 1)
                        act.activation(rs[:, 1, :], rs[:, 0, :], ACT.Ln).then_inc(done, 1)
                        wait(act, done, b * 2 + 1)
                        act.activation(rs[:, 1, :], rs[:, 1, :], ACT.Exp, scale=-0.5).then_inc(done, 1)

                    def unit(b, h, first, last):
                        q = b * H + h
                        v = q + 1
                        vh = (h + 1) % H
                        prep = not (last and h == H - 1)
                        for g in range(NP):
                            decays(q, h, g)
                            c_copy(q, g)
                            if h == 1 and g == 4 and not last:
                                guess_rstd(b + 1, rs1, s_ve1, s_rg1)
                            if h == 0 and g == 6 and not first:
                                guess_rstd(b - 1, rs2, s_ve2, s_rg2)
                            if g == 0 and prep:
                                x_copy(v, vh)
                            if g in (2, 3):
                                if h == 1 and not first:
                                    h2_copy(b - 1, g - 2)
                                if h == 2 and not last:
                                    modulated(b + 1, g - 2)
                            if g == 3 and prep:
                                silus(v, vh)
                            if g == 4 and prep:
                                xd_copy(v, vh)
                                softplus(v, vh)

                    guess_rstd(0, rs1, s_ve1, s_rg1)
                    for c in range(DC):
                        modulated(0, c)
                    wait(act, s_padz, 1)
                    x_copy(0, 0)
                    silus(0, 0)
                    xd_copy(0, 0)
                    softplus(0, 0)

                    def body(b, first, last):
                        for h in range(H):
                            unit(b, h, first, last)
                    batches(act, body)
                    guess_rstd(B - 1, rs2, s_ve2, s_rg2)
                    for c in range(DC):
                        h2_copy(B - 1, c)

                @block.gpsimd
                def _(pool):
                    pool.memset(tap[:, :, 0:KC - 1], 0.0).then_inc(s_padz, 1)

                    def conv(v, h):
                        wait(pool, s_xpad, v + 1)
                        wait(pool, s_u, v)
                        pool.tensor_tensor(cv[:], tap[:, 0, 0:L], tap[:, 1, 1:1 + L], ALU.add).then_inc(s_conv, 1)
                        for k in range(2, KC):
                            wait(pool, s_conv, v * CS + k - 1)
                            pool.tensor_tensor(cv[:], cv[:], tap[:, k, k:k + L], ALU.add).then_inc(s_conv, 1)

                    def split(v, h):
                        wait(pool, s_cast, v + 1)
                        wait(pool, s_xds, v + 1)
                        pool.tensor_tensor(bcr[MID:], xds[MID:], bc3[MID:, h % 2, :], ALU.subtract).then_inc(s_split, 1)
                        wait(pool, s_split, v * 3 + 1)
                        pool.tensor_tensor(bc3[MID:, h % 2, :], xds[MID:], bc3[MID:, h % 2, :],
                                           ALU.subtract).then_inc(s_split, 1)
                        wait(pool, s_split, v * 3 + 2)
                        pool.tensor_tensor(bc3[LOW:, h % 2, :], bcr[LOW:], bc3[LOW:, h % 2, :],
                                           ALU.subtract).then_inc(s_split, 1)
                        wait(pool, s_split, v * 3 + 3)

                    def put_delta(v, h):
                        wait(pool, s_ln, v + 1)
                        pool.tensor_tensor(sp_w[:], sp_e[:], sp_w[:], ALU.subtract).then_inc(s_delta, 1)
                        wait(pool, s_delta, v * 3 + 1)
                        pool.tensor_tensor(sp_w[:], sp_l[:], sp_w[:], ALU.add).then_inc(s_delta, 1)
                        wait(pool, s_spr, v + 1)
                        wait(pool, s_y, v - 1)
                        wait(pool, s_delta, v * 3 + 2)
                        pool.tensor_tensor(delta[:, h % 2, :], sp_w[:], sp_r[:], ALU.add).then_inc(s_delta, 1)

                    def product(q, g):
                        p = q * NP + g
                        wait(pool, s_cev, p + 1)
                        wait(pool, s_scan, p + 1)
                        wait(pool, s_sum, p - 1)
                        pool.tensor_tensor(sc[:, g % 2], st[:, g % 2], cbr[:, g % 2], ALU.mult).then_inc(s_prod, 1)

                    wait(pool, s_padz, 1)
                    conv(0, 0)
                    wait(pool, s_conv, CS)
                    split(0, 0)
                    put_delta(0, 0)

                    def body(b, first, last):
                        for h in range(H):
                            q = b * H + h
                            v = q + 1
                            vh = (h + 1) % H
                            prep = not (last and h == H - 1)
                            for g in range(NP):
                                product(q, g)
                                if g == 0 and prep:
                                    conv(v, vh)
                                if g == 4 and prep:
                                    wait(pool, s_prod, q * NP + g + 1)
                                    split(v, vh)
                                if g == 5 and prep:
                                    put_delta(v, vh)
                    batches(pool, body)

                @block.vector
                def _(dve):
                    def stats(src, out, done):
                        for t in range(TT):
                            dve.bn_stats(out[:, t, :], src[:, t, :]).then_inc(done, 1)

                    def aggregate(b, stat, mv, rs, done_mv, done_ve):
                        for t in range(TT):
                            dve.bn_aggr(mv[:, t, :], stat[:, t, :]).then_inc(done_mv, 1)
                        plus_eps(b, mv, rs, done_mv, done_ve)

                    def plus_eps(b, mv, out, before, done):
                        wait(dve, before, (b + 1) * TT)
                        dve.tensor_scalar(out[:, 0, :], mv[:, :, 1], EPS, None, ALU.add).then_inc(done, 1)

                    def refine(b, rs, guess, done):
                        wait(dve, guess, (b + 1) * 2)
                        for k, (o, x, y) in enumerate(((2, 0, 1), (2, 2, 1))):
                            dve.tensor_tensor(rs[:, o, :], rs[:, x, :], rs[:, y, :], ALU.mult).then_inc(done, 1)
                            wait(dve, done, b * 4 + k + 1)
                        dve.tensor_scalar(rs[:, 2, :], rs[:, 2, :], -0.5, 1.5, ALU.mult, ALU.add).then_inc(done, 1)
                        wait(dve, done, b * 4 + 3)
                        dve.tensor_tensor(rs[:, 3, :], rs[:, 2, :], rs[:, 1, :], ALU.mult).then_inc(done, 1)

                    def centre(b, t, src, mv, rs, dst, before, done):
                        wait(dve, before, (b + 1) * 4)
                        dve.tensor_scalar(dst[:, t, :], src[:, t, :], mv[:, t, 0:1], rs[:, 3, t:t + 1],
                                          ALU.subtract, ALU.mult).then_inc(done, 1)

                    def norm1_stats(b):
                        wait(dve, d_xa, (b + 1) * 16)
                        stats(xa, st1, s_st1)

                    def norm1(b):
                        refine(b, rs1, s_rg1, s_rs1)
                        wait(dve, s_t1, b * DC)
                        for t in range(TT):
                            centre(b, t, xa, mv1, rs1, xn, s_rs1, s_xn1)

                    def residual(b, k):
                        two = slice(2 * k, 2 * k + 2)
                        wait(dve, s_out, b * 2 + k + 1)
                        wait(dve, d_mbc, (b + 1) * 16)
                        wait(dve, d_xr, (b + 1) * 16)
                        wait(dve, d_x2, b * 16)
                        dve.tensor_tensor(x2b[:, two, :], psG[:, 0, :].rearrange("p (t d) -> p t d", t=2),
                                          mbc[:, 0:1, :].broadcast_to([P, 2, D]), ALU.mult).then_inc(s_gated, 1)
                        wait(dve, s_gated, b * 2 + k + 1)
                        dve.tensor_tensor(x2b[:, two, :], x2b[:, two, :], xr[:, two, :], ALU.add).then_inc(s_x2, 1)

                    def norm2_stats(b):
                        wait(dve, s_x2, (b + 1) * 2)
                        stats(x2b, st2, s_st2)

                    def norm2(b):
                        refine(b, rs2, s_rg2, s_rs2)
                        for t in range(TT):
                            centre(b, t, x2b, mv2, rs2, xn2, s_rs2, s_xn2)
                        wait(dve, s_xn2, (b + 1) * TT)
                        dve.tensor_tensor(xn2[:], xn2[:], mbc[:, 2:3, :].broadcast_to([P, TT, D]),
                                          ALU.mult).then_inc(s_mod2, 1)
                        wait(dve, s_mod2, b + 1)
                        wait(dve, s_t2, b * DC)
                        wait(dve, d_h2, b * 16)
                        dve.tensor_tensor(h2n[:], xn2[:], mbc[:, 1:2, :].broadcast_to([P, TT, D]),
                                          ALU.add).then_inc(s_h2, 1)

                    def logits_out(b):
                        wait(dve, s_rt, b + 1)
                        dve.tensor_tensor(logits[:, bass.ds(b * TT, TT), :],
                                          psG[:, 1, 0:TT * E].rearrange("p (t e) -> p t e", t=TT),
                                          br_bc[:].rearrange("p (a e) -> p a e", a=1).broadcast_to([P, TT, E]),
                                          ALU.add).then_inc(s_lg, 1)

                    def rounded(v):
                        wait(dve, s_spe, v + 1)
                        wait(dve, s_delta, v * 3)
                        dve.tensor_scalar(sp_w[:], sp_e[:], 1.0, 1.0, ALU.add, ALU.subtract).then_inc(s_w, 1)
                        wait(dve, s_w, v + 1)
                        wait(dve, s_spl, v + 1)
                        dve.scalar_tensor_tensor(out=sp_l[:], in0=sp_w[:], scalar=0.0, in1=sp_l[:],
                                                 op0=ALU.is_gt, op1=ALU.mult).then_inc(s_ln, 1)

                    def delta_u(v, h):
                        wait(dve, s_delta, (v + 1) * 3)
                        dve.tensor_tensor(du[:, h % 2, :], delta[:, h % 2, :], u[:, h % 2, :],
                                          ALU.mult).then_inc(s_du, 1)

                    def gate(q, h):
                        wait(dve, s_sum, (q + 1) * NP)
                        dve.scalar_tensor_tensor(out=ytmp[:], in0=u[:, h % 2, :], scalar=dsk[:, h:h + 1],
                                                 in1=psY[:, h % 2, :], op0=ALU.mult, op1=ALU.add).then_inc(s_ytmp, 1)
                        wait(dve, s_ytmp, q + 1)
                        dve.tensor_tensor(yT[:, h, :], ytmp[:], zs[:, h % 2, :], ALU.mult).then_inc(s_y, 1)

                    def scans(q, h, g):
                        p = q * NP + g
                        if g == 0:
                            wait(dve, s_du, q + 1)
                        wait(dve, s_B, p + 1)
                        dve.tensor_tensor(dBu[:, g % 2], psB[:], du[:, h % 2:h % 2 + 1, :].broadcast_to([P, 2, L]),
                                          ALU.mult).then_inc(s_mulB, 1)
                        wait(dve, s_mulB, p + 1)
                        wait(dve, s_prod, p - 1)
                        for i in range(2):
                            n = 2 * g + i
                            wait(dve, s_dA, q * NS + n + 1)
                            sc_ = dve.tensor_tensor_scan(out=st[:, g % 2, i, :], data0=dA[:, n % 4, :],
                                                         data1=dBu[:, g % 2, i, :], initial=0.0,
                                                         op0=ALU.mult, op1=ALU.add)
                        sc_.then_inc(s_scan, 1)

                    norm1_stats(0)
                    wait(dve, s_st1, TT)
                    aggregate(0, st1, mv1, rs1, s_mv1, s_ve1)
                    norm1(0)
                    rounded(0)
                    delta_u(0, 0)

                    def body(b, first, last):
                        for h in range(H):
                            q = b * H + h
                            for g in range(NP):
                                if h == 0 and g == 5 and not first:
                                    wait(dve, s_st2, b * TT)
                                if h == 1 and g == 3 and not last:
                                    wait(dve, s_st1, (b + 2) * TT)
                                scans(q, h, g)
                                if h == 0 and g == 5 and not first:
                                    aggregate(b - 1, st2, mv2, rs2, s_mv2, s_ve2)
                                if h == 1 and g == 3 and not last:
                                    aggregate(b + 1, st1, mv1, rs1, s_mv1, s_ve1)
                                if g == 4 and not (last and h == H - 1):
                                    rounded(q + 1)
                                if g == 0 and not (first and h == 0):
                                    if h == 0 and not first:
                                        wait(dve, s_out, (b - 1) * 2)
                                    gate(q - 1, (h + H - 1) % H)
                                if h == 0 and not first:
                                    if g in (2, 3):
                                        residual(b - 1, g - 2)
                                    if g == 4:
                                        norm2_stats(b - 1)
                                    if g == 7:
                                        norm2(b - 1)
                                if h == 1 and g == 2 and not last:
                                    norm1_stats(b + 1)
                                if h == 1 and g == 5 and not last:
                                    norm1(b + 1)
                                if h == 2 and g == 0 and not first:
                                    logits_out(b - 1)
                                if g == 6 and not (last and h == H - 1):
                                    delta_u(q + 1, (h + 1) % H)
                    batches(dve, body)
                    gate(B * H - 1, H - 1)
                    for k in range(2):
                        residual(B - 1, k)
                    norm2_stats(B - 1)
                    wait(dve, s_st2, B * TT)
                    aggregate(B - 1, st2, mv2, rs2, s_mv2, s_ve2)
                    norm2(B - 1)
                    logits_out(B - 1)

        with ExitStack() as ctx:
            def sb(name, shape, dt):
                return ctx.enter_context(nc.sbuf_tensor(name, shape, dt))

            def ps(name, shape, dt=F32):
                return ctx.enter_context(nc.psum_tensor(name, shape, dt))

            mx = sb("mx", [P, NT], F32)
            eq = sb("eq", [P, NT, E], F32)
            hot = sb("hot", [P, NT, E], F32)
            hotb = sb("hotb", [P, NT, E], BF16)
            rank = sb("rank", [P, E], F32)
            before = sb("before", [P, P], BF16)
            ones = sb("ones", [P, P], BF16)
            onesf = sb("onesf", [P, NT], F32)
            run = sb("run", [P, NT, E], F32)
            slot = sb("slot", [P, NT, E], F32)
            padi = sb("padi", [P, E], I32)
            padf = sb("padf", [P, E], F32)
            ends = sb("ends", [P, E], F32)
            offs = sb("offs", [P, E], F32)
            posf = sb("posf", [P, NT], F32)
            pos = sb("pos", [P, NT], U32)
            starts = sb("starts", [1, NB], F32)
            past = sb("past", [1, NB, E], F32)
            expf = sb("expf", [1, NB], F32)
            block_expert = sb("block_expert", [1, NB], I32)
            rows = sb("rows", [P, NT, D], F32)
            x2s = sb("x2s", [P, NT, D], F32)
            psR = ps("psR", [P, 2, NT, E])

            r_const = sem("r_const")
            r_rows = sem("r_rows")
            r_x2 = sem("r_x2")
            r_gb = sem("r_gb")
            r_hot = sem("r_hot")
            r_count = sem("r_count")
            r_step = sem("r_step")
            r_pos = sem("r_pos")
            r_blocks = sem("r_blocks")
            r_scat = sem("r_scat")

            with nc.Block() as block:
                @block.sync
                def _(sp):
                    sp.dma_start(rows[:], h2_d.rearrange("(t p) d -> p t d", p=P)).then_inc(r_rows, 16)
                    sp.dma_start(x2s[:], x2_d.rearrange("(t p) d -> p t d", p=P)).then_inc(r_x2, 16)
                    sp.wait_ge(r_x2, 16)

                @block.gpsimd
                def _(pool):
                    pool.memset(before[:], 1.0).then_inc(r_const, 1)
                    pool.memset(ones[:], 1.0).then_inc(r_const, 1)
                    pool.memset(onesf[:], 1.0).then_inc(r_const, 1)
                    pool.iota(rank[:], pattern=[[-1, E]], base=E, channel_multiplier=0,
                              allow_small_or_imprecise_dtypes=True).then_inc(r_const, 1)
                    pool.iota(starts[:], pattern=[[BLK, NB]], base=0, channel_multiplier=0,
                              allow_small_or_imprecise_dtypes=True).then_inc(r_const, 1)
                    pool.wait_ge(r_const, 5)
                    pool.affine_select(out=before[:], in_=before[:], compare_op=ALU.is_gt, fill=0.0, base=0,
                                       pattern=[[1, P]], channel_multiplier=-1).then_inc(r_const, 1)
                    pool.wait_ge(r_rows, 16)
                    pool.wait_ge(r_pos, 1)
                    for t in range(NT):
                        pool.indirect_dma_start(hs_d, bass.IndirectOffsetOnAxis(ap=pos[:, t:t + 1], axis=0),
                                                rows[:, t, :], None).then_inc(r_scat, 16)
                    pool.wait_ge(r_scat, 16 * NT)

                @block.tensor
                def _(pe):
                    pe.wait_ge(r_const, 6)
                    pe.wait_ge(r_hot, 1)
                    flat = hotb[:].rearrange("p t e -> p (t e)")
                    pe.matmul(psR[:, 0].rearrange("p t e -> p (t e)"), before[:], flat, start=True, stop=True)
                    pe.matmul(psR[:, 1].rearrange("p t e -> p (t e)"), ones[:], flat, start=True,
                              stop=True).then_inc(r_count, 1)

                @block.vector
                def _(dve):
                    steps = [0]

                    def step(ins):
                        steps[0] += 1
                        ins.then_inc(r_step, 1)
                        dve.wait_ge(r_step, steps[0])

                    def per_tile(ap):
                        return ap[:].rearrange("p (t a) -> p t a", a=1).broadcast_to([P, NT, E])

                    def per_expert(ap):
                        return ap[:].rearrange("p (a e) -> p a e", a=1).broadcast_to([P, NT, E])

                    dve.wait_ge(r_const, 5)
                    step(dve.tensor_reduce(mx[:], logits[:], AX_X, ALU.max))
                    step(dve.tensor_tensor(eq[:], logits[:], per_tile(mx), ALU.is_equal))
                    step(dve.tensor_tensor(eq[:], eq[:], per_expert(rank), ALU.mult))
                    step(dve.tensor_reduce(mx[:], eq[:], AX_X, ALU.max))
                    step(dve.tensor_tensor(hot[:], eq[:], per_tile(mx), ALU.is_equal))
                    dve.tensor_copy(hotb[:], hot[:]).then_inc(r_hot, 1)
                    dve.wait_ge(r_count, 1)
                    for e in range(E):
                        last = dve.tensor_tensor_scan(out=run[:, :, e], data0=onesf[:], data1=psR[:, 1, :, e],
                                                      initial=0.0, op0=ALU.mult, op1=ALU.add)
                    step(last)
                    step(dve.tensor_scalar(padi[:], run[:, NT - 1, :], float(BLK - 1), None, ALU.add))
                    step(dve.tensor_scalar(padi[:], padi[:], BLK_BITS, BLK_BITS, ALU.arith_shift_right,
                                           ALU.arith_shift_left))
                    step(dve.tensor_copy(padf[:], padi[:]))
                    step(dve.tensor_tensor_scan(out=ends[:], data0=onesf[:, 0:E], data1=padf[:], initial=0.0,
                                                op0=ALU.mult, op1=ALU.add))
                    step(dve.tensor_tensor(offs[:], ends[:], padf[:], ALU.subtract))
                    step(dve.tensor_tensor(slot[:], run[:], psR[:, 1], ALU.subtract))
                    step(dve.tensor_tensor(slot[:], slot[:], psR[:, 0], ALU.add))
                    step(dve.tensor_tensor(slot[:], slot[:], per_expert(offs), ALU.add))
                    step(dve.tensor_tensor(slot[:], slot[:], hot[:], ALU.mult))
                    step(dve.tensor_reduce(posf[:], slot[:], AX_X, ALU.add))
                    dve.tensor_copy(pos[:], posf[:]).then_inc(r_pos, 1)
                    step(dve.tensor_tensor(past[:], starts[:].rearrange("p (b a) -> p b a", a=1).broadcast_to([1, NB, E]),
                                           ends[0:1, :].rearrange("p (a e) -> p a e", a=1).broadcast_to([1, NB, E]),
                                           ALU.is_ge))
                    step(dve.tensor_reduce(expf[:], past[:], AX_X, ALU.add))
                    dve.tensor_scalar(block_expert[:], expf[:], float(E - 1), None, ALU.min).then_inc(r_blocks, 1)

            F1, F2 = w1.shape[2], w2.shape[2]
            M1, M2 = F1 // P, F2 // P
            RT = BLK // P
            w1s = sb("w1s", [P, DC, F1], F32)
            w2s = sb("w2s", [P, M1, F2], F32)
            w3s = sb("w3s", [P, M2, D], F32)
            b12s = sb("b12s", [P, M1 + M2], F32)
            b3s = sb("b3s", [P, D], F32)
            hrow = sb("hrow", [P, RT, D], F32)
            hsT = sb("hsT", [P, DC, BLK], F32)
            g1 = sb("g1", [P, M1, BLK], F32)
            g2 = sb("g2", [P, M2, BLK], F32)
            yrow = sb("yrow", [P, RT, D], F32)
            psT = ps("psT", [P, DC, BLK])
            ps1 = ps("ps1", [P, 2, 2, BLK])
            ps2 = ps("ps2", [P, M2, L])
            ps3 = psR[:].rearrange("p k t e -> p (k t e)").rearrange("p (r d) -> p r d", r=RT)

            f_h = sem("f_h")
            f_w1 = sem("f_w1")
            f_w2 = [sem(f"f_w2_{k}") for k in range(2)]
            f_w3 = sem("f_w3")
            f_b12 = sem("f_b12")
            f_b3 = sem("f_b3")
            f_t = sem("f_t")
            f_hT = sem("f_hT")
            f_l1 = sem("f_l1")
            f_g1 = sem("f_g1")
            f_k2 = sem("f_k2")
            f_l2 = sem("f_l2")
            f_g2 = sem("f_g2")
            f_l3 = sem("f_l3")
            f_y = sem("f_y")
            f_st = sem("f_st")

            w1_v = w1.rearrange("e (c p) n -> e p c n", p=P)
            w2_v = w2.rearrange("e (c p) n -> e p c n", p=P)
            w3_v = w3.rearrange("e (c p) n -> e p c n", p=P)
            hs_v = hs_d.rearrange("(j r p) d -> j p r d", r=RT, p=P)
            ys_v = ys_d.rearrange("(j r p) d -> j p r d", r=RT, p=P)

            def one(view, i):
                return view[bass.ds(i, 1)].rearrange("a p c n -> (a p) c n")

            def blocks(eng, body):
                body(0)
                with eng.Fori(1, NB) as j:
                    body(j)

            half = M1 // 2
            with nc.Block() as block:
                @block.sync
                def _(sp):
                    def body(j):
                        e = sp.value_load(block_expert[0:1, bass.ds(j, 1)], min_val=0, max_val=E - 1)
                        wait(sp, f_t, j)
                        sp.dma_start(hrow[:], one(hs_v, j)).then_inc(f_h, 16)
                        wait(sp, f_l1, j * (M1 // 2))
                        sp.dma_start(w1s[:], one(w1_v, e)).then_inc(f_w1, 16)
                        for k in range(2):
                            if k == 0:
                                wait(sp, f_k2, j)
                            else:
                                wait(sp, f_l2, j * M2)
                            sp.dma_start(w2s[:, k * half:(k + 1) * half, :],
                                         one(w2_v, e)[:, k * half:(k + 1) * half, :]).then_inc(f_w2[k], 16)
                            if k == 0:
                                wait(sp, f_g2, j * M2)
                                sp.dma_start(b12s[:], b12[bass.ds(e, 1)].rearrange("a p n -> (a p) n")
                                             ).then_inc(f_b12, 16)
                        wait(sp, f_l3, j)
                        sp.dma_start(w3s[:], one(w3_v, e)).then_inc(f_w3, 16)
                        wait(sp, f_y, j)
                        sp.dma_start(b3s[:], b3[bass.ds(e, 1)].rearrange("a d -> (a d)").partition_broadcast(P)
                                     ).then_inc(f_b3, 16)
                    blocks(sp, body)

                @block.gpsimd
                def _(pool):
                    def body(j):
                        wait(pool, f_y, j + 1)
                        pool.dma_start(one(ys_v, j), yrow[:]).then_inc(f_st, 16)
                    blocks(pool, body)
                    pool.wait_ge(f_st, 16 * NB)

                @block.tensor
                def _(pe):
                    def body(j):
                        wait(pe, f_h, (j + 1) * 16)
                        wait(pe, f_hT, j)
                        for c in range(DC):
                            for r in range(RT):
                                mm = pe.transpose(psT[:, c, r * P:(r + 1) * P], hrow[:, r, c * P:(c + 1) * P], ident[:])
                        mm.then_inc(f_t, 1)
                        wait(pe, f_w1, (j + 1) * 16)
                        wait(pe, f_hT, j + 1)
                        for m in range(M1):
                            if m % 2 == 0:
                                wait(pe, f_g1, j * M1 + m - 2)
                            for c in range(DC):
                                mm = pe.matmul(ps1[:, m // 2 % 2, m % 2, :], w1s[:, c, m * P:(m + 1) * P], hsT[:, c, :],
                                               start=(c == 0), stop=(c == DC - 1))
                            if m % 2:
                                mm.then_inc(f_l1, 1)
                        wait(pe, f_g2, j * M2)
                        for k in range(M1):
                            if k % half == 0:
                                wait(pe, f_w2[k // half], (j + 1) * 16)
                            wait(pe, f_g1, j * M1 + k + 1)
                            for m in range(M2):
                                mm = pe.matmul(ps2[:, m, 0:BLK], w2s[:, k, m * P:(m + 1) * P], g1[:, k, :],
                                               start=(k == 0), stop=(k == M1 - 1))
                                if k == M1 - 1:
                                    mm.then_inc(f_l2, 1)
                            if k == half - 1:
                                mm.then_inc(f_k2, 1)
                        wait(pe, f_w3, (j + 1) * 16)
                        wait(pe, f_y, j)
                        wait(pe, f_g2, (j + 1) * M2)
                        for r in range(RT):
                            for k in range(M2):
                                mm = pe.matmul(ps3[:, r, :], g2[:, k, r * P:(r + 1) * P], w3s[:, k, :],
                                               start=(k == 0), stop=(k == M2 - 1))
                        mm.then_inc(f_l3, 1)
                    blocks(pe, body)

                @block.scalar
                def _(act):
                    def body(j):
                        wait(act, f_b12, (j + 1) * 16)
                        for m in range(M1):
                            wait(act, f_l1, j * (M1 // 2) + m // 2 + 1)
                            wait(act, f_l2, j * M2)
                            act.activation(g1[:, m, :], ps1[:, m // 2 % 2, m % 2, :], ACT.Gelu,
                                           bias=b12s[:, m:m + 1]).then_inc(f_g1, 1)
                        wait(act, f_l3, j)
                        for m in range(M2):
                            wait(act, f_l2, j * M2 + m + 1)
                            act.activation(g2[:, m, :], ps2[:, m, 0:BLK], ACT.Gelu,
                                           bias=b12s[:, M1 + m:M1 + m + 1]).then_inc(f_g2, 1)
                    blocks(act, body)

                @block.vector
                def _(dve):
                    def body(j):
                        wait(dve, f_t, j + 1)
                        wait(dve, f_l1, j * (M1 // 2))
                        dve.tensor_copy(hsT[:], psT[:]).then_inc(f_hT, 1)
                        wait(dve, f_l3, j + 1)
                        wait(dve, f_b3, (j + 1) * 16)
                        wait(dve, f_st, j * 16)
                        dve.tensor_tensor(yrow[:], ps3, b3s[:].rearrange("p (a d) -> p a d", a=1)
                                          .broadcast_to([P, RT, D]), ALU.add).then_inc(f_y, 1)
                    blocks(dve, body)

            gbb = sb("gbb", [P, B, D], F32)
            c_gb = sem("c_gb")
            c_row = [sem(f"c_row{b}") for b in range(B)]
            c_gate = sem("c_gate")
            c_sum = sem("c_sum")
            c_out = sem("c_out")
            out_v = out.rearrange("b (t p) d -> b p t d", p=P)
            with nc.Block() as block:
                @block.sync
                def _(sp):
                    sp.dma_start(gbb[:], mod_d[:, 3, :].partition_broadcast(P)).then_inc(c_gb, 16)
                    for b in range(B):
                        sp.wait_ge(c_sum, b + 1)
                        sp.dma_start(out_v[b], x2s[:, b * TT:(b + 1) * TT, :]).then_inc(c_out, 16)
                    sp.wait_ge(c_out, 16 * B)

                @block.gpsimd
                def _(pool):
                    for t in range(NT):
                        pool.indirect_dma_start(rows[:, t, :], None, ys_d,
                                                bass.IndirectOffsetOnAxis(ap=pos[:, t:t + 1], axis=0)
                                                ).then_inc(c_row[t // TT], 16)

                @block.vector
                def _(dve):
                    dve.wait_ge(c_gb, 16)
                    for b in range(B):
                        batch = slice(b * TT, (b + 1) * TT)
                        dve.wait_ge(c_row[b], 16 * TT)
                        dve.tensor_tensor(rows[:, batch, :], rows[:, batch, :],
                                          gbb[:, b:b + 1, :].broadcast_to([P, TT, D]), ALU.mult).then_inc(c_gate, 1)
                        dve.wait_ge(c_gate, b + 1)
                        dve.tensor_tensor(x2s[:, batch, :], x2s[:, batch, :], rows[:, batch, :],
                                          ALU.add).then_inc(c_sum, 1)


_INS = ["x_in", "in_wT", "conv_w", "conv_b", "xp_wT", "dt_wT", "dt_b", "a_log", "d_skip", "out_wT",
        "wr", "br", "w1", "b12", "w2", "w3", "b3", "cT", "wmod"]


def kernel(L0_attn_hidden_states, L0_attn_in_proj_w, L0_attn_conv_w, L0_attn_conv_b, L0_attn_x_proj_w,
           L0_attn_dt_proj_w, L0_attn_dt_proj_b, L0_attn_A_log, L0_attn_Dskip, L0_attn_out_proj_w,
           L0_ffn_Wr, L0_ffn_br, L0_ffn_W1, L0_ffn_b1, L0_ffn_W2, L0_ffn_b2, L0_ffn_W3, L0_ffn_b3,
           L0_c, L0_wmod):
    import numpy as np
    import concourse.bacc as bacc
    from concourse.bass_utils import run_bass_kernel_spmd

    ac = lambda a: np.ascontiguousarray(np.asarray(a))
    H = 4
    ch = lambda a: ac(np.asarray(a).reshape(H, P, *np.asarray(a).shape[1:]).swapaxes(0, 1))
    b1 = np.asarray(L0_ffn_b1)
    b2 = np.asarray(L0_ffn_b2)
    E = b1.shape[0]
    data = dict(
        x_in=ac(L0_attn_hidden_states),
        in_wT=ac(np.asarray(L0_attn_in_proj_w).T),
        conv_w=ch(np.asarray(L0_attn_conv_w)[:, 0, :]),
        conv_b=ch(L0_attn_conv_b),
        xp_wT=ac(np.asarray(L0_attn_x_proj_w).reshape(H, -1, P).transpose(2, 0, 1)),
        dt_wT=ac(np.asarray(L0_attn_dt_proj_w).T),
        dt_b=ch(L0_attn_dt_proj_b),
        a_log=ch(L0_attn_A_log),
        d_skip=ch(L0_attn_Dskip),
        out_wT=ac(np.asarray(L0_attn_out_proj_w).T),
        wr=ac(np.asarray(L0_ffn_Wr).reshape(-1, P, E).swapaxes(0, 1)),
        br=ac(L0_ffn_br),
        w1=ac(L0_ffn_W1),
        b12=ac(np.concatenate([b1.reshape(E, -1, P), b2.reshape(E, -1, P)], axis=1).transpose(0, 2, 1)),
        w2=ac(L0_ffn_W2),
        w3=ac(L0_ffn_W3),
        b3=ac(L0_ffn_b3),
        cT=ac(np.asarray(L0_c).T.reshape(-1, P, L0_c.shape[0]).swapaxes(0, 1)),
        wmod=ac(L0_wmod),
    )
    nc = bacc.Bacc("TRN2", target_bir_lowering=False, num_devices=1)
    args = [nc.dram_tensor(f"in_{n}", data[n].shape, mybir.dt.from_np(data[n].dtype), kind="ExternalInput").ap()
            for n in _INS]
    o = nc.dram_tensor("out", data["x_in"].shape, F32, kind="ExternalOutput").ap()
    build(nc, *args, o)
    r = run_bass_kernel_spmd(nc, [{f"in_{n}": data[n] for n in _INS}], core_ids=[0])
    return r.results[0]["out"]
```

```python
from contextlib import ExitStack

import concourse.bass as bass
from concourse import mybir

F32 = mybir.dt.float32
BF16 = mybir.dt.bfloat16
I32 = mybir.dt.int32
U32 = mybir.dt.uint32
ALU = mybir.AluOpType
ACT = mybir.ActivationFunctionType
AX_X = mybir.AxisListType.X

P = 128
EPS = 1e-5
EXP_LN = "natural_log_exp_and_others"


def build(nc, x_in, in_wT, conv_w, conv_b, xp_wT, dt_wT, dt_b, a_log, d_skip, out_wT,
          wr, br, w1, b12, w2, w3, b3, cT, wmod, out):
    B, L, D = x_in.shape
    H = 4
    NS = a_log.shape[2]
    TT = L // P
    DC = D // P
    KC = conv_w.shape[2]
    NP = NS // 2
    DTR = dt_wT.shape[0]
    E = wr.shape[2]
    DT0 = 32
    MID, LOW = 64, 96
    NT = B * TT
    BLK_BITS = 8
    BLK = 1 << BLK_BITS
    NB = (NT * P + E * (BLK - 1)) // BLK

    mod_d = nc.dram_tensor("mod_rows", (B, 4, D), F32).ap()
    x2_d = nc.dram_tensor("x2_rows", (NT * P, D), F32).ap()
    h2_d = nc.dram_tensor("h2_rows", (NT * P, D), F32).ap()
    hs_d = nc.dram_tensor("h2_slots", (NB * BLK, D), F32).ap()
    ys_d = nc.dram_tensor("y_slots", (NB * BLK, D), F32).ap()

    with ExitStack() as outer:
        def keep(name, shape, dt):
            return outer.enter_context(nc.sbuf_tensor(name, shape, dt))

        def sem(name):
            return outer.enter_context(nc.semaphore(name))

        def wait(eng, s, v):
            if not (isinstance(v, int) and v <= 0):
                eng.wait_ge(s, v)

        logits = keep("logits", [P, NT, E], F32)
        ident = keep("ident", [P, P], F32)

        with ExitStack() as ctx:
            def sb(name, shape, dt):
                return ctx.enter_context(nc.sbuf_tensor(name, shape, dt))

            def ps(name, shape, dt=F32):
                return ctx.enter_context(nc.psum_tensor(name, shape, dt))

            in_w = sb("in_w", [P, DC, 2 * H * P], F32)
            xp_w = sb("xp_w", [P, H, P], F32)
            dt_w = sb("dt_w", [P, H * P], F32)
            out_w = sb("out_w", [P, H, D], F32)
            cw = sb("cw", [P, H, KC], F32)
            cb = sb("cb", [P, H], F32)
            dtb = sb("dtb", [P, H], F32)
            dsk = sb("dsk", [P, H], F32)
            a_neg = sb("a_neg", [P, H, NS], F32)
            wr_sb = sb("wr_sb", [P, DC, E], F32)
            br_bc = sb("br_bc", [P, E], F32)
            sel = sb("sel", [P, 2 * NS, P], BF16)
            taps = sb("taps", [P, H, KC, P], F32)
            c_sb = sb("c_sb", [P, DC, B], F32)
            sh_pp = sb("sh_pp", [P, DC, B], F32)
            sc_pp = sb("sc_pp", [P, DC, B], F32)
            psB = ps("psB", [P, 2, L])
            psC = ps("psC", [P, 2, L])
            psY = ps("psY", [P, 2, L])
            psG = ps("psG", [P, 2, L])

            s_par = sem("s_par")
            s_small = sem("s_small")
            s_wload = sem("s_wload")
            s_zero = sem("s_zero")
            s_const = sem("s_const")
            s_cact = sem("s_cact")
            s_aexp = sem("s_aexp")
            s_aneg = sem("s_aneg")
            s_taps = sem("s_taps")
            s_modps = sem("s_modps")
            s_modrow = sem("s_modrow")
            s_guard = sem("s_guard")
            s_modst = sem("s_modst")
            s_zrow = sem("s_zrow")
            s_zst = sem("s_zst")

            with nc.sbuf_tensor("wm", [P, DC, 6 * D], F32) as wm, \
                    nc.sbuf_tensor("modr", [B, 4, D], F32) as modr, \
                    nc.sbuf_tensor("sgn", [B, 2, D], F32) as sgn, \
                    nc.sbuf_tensor("mag", [B, 2, D], F32) as mag, \
                    nc.sbuf_tensor("zrow", [P, D], F32) as zrow, \
                    nc.sbuf_tensor("aex", [P, H, NS], F32) as aex, \
                    nc.Block() as block:
                small = [(c_sb[:], cT), (aex[:], a_log), (cw[:], conv_w), (cb[:], conv_b), (dtb[:], dt_b),
                         (dsk[:], d_skip), (wr_sb[:], wr), (br_bc[:], br.partition_broadcast(P))]

                @block.sync
                def _(sp):
                    sp.dma_start(wm[:], wmod.rearrange("(c p) n -> p c n", p=P)).then_inc(s_wload, 16)
                    for dst, src in small:
                        sp.dma_start(dst, src).then_inc(s_small, 16)
                    sp.dma_start(in_w[:], in_wT.rearrange("(c p) n -> p c n", p=P)).then_inc(s_par, 16)
                    sp.dma_start(dt_w[DT0:DT0 + DTR, :], dt_wT).then_inc(s_par, 16)
                    sp.dma_start(out_w[:], out_wT.rearrange("(h p) n -> p h n", p=P)).then_inc(s_par, 16)
                    sp.wait_ge(s_zero, 1)
                    for at in (0, MID, LOW):
                        sp.dma_start(xp_w[:, :, at:at + 2 * NS], xp_wT[:, :, DTR:]).then_inc(s_par, 16)
                    sp.dma_start(xp_w[:, :, DT0:DT0 + DTR], xp_wT[:, :, 0:DTR]).then_inc(s_par, 16)
                    sp.wait_ge(s_modrow, 6)
                    sp.dma_start(mod_d, modr[:]).then_inc(s_modst, 16)
                    sp.wait_ge(s_modst, 16)
                    sp.wait_ge(s_zrow, 1)
                    sp.dma_start(hs_d.rearrange("(n p) d -> p n d", p=P),
                                 zrow[:].rearrange("p (a d) -> p a d", a=1).broadcast_to([P, NB * BLK // P, D])
                                 ).then_inc(s_zst, 16)
                    sp.wait_ge(s_zst, 16)
                    sp.wait_ge(s_par, 16 * 7)
                    sp.wait_ge(s_small, 16 * len(small))

                @block.gpsimd
                def _(pool):
                    pool.memset(xp_w[:], 0.0).then_inc(s_zero, 1)
                    pool.memset(zrow[:], 0.0).then_inc(s_zrow, 1)
                    pool.memset(ident[:], 0.0).then_inc(s_const, 1)
                    pool.memset(sel[:], 0.0).then_inc(s_const, 1)
                    pool.wait_ge(s_const, 2)
                    pool.affine_select(out=ident[:], in_=ident[:], compare_op=ALU.not_equal, fill=1.0, base=0,
                                       pattern=[[-1, P]], channel_multiplier=1).then_inc(s_const, 1)
                    for k, at in enumerate((0, MID, LOW)):
                        pool.affine_select(out=sel[:], in_=sel[:], compare_op=ALU.not_equal, fill=1.0, base=-at,
                                           pattern=[[-1, 2 * NS], [0, P]], channel_multiplier=1).then_inc(s_const, 1)
                        pool.wait_ge(s_const, 4 + k)

                @block.scalar
                def _(act):
                    act.wait_ge(s_small, 16 * len(small))
                    act.activation(c_sb[:], c_sb[:], ACT.Silu).then_inc(s_cact, 1)
                    act.activation(aex[:], aex[:], ACT.Exp).then_inc(s_aexp, 1)

                @block.tensor
                def _(pe):
                    pe.wait_ge(s_wload, 16)
                    pe.wait_ge(s_cact, 1)
                    for j in range(2 * DC):
                        for c in range(DC):
                            mm = pe.matmul(psG[:, 0, j * B:(j + 1) * B], wm[:, c, j * P:(j + 1) * P], c_sb[:, c, :],
                                           start=(c == 0), stop=(c == DC - 1))
                    mm.then_inc(s_modps, 1)
                    for j in range(2):
                        for c in range(DC):
                            mm = pe.matmul(psY[0:B, j, :], c_sb[:, c, :], wm[:, c, (2 + 2 * j) * D:(4 + 2 * j) * D],
                                           start=(c == 0), stop=(c == DC - 1))
                    mm.then_inc(s_modps, 1)

                @block.vector
                def _(dve):
                    dve.wait_ge(s_aexp, 1)
                    dve.tensor_scalar(a_neg[:], aex[:], -1.0, None, ALU.mult).then_inc(s_aneg, 1)
                    dve.wait_ge(s_const, 3)
                    dve.wait_ge(s_small, 16 * len(small))
                    for h in range(H):
                        for k in range(KC):
                            dve.tensor_scalar(taps[:, h, k, :], ident[:], cw[:, h, k:k + 1], None,
                                              ALU.mult).then_inc(s_taps, 1)
                    dve.wait_ge(s_modps, 2)
                    pp = psG[:, 0, 0:2 * DC * B].rearrange("p (k c b) -> p k c b", k=2, c=DC)
                    dve.tensor_copy(sh_pp[:], pp[:, 0]).then_inc(s_modrow, 1)
                    dve.tensor_scalar(sc_pp[:], pp[:, 1], 1.0, None, ALU.add).then_inc(s_modrow, 1)
                    gates = [psY[0:B, 0, 0:D], psY[0:B, 1, D:2 * D]]
                    for k in range(2):
                        dve.tensor_copy(mag[:, k, :], gates[k]).then_inc(s_guard, 1)
                        dve.tensor_scalar(sgn[:, k, :], gates[k], 0.0, 2.0, ALU.is_ge, ALU.mult).then_inc(s_guard, 1)
                        dve.wait_ge(s_guard, 4 * k + 2)
                        dve.tensor_scalar(sgn[:, k, :], sgn[:, k, :], 1.0, None, ALU.subtract).then_inc(s_guard, 1)
                        dve.scalar_tensor_tensor(out=mag[:, k, :], in0=mag[:, k, :], scalar=-1.0, in1=mag[:, k, :],
                                                 op0=ALU.mult, op1=ALU.max).then_inc(s_guard, 1)
                        dve.wait_ge(s_guard, 4 * k + 4)
                        dve.scalar_tensor_tensor(out=modr[:, 3 * k, :], in0=mag[:, k, :], scalar=0.25,
                                                 in1=sgn[:, k, :], op0=ALU.max, op1=ALU.mult).then_inc(s_modrow, 1)
                    dve.tensor_copy(modr[:, 1, :], psY[0:B, 0, D:2 * D]).then_inc(s_modrow, 1)
                    dve.tensor_scalar(modr[:, 2, :], psY[0:B, 1, 0:D], 1.0, None, ALU.add).then_inc(s_modrow, 1)

            xa = sb("xa", [P, TT, D], F32)
            xr = sb("xr", [P, TT, D], F32)
            mbc = sb("mbc", [P, 4, D], F32)
            xn = sb("xn", [P, TT, D], F32)
            x2b = sb("x2b", [P, TT, D], F32)
            h2n = sb("h2n", [P, TT, D], F32)
            st1 = sb("st1", [P, TT, 6], F32)
            mv1 = sb("mv1", [P, TT, 2], F32)
            rs1 = sb("rs1", [P, 4, TT], F32)
            st2 = sb("st2", [P, TT, 6], F32)
            mv2 = sb("mv2", [P, TT, 2], F32)
            rs2 = sb("rs2", [P, 4, TT], F32)
            hT = sb("hT", [P, DC, L], F32)
            h2T = sb("h2T", [P, DC, L], F32)
            xpad = sb("xpad", [P, KC - 1 + L], F32)
            u = sb("u", [P, 2, L], F32)
            ud = sb("ud", [P, L], F32)
            zs = sb("zs", [P, H, L], F32)
            xds = sb("xds", [P, L], F32)
            bc3 = sb("bc3", [P, 2, L], BF16)
            bcr = sb("bcr", [P, L], F32)
            sp_a = sb("sp_a", [P, L], F32)
            sp_r = sb("sp_r", [P, L], F32)
            sp_e = sb("sp_e", [P, L], F32)
            sp_l = sb("sp_l", [P, L], F32)
            sp_w = sb("sp_w", [P, L], F32)
            delta = sb("delta", [P, 2, L], F32)
            du = sb("du", [P, 2, L], F32)
            RA, RS, RC, RP = 4, 4, 4, 4
            LAG = 2
            dA = sb("dA", [P, RA, 2, L], F32)
            dBu = sb("dBu", [P, 2, 2, L], F32)
            st = sb("st", [P, RS, 2, L], F32)
            cbr = sb("cbr", [P, RC, 2, L], F32)
            sc = sb("sc", [P, RP, 2, L], F32)
            yg = sb("yg", [P, TT, P], F32)
            yT = sb("yT", [P, H, L], F32)

            d_xa = sem("d_xa")
            d_xr = sem("d_xr")
            d_mbc = sem("d_mbc")
            d_x2 = sem("d_x2")
            d_h2 = sem("d_h2")
            s_st1 = sem("s_st1")
            s_mv1 = sem("s_mv1")
            s_ve1 = sem("s_ve1")
            s_rg1 = sem("s_rg1")
            s_rs1 = sem("s_rs1")
            s_xn1 = sem("s_xn1")
            s_t1 = sem("s_t1")
            s_hT = sem("s_hT")
            s_padz = sem("s_padz")
            s_xin = sem("s_xin")
            s_xpad = sem("s_xpad")
            s_conv = sem("s_conv")
            s_u = sem("s_u")
            s_zin = sem("s_zin")
            s_zs = sem("s_zs")
            s_xd = sem("s_xd")
            s_cast = sem("s_cast")
            s_xds = sem("s_xds")
            s_split = sem("s_split")
            s_dtp = sem("s_dtp")
            s_spa = sem("s_spa")
            s_spr = sem("s_spr")
            s_spe = sem("s_spe")
            s_spl = sem("s_spl")
            s_delta = sem("s_delta")
            s_w = sem("s_w")
            s_ln = sem("s_ln")
            s_du = sem("s_du")
            s_B = sem("s_B")
            s_C = sem("s_C")
            s_cev = sem("s_cev")
            s_mulB = sem("s_mulB")
            s_scan = sem("s_scan")
            s_prod = sem("s_prod")
            s_sum = sem("s_sum")
            s_dA = sem("s_dA")
            s_ud = sem("s_ud")
            s_udt = sem("s_udt")
            s_gate = sem("s_gate")
            s_back = sem("s_back")
            s_yT = sem("s_yT")
            s_out = sem("s_out")
            s_gated = sem("s_gated")
            s_x2 = sem("s_x2")
            s_st2 = sem("s_st2")
            s_mv2 = sem("s_mv2")
            s_ve2 = sem("s_ve2")
            s_rg2 = sem("s_rg2")
            s_rs2 = sem("s_rs2")
            s_xn2 = sem("s_xn2")
            s_mod2 = sem("s_mod2")
            s_h2 = sem("s_h2")
            s_t2 = sem("s_t2")
            s_h2T = sem("s_h2T")
            s_rt = sem("s_rt")
            s_lg = sem("s_lg")

            x_v = x_in.rearrange("b (t p) d -> b p t d", p=P)
            x2_v = x2_d.rearrange("(b t p) d -> b p t d", t=TT, p=P)
            h2_v = h2_d.rearrange("(b t p) d -> b p t d", t=TT, p=P)

            def batches(eng, body):
                body(0, True, False)
                body(1, False, False)
                with eng.Fori(2, B - 1) as b:
                    body(b, False, False)
                body(B - 1, False, True)

            def of_batch(view, b):
                return view[bass.ds(b, 1)].rearrange("a p t d -> (a p) t d")

            with nc.Block() as block:
                @block.sync
                def _(sp):
                    def load_tokens(b):
                        wait(sp, s_xn1, b * TT)
                        sp.dma_start(xa[:], of_batch(x_v, b)).then_inc(d_xa, 16)

                    def load_tail(b):
                        wait(sp, s_x2, b * 2)
                        sp.dma_start(xr[:], of_batch(x_v, b)).then_inc(d_xr, 16)
                        wait(sp, s_h2, b)
                        sp.dma_start(mbc[:].rearrange("p k d -> p (k d)"),
                                     mod_d[bass.ds(b, 1)].rearrange("a k d -> (a k d)").partition_broadcast(P)
                                     ).then_inc(d_mbc, 16)

                    def store_tail(b):
                        wait(sp, s_x2, (b + 1) * 2)
                        sp.dma_start(of_batch(x2_v, b), x2b[:]).then_inc(d_x2, 16)
                        wait(sp, s_h2, b + 1)
                        sp.dma_start(of_batch(h2_v, b), h2n[:]).then_inc(d_h2, 16)

                    def body(b, first, last):
                        if not first:
                            load_tail(b - 1)
                        if not last:
                            load_tokens(b + 1)
                        if not first:
                            store_tail(b - 1)
                    load_tokens(0)
                    batches(sp, body)
                    load_tail(B - 1)
                    store_tail(B - 1)
                    sp.wait_ge(d_x2, 16 * B)
                    sp.wait_ge(d_h2, 16 * B)

                @block.tensor
                def _(pe):
                    def xdbl_mm(v, h):
                        wait(pe, s_u, v + 1)
                        pe.matmul(psG[:, 0, :], xp_w[:, h, :], u[:, h % 2, :], start=True, stop=True).then_inc(s_xd, 1)

                    def dt_mm(v, h):
                        wait(pe, s_xds, v + 1)
                        pe.matmul(psG[:, 1, :], dt_w[DT0:DT0 + DTR, h * P:(h + 1) * P], xds[DT0:DT0 + DTR, :],
                                  start=True, stop=True).then_inc(s_dtp, 1)

                    def xin_mm(v, h):
                        for c in range(DC):
                            mm = pe.matmul(psG[:, 0, :], in_w[:, c, h * P:(h + 1) * P], hT[:, c, :],
                                           start=(c == 0), stop=(c == DC - 1))
                        mm.then_inc(s_xin, 1)

                    def zin_mm(v, h):
                        for t in range(TT):
                            for c in range(DC):
                                mm = pe.matmul(psG[:, 1, t * P:(t + 1) * P], hT[:, c, t * P:(t + 1) * P],
                                               in_w[:, c, (H + h) * P:(H + h + 1) * P],
                                               start=(c == 0), stop=(c == DC - 1))
                        mm.then_inc(s_zin, 1)

                    def conv_mm(v, h):
                        wait(pe, s_xpad, v + 1)
                        for k in range(KC):
                            mm = pe.matmul(psG[:, 0, :], taps[:, h, k, :], xpad[:, k:k + L],
                                           start=(k == 0), stop=(k == KC - 1))
                        mm.then_inc(s_conv, 1)

                    def back(q):
                        wait(pe, s_gate, q + 1)
                        for t in range(TT):
                            mm = pe.transpose(psG[:, 1, t * P:(t + 1) * P], yg[:, t, :], ident[:])
                        mm.then_inc(s_back, 1)

                    def out_mm(b, k):
                        for t in (2 * k, 2 * k + 1):
                            for h in range(H):
                                mm = pe.matmul(psG[:, 0, (t % 2) * D:(t % 2 + 1) * D], yT[:, h, t * P:(t + 1) * P],
                                               out_w[:, h, :], start=(h == 0), stop=(h == H - 1))
                        mm.then_inc(s_out, 1)

                    def turn(src, c, done):
                        for t in range(TT):
                            mm = pe.transpose(psG[:, 0, t * P:(t + 1) * P], src[:, t, c * P:(c + 1) * P], ident[:])
                        mm.then_inc(done, 1)

                    def router_mm(b):
                        wait(pe, s_h2T, (b + 1) * DC)
                        for t in range(TT):
                            for c in range(DC):
                                mm = pe.matmul(psG[:, 1, t * E:(t + 1) * E], h2T[:, c, t * P:(t + 1) * P],
                                               wr_sb[:, c, :], start=(c == 0), stop=(c == DC - 1))
                        mm.then_inc(s_rt, 1)

                    def broadcast(q, h, g):
                        p = q * NP + g
                        if g == 0:
                            wait(pe, s_split, (q + 1) * 3)
                        wait(pe, s_mulB, p)
                        for i in range(2):
                            mm = pe.matmul(psB[:, i, :], sel[:, 2 * g + i, :], bc3[:, h % 2, :], start=True, stop=True)
                        mm.then_inc(s_B, 1)
                        wait(pe, s_cev, p)
                        for i in range(2):
                            mm = pe.matmul(psC[:, i, :], sel[:, NS + 2 * g + i, :], bc3[:, h % 2, :],
                                           start=True, stop=True)
                        mm.then_inc(s_C, 1)

                    def turn_add(h, src, first, last):
                        for t in range(TT):
                            mm = pe.matmul(psY[:, h % 2, t * P:(t + 1) * P], src[:, t * P:(t + 1) * P], ident[:],
                                           is_transpose=True, start=first and t == 0, stop=last and t == TT - 1,
                                           skip_group_check=True)
                        return mm

                    def skip_term(q, h):
                        wait(pe, s_gate, q - 1)
                        wait(pe, s_ud, q + 1)
                        turn_add(h, ud, True, False).then_inc(s_udt, 1)

                    def sums(q, h, g):
                        wait(pe, s_prod, q * NP + g + 1)
                        for i in range(2):
                            mm = turn_add(h, sc[:, g % RP, i, :], False, g == NP - 1 and i == 1)
                        mm.then_inc(s_sum, 1)

                    def guest(b, h, k, first, last):
                        if h == 0:
                            if k == 0:
                                wait(pe, s_yT, b * H)
                            wait(pe, s_gated, (b - 1) * 2 + k)
                            out_mm(b - 1, k)
                        if h == 1:
                            wait(pe, s_xn1, (b + 2) * TT)
                            wait(pe, s_hT, (b + 1) * DC + k)
                            turn(xn, k, s_t1)
                        if h == 2:
                            wait(pe, s_h2, b)
                            wait(pe, s_h2T, (b - 1) * DC + k)
                            turn(h2n, k, s_t2)

                    def has_guests(h, first, last):
                        return (h in (0, 2) and not first) or (h == 1 and not last)

                    def guests_left(b, h, first, last):
                        if h == 0 and not first:
                            wait(pe, s_gated, b * 2)
                        if h == 1 and not last:
                            wait(pe, s_hT, (b + 2) * DC)
                        if h == 2 and not first:
                            wait(pe, s_h2T, b * DC)

                    def unit(b, h, first, last):
                        q = b * H + h
                        vb, hb = q + 1, (h + 1) % H
                        va, ha = q + 2, (h + 2) % H
                        prep_b = not (last and h == H - 1)
                        prep_a = not (last and h >= H - 2)
                        for g in range(NP):
                            broadcast(q, h, g)
                            if g >= LAG:
                                sums(q, h, g - LAG)
                            elif not (first and h == 0):
                                sums(q - 1, (h + 1) % 2, NP - LAG + g)
                            if g == LAG - 1:
                                skip_term(q, h)
                            if g == 0:
                                if prep_b:
                                    if h == 0 or (first and h == 3):
                                        wait(pe, s_u, vb + 1)
                                    elif h == 1 and first:
                                        wait(pe, s_u, vb + 1)
                                    else:
                                        guests_left(b, h - 1, first, last)
                                    xdbl_mm(vb, hb)
                            if g == 1 and prep_b:
                                if h == 3 and not first:
                                    wait(pe, s_lg, b)
                                wait(pe, s_yT, q - 1)
                                wait(pe, s_zs, vb + 1)
                                dt_mm(vb, hb)
                            if g == 2 and prep_a:
                                wait(pe, s_xds, vb + 1)
                                if h == 2:
                                    wait(pe, s_hT, (b + 2) * DC)
                                xin_mm(va, ha)
                                wait(pe, s_spr, vb + 1)
                                zin_mm(va, ha)
                            if g == 3 and prep_a:
                                conv_mm(va, ha)
                            if g == 4 and not (first and h == 0):
                                if prep_a:
                                    wait(pe, s_zs, va + 1)
                                elif prep_b:
                                    wait(pe, s_spr, vb + 1)
                                back(q - 1)
                            if g in (5, 6) and has_guests(h, first, last):
                                if g == 5:
                                    if prep_a:
                                        wait(pe, s_u, va + 1)
                                    elif prep_b:
                                        wait(pe, s_xds, vb + 1)
                                guest(b, h, g - 5, first, last)
                            if g == 7 and h == 2 and not first:
                                wait(pe, s_yT, q)
                                router_mm(b - 1)

                    for c in range(DC):
                        wait(pe, s_xn1, TT)
                        wait(pe, s_hT, c)
                        turn(xn, c, s_t1)
                    wait(pe, s_hT, DC)
                    for v in range(2):
                        wait(pe, s_u, v)
                        xin_mm(v, v)
                        zin_mm(v, v) if v == 0 else None
                        if v == 1:
                            wait(pe, s_zs, 1)
                            zin_mm(v, v)
                        conv_mm(v, v)
                    wait(pe, s_u, 2)
                    xdbl_mm(0, 0)
                    wait(pe, s_zs, 2)
                    dt_mm(0, 0)

                    def body(b, first, last):
                        for h in range(H):
                            unit(b, h, first, last)
                    batches(pe, body)
                    for g in range(NP - LAG, NP):
                        sums(B * H - 1, H - 1, g)
                    wait(pe, s_yT, B * H - 1)
                    back(B * H - 1)
                    wait(pe, s_yT, B * H)
                    for k in range(2):
                        wait(pe, s_gated, (B - 1) * 2 + k)
                        out_mm(B - 1, k)
                    wait(pe, s_h2, B)
                    wait(pe, s_gated, B * 2)
                    for k in range(2):
                        wait(pe, s_h2T, (B - 1) * DC + k)
                        turn(h2n, k, s_t2)
                    router_mm(B - 1)

                @block.scalar
                def _(act):
                    def x_copy(v):
                        wait(act, s_xin, v + 1)
                        wait(act, s_conv, v)
                        act.activation(xpad[:, KC - 1:], psG[:, 0, :], ACT.Copy).then_inc(s_xpad, 1)

                    def silus(v, h):
                        wait(act, s_conv, v + 1)
                        wait(act, s_xd, v - 1)
                        wait(act, s_du, v - 1)
                        act.activation(u[:, h % 2, :], psG[:, 0, :], ACT.Silu, bias=cb[:, h:h + 1]).then_inc(s_u, 1)
                        wait(act, s_zin, v + 1)
                        wait(act, s_gate, v - 3)
                        act.activation(zs[:, h, :], psG[:, 1, :], ACT.Silu).then_inc(s_zs, 1)
                        act.preload_act_table_set(EXP_LN)

                    def xd_copy(v, h):
                        wait(act, s_xd, v + 1)
                        wait(act, s_C, (v - 1) * NP)
                        act.activation(bc3[:, h % 2, :], psG[:, 0, :], ACT.Copy).then_inc(s_cast, 1)
                        wait(act, s_split, v * 3)
                        wait(act, s_dtp, v)
                        act.activation(xds[:], psG[:, 0, :], ACT.Copy).then_inc(s_xds, 1)

                    def skip(v, h):
                        wait(act, s_udt, v)
                        act.activation(ud[:], u[:, h % 2, :], ACT.Copy, scale=dsk[:, h:h + 1]).then_inc(s_ud, 1)

                    def y_copy(q, h):
                        wait(act, s_back, q + 1)
                        act.activation(yT[:, h, :], psG[:, 1, :], ACT.Copy).then_inc(s_yT, 1)

                    def softplus(v, h):
                        wait(act, s_dtp, v + 1)
                        wait(act, s_delta, v * 3)
                        act.activation(sp_a[:], psG[:, 1, :], ACT.Abs, bias=dtb[:, h:h + 1]).then_inc(s_spa, 1)
                        act.activation(sp_r[:], psG[:, 1, :], ACT.Relu, bias=dtb[:, h:h + 1]).then_inc(s_spr, 1)
                        wait(act, s_spa, v + 1)
                        act.activation(sp_e[:], sp_a[:], ACT.Exp, scale=-1.0).then_inc(s_spe, 1)
                        wait(act, s_spe, v + 1)
                        act.activation(sp_l[:], sp_e[:], ACT.Ln, bias=1.0).then_inc(s_spl, 1)

                    def decays(q, h, g):
                        p = q * NP + g
                        if g == 0:
                            wait(act, s_delta, (q + 1) * 3)
                        wait(act, s_scan, p - RA + 1)
                        for i in range(2):
                            n = 2 * g + i
                            act.activation(dA[:, g % RA, i, :], delta[:, h % 2, :], ACT.Exp,
                                           scale=a_neg[:, h, n:n + 1]).then_inc(s_dA, 1)

                    def c_copy(q, g):
                        p = q * NP + g
                        wait(act, s_C, p + 1)
                        wait(act, s_prod, p - RC + 1)
                        act.activation(cbr[:, g % RC], psC[:], ACT.Copy).then_inc(s_cev, 1)

                    def modulated(b, c):
                        wait(act, s_t1, b * DC + c + 1)
                        act.activation(hT[:, c, :], psG[:, 0, :], ACT.Identity, bias=sh_pp[:, c, bass.ds(b, 1)],
                                       scale=sc_pp[:, c, bass.ds(b, 1)]).then_inc(s_hT, 1)

                    def h2_copy(b, c):
                        wait(act, s_t2, b * DC + c + 1)
                        act.activation(h2T[:, c, :], psG[:, 0, :], ACT.Copy).then_inc(s_h2T, 1)

                    def guess_rstd(b, rs, before, done):
                        wait(act, before, b + 1)
                        act.activation(rs[:, 1, :], rs[:, 0, :], ACT.Ln).then_inc(done, 1)
                        wait(act, done, b * 2 + 1)
                        act.activation(rs[:, 1, :], rs[:, 1, :], ACT.Exp, scale=-0.5).then_inc(done, 1)

                    def unit(b, h, first, last):
                        q = b * H + h
                        vb, hb = q + 1, (h + 1) % H
                        va, ha = q + 2, (h + 2) % H
                        prep_b = not (last and h == H - 1)
                        prep_a = not (last and h >= H - 2)
                        for g in range(NP):
                            decays(q, h, g)
                            c_copy(q, g)
                            if g == 0 and prep_b:
                                xd_copy(vb, hb)
                            if g == 1 and prep_b:
                                softplus(vb, hb)
                                skip(vb, hb)
                            if g == 2 and prep_a:
                                x_copy(va)
                            if g == 3 and prep_a:
                                silus(va, ha)
                            if g == 4 and not (first and h == 0):
                                if h == 1 and not first:
                                    wait(act, s_out, b * 2)
                                y_copy(q - 1, (h + H - 1) % H)
                            if g in (5, 6):
                                if h == 1 and not last:
                                    modulated(b + 1, g - 5)
                                if h == 2 and not first:
                                    h2_copy(b - 1, g - 5)
                            if h == 0 and g == 5 and not last:
                                guess_rstd(b + 1, rs1, s_ve1, s_rg1)
                            if h == 1 and g == 3 and not first:
                                guess_rstd(b - 1, rs2, s_ve2, s_rg2)

                    guess_rstd(0, rs1, s_ve1, s_rg1)
                    for c in range(DC):
                        modulated(0, c)
                    wait(act, s_padz, 1)
                    for v in range(2):
                        x_copy(v)
                        silus(v, v)
                    xd_copy(0, 0)
                    softplus(0, 0)
                    skip(0, 0)

                    def body(b, first, last):
                        for h in range(H):
                            unit(b, h, first, last)
                    batches(act, body)
                    y_copy(B * H - 1, H - 1)
                    guess_rstd(B - 1, rs2, s_ve2, s_rg2)
                    for c in range(DC):
                        h2_copy(B - 1, c)

                @block.gpsimd
                def _(pool):
                    pool.memset(xpad[:, 0:KC - 1], 0.0).then_inc(s_padz, 1)

                    def split(v, h):
                        wait(pool, s_cast, v + 1)
                        wait(pool, s_xds, v + 1)
                        pool.tensor_tensor(bcr[MID:], xds[MID:], bc3[MID:, h % 2, :], ALU.subtract).then_inc(s_split, 1)
                        wait(pool, s_split, v * 3 + 1)
                        pool.tensor_tensor(bc3[MID:, h % 2, :], xds[MID:], bc3[MID:, h % 2, :],
                                           ALU.subtract).then_inc(s_split, 1)
                        wait(pool, s_split, v * 3 + 2)
                        pool.tensor_tensor(bc3[LOW:, h % 2, :], bcr[LOW:], bc3[LOW:, h % 2, :],
                                           ALU.subtract).then_inc(s_split, 1)
                        wait(pool, s_split, v * 3 + 3)

                    def put_delta(v, h):
                        wait(pool, s_ln, v + 1)
                        pool.tensor_tensor(sp_w[:], sp_e[:], sp_w[:], ALU.subtract).then_inc(s_delta, 1)
                        wait(pool, s_delta, v * 3 + 1)
                        pool.tensor_tensor(sp_w[:], sp_l[:], sp_w[:], ALU.add).then_inc(s_delta, 1)
                        wait(pool, s_spr, v + 1)
                        wait(pool, s_dA, (v - 1) * NS)
                        wait(pool, s_du, v - 1)
                        wait(pool, s_delta, v * 3 + 2)
                        pool.tensor_tensor(delta[:, h % 2, :], sp_w[:], sp_r[:], ALU.add).then_inc(s_delta, 1)

                    def product(q, g):
                        p = q * NP + g
                        wait(pool, s_cev, p + 1)
                        wait(pool, s_scan, p + 1)
                        wait(pool, s_sum, p - RP + 1)
                        pool.tensor_tensor(sc[:, g % RP], st[:, g % RS], cbr[:, g % RC], ALU.mult).then_inc(s_prod, 1)

                    wait(pool, s_padz, 1)
                    split(0, 0)
                    put_delta(0, 0)

                    def body(b, first, last):
                        for h in range(H):
                            q = b * H + h
                            v = q + 1
                            vh = (h + 1) % H
                            prep = not (last and h == H - 1)
                            for g in range(NP):
                                product(q, g)
                                if g == 1 and prep:
                                    wait(pool, s_prod, q * NP + g + 1)
                                    split(v, vh)
                                if g == 3 and prep:
                                    put_delta(v, vh)
                    batches(pool, body)

                @block.vector
                def _(dve):
                    def stats(src, out, done):
                        for t in range(TT):
                            dve.bn_stats(out[:, t, :], src[:, t, :]).then_inc(done, 1)

                    def aggregate(b, stat, mv, rs, done_mv, done_ve):
                        for t in range(TT):
                            dve.bn_aggr(mv[:, t, :], stat[:, t, :]).then_inc(done_mv, 1)
                        plus_eps(b, mv, rs, done_mv, done_ve)

                    def plus_eps(b, mv, out, before, done):
                        wait(dve, before, (b + 1) * TT)
                        dve.tensor_scalar(out[:, 0, :], mv[:, :, 1], EPS, None, ALU.add).then_inc(done, 1)

                    def refine(b, rs, guess, done):
                        wait(dve, guess, (b + 1) * 2)
                        for k, (o, x, y) in enumerate(((2, 0, 1), (2, 2, 1))):
                            dve.tensor_tensor(rs[:, o, :], rs[:, x, :], rs[:, y, :], ALU.mult).then_inc(done, 1)
                            wait(dve, done, b * 4 + k + 1)
                        dve.tensor_scalar(rs[:, 2, :], rs[:, 2, :], -0.5, 1.5, ALU.mult, ALU.add).then_inc(done, 1)
                        wait(dve, done, b * 4 + 3)
                        dve.tensor_tensor(rs[:, 3, :], rs[:, 2, :], rs[:, 1, :], ALU.mult).then_inc(done, 1)

                    def centre(b, t, src, mv, rs, dst, before, done):
                        wait(dve, before, (b + 1) * 4)
                        dve.tensor_scalar(dst[:, t, :], src[:, t, :], mv[:, t, 0:1], rs[:, 3, t:t + 1],
                                          ALU.subtract, ALU.mult).then_inc(done, 1)

                    def norm1_stats(b):
                        wait(dve, d_xa, (b + 1) * 16)
                        stats(xa, st1, s_st1)

                    def norm1(b):
                        refine(b, rs1, s_rg1, s_rs1)
                        wait(dve, s_t1, b * DC)
                        for t in range(TT):
                            centre(b, t, xa, mv1, rs1, xn, s_rs1, s_xn1)

                    def residual(b, k):
                        two = slice(2 * k, 2 * k + 2)
                        wait(dve, s_out, b * 2 + k + 1)
                        wait(dve, d_mbc, (b + 1) * 16)
                        wait(dve, d_xr, (b + 1) * 16)
                        wait(dve, d_x2, b * 16)
                        dve.tensor_tensor(x2b[:, two, :], psG[:, 0, :].rearrange("p (t d) -> p t d", t=2),
                                          mbc[:, 0:1, :].broadcast_to([P, 2, D]), ALU.mult).then_inc(s_gated, 1)
                        wait(dve, s_gated, b * 2 + k + 1)
                        dve.tensor_tensor(x2b[:, two, :], x2b[:, two, :], xr[:, two, :], ALU.add).then_inc(s_x2, 1)

                    def norm2_stats(b):
                        wait(dve, s_x2, (b + 1) * 2)
                        stats(x2b, st2, s_st2)

                    def norm2(b):
                        refine(b, rs2, s_rg2, s_rs2)
                        wait(dve, s_t2, b * DC)
                        wait(dve, d_h2, b * 16)
                        for t in range(TT):
                            centre(b, t, x2b, mv2, rs2, h2n, s_rs2, s_xn2)
                        wait(dve, s_xn2, (b + 1) * TT)
                        dve.tensor_tensor(h2n[:], h2n[:], mbc[:, 2:3, :].broadcast_to([P, TT, D]),
                                          ALU.mult).then_inc(s_mod2, 1)
                        wait(dve, s_mod2, b + 1)
                        dve.tensor_tensor(h2n[:], h2n[:], mbc[:, 1:2, :].broadcast_to([P, TT, D]),
                                          ALU.add).then_inc(s_h2, 1)

                    def logits_out(b):
                        wait(dve, s_rt, b + 1)
                        dve.tensor_tensor(logits[:, bass.ds(b * TT, TT), :],
                                          psG[:, 1, 0:TT * E].rearrange("p (t e) -> p t e", t=TT),
                                          br_bc[:].rearrange("p (a e) -> p a e", a=1).broadcast_to([P, TT, E]),
                                          ALU.add).then_inc(s_lg, 1)

                    def rounded(v):
                        wait(dve, s_spe, v + 1)
                        wait(dve, s_delta, v * 3)
                        dve.tensor_scalar(sp_w[:], sp_e[:], 1.0, 1.0, ALU.add, ALU.subtract).then_inc(s_w, 1)
                        wait(dve, s_w, v + 1)
                        wait(dve, s_spl, v + 1)
                        dve.scalar_tensor_tensor(out=sp_l[:], in0=sp_w[:], scalar=0.0, in1=sp_l[:],
                                                 op0=ALU.is_gt, op1=ALU.mult).then_inc(s_ln, 1)

                    def delta_u(v, h):
                        wait(dve, s_delta, (v + 1) * 3)
                        dve.tensor_tensor(du[:, h % 2, :], delta[:, h % 2, :], u[:, h % 2, :],
                                          ALU.mult).then_inc(s_du, 1)

                    def gate(q, h):
                        wait(dve, s_sum, (q + 1) * NP)
                        wait(dve, s_back, q)
                        dve.tensor_tensor(yg[:].rearrange("p t d -> p (t d)"), psY[:, h % 2, :], zs[:, h, :],
                                          ALU.mult).then_inc(s_gate, 1)

                    def scans(q, h, g):
                        p = q * NP + g
                        if g == 0:
                            wait(dve, s_du, q + 1)
                        wait(dve, s_B, p + 1)
                        dve.tensor_tensor(dBu[:, g % 2], psB[:], du[:, h % 2:h % 2 + 1, :].broadcast_to([P, 2, L]),
                                          ALU.mult).then_inc(s_mulB, 1)
                        wait(dve, s_mulB, p + 1)
                        wait(dve, s_prod, p - RS + 1)
                        for i in range(2):
                            wait(dve, s_dA, q * NS + 2 * g + i + 1)
                            last = dve.tensor_tensor_scan(out=st[:, g % RS, i, :], data0=dA[:, g % RA, i, :],
                                                          data1=dBu[:, g % 2, i, :], initial=0.0,
                                                          op0=ALU.mult, op1=ALU.add)
                        last.then_inc(s_scan, 1)

                    norm1_stats(0)
                    wait(dve, s_st1, TT)
                    aggregate(0, st1, mv1, rs1, s_mv1, s_ve1)
                    norm1(0)
                    rounded(0)
                    delta_u(0, 0)

                    def body(b, first, last):
                        for h in range(H):
                            q = b * H + h
                            for g in range(NP):
                                if h == 1 and g == 1 and not first:
                                    wait(dve, s_st2, b * TT)
                                if h == 0 and g == 4 and not last:
                                    wait(dve, s_st1, (b + 2) * TT)
                                scans(q, h, g)
                                if h == 1 and g == 1 and not first:
                                    aggregate(b - 1, st2, mv2, rs2, s_mv2, s_ve2)
                                if h == 0 and g == 4 and not last:
                                    aggregate(b + 1, st1, mv1, rs1, s_mv1, s_ve1)
                                if g == 2 and not (last and h == H - 1):
                                    rounded(q + 1)
                                if g == LAG and not (first and h == 0):
                                    gate(q - 1, (h + H - 1) % H)
                                if h == 0 and g in (6, 7) and not first:
                                    residual(b - 1, g - 6)
                                if h == 1 and g == 0 and not first:
                                    norm2_stats(b - 1)
                                if h == 1 and g == 5 and not first:
                                    norm2(b - 1)
                                if h == 0 and g == 3 and not last:
                                    norm1_stats(b + 1)
                                if h == 1 and g == 0 and not last:
                                    norm1(b + 1)
                                if h == 3 and g == 0 and not first:
                                    logits_out(b - 1)
                                if g == 5 and not (last and h == H - 1):
                                    delta_u(q + 1, (h + 1) % H)
                    batches(dve, body)
                    gate(B * H - 1, H - 1)
                    for k in range(2):
                        residual(B - 1, k)
                    norm2_stats(B - 1)
                    wait(dve, s_st2, B * TT)
                    aggregate(B - 1, st2, mv2, rs2, s_mv2, s_ve2)
                    norm2(B - 1)
                    logits_out(B - 1)

        with ExitStack() as ctx:
            def sb(name, shape, dt):
                return ctx.enter_context(nc.sbuf_tensor(name, shape, dt))

            def ps(name, shape, dt=F32):
                return ctx.enter_context(nc.psum_tensor(name, shape, dt))

            mx = sb("mx", [P, NT], F32)
            eq = sb("eq", [P, NT, E], F32)
            hot = sb("hot", [P, NT, E], F32)
            hotb = sb("hotb", [P, NT, E], BF16)
            rank = sb("rank", [P, E], F32)
            before = sb("before", [P, P], BF16)
            ones = sb("ones", [P, P], BF16)
            onesf = sb("onesf", [P, NT], F32)
            run = sb("run", [P, NT, E], F32)
            slot = sb("slot", [P, NT, E], F32)
            padi = sb("padi", [P, E], I32)
            padf = sb("padf", [P, E], F32)
            ends = sb("ends", [P, E], F32)
            offs = sb("offs", [P, E], F32)
            posf = sb("posf", [P, NT], F32)
            pos = sb("pos", [P, NT], U32)
            starts = sb("starts", [1, NB], F32)
            past = sb("past", [1, NB, E], F32)
            expf = sb("expf", [1, NB], F32)
            block_expert = sb("block_expert", [1, NB], I32)
            rows = sb("rows", [P, NT, D], F32)
            x2s = sb("x2s", [P, NT, D], F32)
            psR = ps("psR", [P, 2, NT, E])

            r_const = sem("r_const")
            r_rows = sem("r_rows")
            r_x2 = sem("r_x2")
            r_gb = sem("r_gb")
            r_hot = sem("r_hot")
            r_count = sem("r_count")
            r_step = sem("r_step")
            r_pos = sem("r_pos")
            r_blocks = sem("r_blocks")
            r_scat = sem("r_scat")

            with nc.Block() as block:
                @block.sync
                def _(sp):
                    sp.dma_start(rows[:], h2_d.rearrange("(t p) d -> p t d", p=P)).then_inc(r_rows, 16)
                    sp.dma_start(x2s[:], x2_d.rearrange("(t p) d -> p t d", p=P)).then_inc(r_x2, 16)
                    sp.wait_ge(r_x2, 16)

                @block.gpsimd
                def _(pool):
                    pool.memset(before[:], 1.0).then_inc(r_const, 1)
                    pool.memset(ones[:], 1.0).then_inc(r_const, 1)
                    pool.memset(onesf[:], 1.0).then_inc(r_const, 1)
                    pool.iota(rank[:], pattern=[[-1, E]], base=E, channel_multiplier=0,
                              allow_small_or_imprecise_dtypes=True).then_inc(r_const, 1)
                    pool.iota(starts[:], pattern=[[BLK, NB]], base=0, channel_multiplier=0,
                              allow_small_or_imprecise_dtypes=True).then_inc(r_const, 1)
                    pool.wait_ge(r_const, 5)
                    pool.affine_select(out=before[:], in_=before[:], compare_op=ALU.is_gt, fill=0.0, base=0,
                                       pattern=[[1, P]], channel_multiplier=-1).then_inc(r_const, 1)
                    pool.wait_ge(r_rows, 16)
                    pool.wait_ge(r_pos, 1)
                    for t in range(NT):
                        pool.indirect_dma_start(hs_d, bass.IndirectOffsetOnAxis(ap=pos[:, t:t + 1], axis=0),
                                                rows[:, t, :], None).then_inc(r_scat, 16)
                    pool.wait_ge(r_scat, 16 * NT)

                @block.tensor
                def _(pe):
                    pe.wait_ge(r_const, 6)
                    pe.wait_ge(r_hot, 1)
                    flat = hotb[:].rearrange("p t e -> p (t e)")
                    pe.matmul(psR[:, 0].rearrange("p t e -> p (t e)"), before[:], flat, start=True, stop=True)
                    pe.matmul(psR[:, 1].rearrange("p t e -> p (t e)"), ones[:], flat, start=True,
                              stop=True).then_inc(r_count, 1)

                @block.vector
                def _(dve):
                    steps = [0]

                    def step(ins):
                        steps[0] += 1
                        ins.then_inc(r_step, 1)
                        dve.wait_ge(r_step, steps[0])

                    def per_tile(ap):
                        return ap[:].rearrange("p (t a) -> p t a", a=1).broadcast_to([P, NT, E])

                    def per_expert(ap):
                        return ap[:].rearrange("p (a e) -> p a e", a=1).broadcast_to([P, NT, E])

                    dve.wait_ge(r_const, 5)
                    step(dve.tensor_reduce(mx[:], logits[:], AX_X, ALU.max))
                    step(dve.tensor_tensor(eq[:], logits[:], per_tile(mx), ALU.is_equal))
                    step(dve.tensor_tensor(eq[:], eq[:], per_expert(rank), ALU.mult))
                    step(dve.tensor_reduce(mx[:], eq[:], AX_X, ALU.max))
                    step(dve.tensor_tensor(hot[:], eq[:], per_tile(mx), ALU.is_equal))
                    dve.tensor_copy(hotb[:], hot[:]).then_inc(r_hot, 1)
                    dve.wait_ge(r_count, 1)
                    for e in range(E):
                        last = dve.tensor_tensor_scan(out=run[:, :, e], data0=onesf[:], data1=psR[:, 1, :, e],
                                                      initial=0.0, op0=ALU.mult, op1=ALU.add)
                    step(last)
                    step(dve.tensor_scalar(padi[:], run[:, NT - 1, :], float(BLK - 1), None, ALU.add))
                    step(dve.tensor_scalar(padi[:], padi[:], BLK_BITS, BLK_BITS, ALU.arith_shift_right,
                                           ALU.arith_shift_left))
                    step(dve.tensor_copy(padf[:], padi[:]))
                    step(dve.tensor_tensor_scan(out=ends[:], data0=onesf[:, 0:E], data1=padf[:], initial=0.0,
                                                op0=ALU.mult, op1=ALU.add))
                    step(dve.tensor_tensor(offs[:], ends[:], padf[:], ALU.subtract))
                    step(dve.tensor_tensor(slot[:], run[:], psR[:, 1], ALU.subtract))
                    step(dve.tensor_tensor(slot[:], slot[:], psR[:, 0], ALU.add))
                    step(dve.tensor_tensor(slot[:], slot[:], per_expert(offs), ALU.add))
                    step(dve.tensor_tensor(slot[:], slot[:], hot[:], ALU.mult))
                    step(dve.tensor_reduce(posf[:], slot[:], AX_X, ALU.add))
                    dve.tensor_copy(pos[:], posf[:]).then_inc(r_pos, 1)
                    step(dve.tensor_tensor(past[:], starts[:].rearrange("p (b a) -> p b a", a=1).broadcast_to([1, NB, E]),
                                           ends[0:1, :].rearrange("p (a e) -> p a e", a=1).broadcast_to([1, NB, E]),
                                           ALU.is_ge))
                    step(dve.tensor_reduce(expf[:], past[:], AX_X, ALU.add))
                    dve.tensor_scalar(block_expert[:], expf[:], float(E - 1), None, ALU.min).then_inc(r_blocks, 1)

            F1, F2 = w1.shape[2], w2.shape[2]
            M1, M2 = F1 // P, F2 // P
            RT = BLK // P
            w1s = sb("w1s", [P, DC, F1], F32)
            w2s = sb("w2s", [P, M1, F2], F32)
            w3s = sb("w3s", [P, M2, D], F32)
            b12s = sb("b12s", [P, M1 + M2], F32)
            b3s = sb("b3s", [P, D], F32)
            hrow = sb("hrow", [P, RT, D], F32)
            hsT = sb("hsT", [P, DC, BLK], F32)
            g1 = sb("g1", [P, M1, BLK], F32)
            g2 = sb("g2", [P, M2, BLK], F32)
            yrow = sb("yrow", [P, RT, D], F32)
            psT = ps("psT", [P, DC, BLK])
            ps1 = ps("ps1", [P, 2, 2, BLK])
            ps2 = ps("ps2", [P, M2, L])
            ps3 = psR[:].rearrange("p k t e -> p (k t e)").rearrange("p (r d) -> p r d", r=RT)

            f_h = sem("f_h")
            f_w1 = sem("f_w1")
            f_w2 = [sem(f"f_w2_{k}") for k in range(2)]
            f_w3 = sem("f_w3")
            f_b12 = sem("f_b12")
            f_b3 = sem("f_b3")
            f_t = sem("f_t")
            f_hT = sem("f_hT")
            f_l1 = sem("f_l1")
            f_g1 = sem("f_g1")
            f_k2 = sem("f_k2")
            f_l2 = sem("f_l2")
            f_g2 = sem("f_g2")
            f_l3 = sem("f_l3")
            f_y = sem("f_y")
            f_st = sem("f_st")

            w1_v = w1.rearrange("e (c p) n -> e p c n", p=P)
            w2_v = w2.rearrange("e (c p) n -> e p c n", p=P)
            w3_v = w3.rearrange("e (c p) n -> e p c n", p=P)
            hs_v = hs_d.rearrange("(j r p) d -> j p r d", r=RT, p=P)
            ys_v = ys_d.rearrange("(j r p) d -> j p r d", r=RT, p=P)

            def one(view, i):
                return view[bass.ds(i, 1)].rearrange("a p c n -> (a p) c n")

            def blocks(eng, body):
                body(0)
                with eng.Fori(1, NB) as j:
                    body(j)

            half = M1 // 2
            with nc.Block() as block:
                @block.sync
                def _(sp):
                    def body(j):
                        e = sp.value_load(block_expert[0:1, bass.ds(j, 1)], min_val=0, max_val=E - 1)
                        wait(sp, f_t, j)
                        sp.dma_start(hrow[:], one(hs_v, j)).then_inc(f_h, 16)
                        wait(sp, f_l1, j * (M1 // 2))
                        sp.dma_start(w1s[:], one(w1_v, e)).then_inc(f_w1, 16)
                        for k in range(2):
                            if k == 0:
                                wait(sp, f_k2, j)
                            else:
                                wait(sp, f_l2, j * M2)
                            sp.dma_start(w2s[:, k * half:(k + 1) * half, :],
                                         one(w2_v, e)[:, k * half:(k + 1) * half, :]).then_inc(f_w2[k], 16)
                            if k == 0:
                                wait(sp, f_g2, j * M2)
                                sp.dma_start(b12s[:], b12[bass.ds(e, 1)].rearrange("a p n -> (a p) n")
                                             ).then_inc(f_b12, 16)
                        wait(sp, f_l3, j)
                        sp.dma_start(w3s[:], one(w3_v, e)).then_inc(f_w3, 16)
                        wait(sp, f_y, j)
                        sp.dma_start(b3s[:], b3[bass.ds(e, 1)].rearrange("a d -> (a d)").partition_broadcast(P)
                                     ).then_inc(f_b3, 16)
                    blocks(sp, body)

                @block.gpsimd
                def _(pool):
                    def body(j):
                        wait(pool, f_y, j + 1)
                        pool.dma_start(one(ys_v, j), yrow[:]).then_inc(f_st, 16)
                    blocks(pool, body)
                    pool.wait_ge(f_st, 16 * NB)

                @block.tensor
                def _(pe):
                    def body(j):
                        wait(pe, f_h, (j + 1) * 16)
                        wait(pe, f_hT, j)
                        for c in range(DC):
                            for r in range(RT):
                                mm = pe.transpose(psT[:, c, r * P:(r + 1) * P], hrow[:, r, c * P:(c + 1) * P], ident[:])
                        mm.then_inc(f_t, 1)
                        wait(pe, f_w1, (j + 1) * 16)
                        wait(pe, f_hT, j + 1)
                        for m in range(M1):
                            if m % 2 == 0:
                                wait(pe, f_g1, j * M1 + m - 2)
                            for c in range(DC):
                                mm = pe.matmul(ps1[:, m // 2 % 2, m % 2, :], w1s[:, c, m * P:(m + 1) * P], hsT[:, c, :],
                                               start=(c == 0), stop=(c == DC - 1))
                            if m % 2:
                                mm.then_inc(f_l1, 1)
                        wait(pe, f_g2, j * M2)
                        for k in range(M1):
                            if k % half == 0:
                                wait(pe, f_w2[k // half], (j + 1) * 16)
                            wait(pe, f_g1, j * M1 + k + 1)
                            for m in range(M2):
                                mm = pe.matmul(ps2[:, m, 0:BLK], w2s[:, k, m * P:(m + 1) * P], g1[:, k, :],
                                               start=(k == 0), stop=(k == M1 - 1))
                                if k == M1 - 1:
                                    mm.then_inc(f_l2, 1)
                            if k == half - 1:
                                mm.then_inc(f_k2, 1)
                        wait(pe, f_w3, (j + 1) * 16)
                        wait(pe, f_y, j)
                        wait(pe, f_g2, (j + 1) * M2)
                        for r in range(RT):
                            for k in range(M2):
                                mm = pe.matmul(ps3[:, r, :], g2[:, k, r * P:(r + 1) * P], w3s[:, k, :],
                                               start=(k == 0), stop=(k == M2 - 1))
                        mm.then_inc(f_l3, 1)
                    blocks(pe, body)

                @block.scalar
                def _(act):
                    def body(j):
                        wait(act, f_b12, (j + 1) * 16)
                        for m in range(M1):
                            wait(act, f_l1, j * (M1 // 2) + m // 2 + 1)
                            wait(act, f_l2, j * M2)
                            act.activation(g1[:, m, :], ps1[:, m // 2 % 2, m % 2, :], ACT.Gelu,
                                           bias=b12s[:, m:m + 1]).then_inc(f_g1, 1)
                        wait(act, f_l3, j)
                        for m in range(M2):
                            wait(act, f_l2, j * M2 + m + 1)
                            act.activation(g2[:, m, :], ps2[:, m, 0:BLK], ACT.Gelu,
                                           bias=b12s[:, M1 + m:M1 + m + 1]).then_inc(f_g2, 1)
                    blocks(act, body)

                @block.vector
                def _(dve):
                    def body(j):
                        wait(dve, f_t, j + 1)
                        wait(dve, f_l1, j * (M1 // 2))
                        dve.tensor_copy(hsT[:], psT[:]).then_inc(f_hT, 1)
                        wait(dve, f_l3, j + 1)
                        wait(dve, f_b3, (j + 1) * 16)
                        wait(dve, f_st, j * 16)
                        dve.tensor_tensor(yrow[:], ps3, b3s[:].rearrange("p (a d) -> p a d", a=1)
                                          .broadcast_to([P, RT, D]), ALU.add).then_inc(f_y, 1)
                    blocks(dve, body)

            gbb = sb("gbb", [P, B, D], F32)
            c_gb = sem("c_gb")
            c_row = [sem(f"c_row{b}") for b in range(B)]
            c_gate = sem("c_gate")
            c_sum = sem("c_sum")
            c_out = sem("c_out")
            out_v = out.rearrange("b (t p) d -> b p t d", p=P)
            with nc.Block() as block:
                @block.sync
                def _(sp):
                    sp.dma_start(gbb[:], mod_d[:, 3, :].partition_broadcast(P)).then_inc(c_gb, 16)
                    for b in range(B):
                        sp.wait_ge(c_sum, b + 1)
                        sp.dma_start(out_v[b], x2s[:, b * TT:(b + 1) * TT, :]).then_inc(c_out, 16)
                    sp.wait_ge(c_out, 16 * B)

                @block.gpsimd
                def _(pool):
                    for t in range(NT):
                        pool.indirect_dma_start(rows[:, t, :], None, ys_d,
                                                bass.IndirectOffsetOnAxis(ap=pos[:, t:t + 1], axis=0)
                                                ).then_inc(c_row[t // TT], 16)

                @block.vector
                def _(dve):
                    dve.wait_ge(c_gb, 16)
                    for b in range(B):
                        batch = slice(b * TT, (b + 1) * TT)
                        dve.wait_ge(c_row[b], 16 * TT)
                        dve.tensor_tensor(rows[:, batch, :], rows[:, batch, :],
                                          gbb[:, b:b + 1, :].broadcast_to([P, TT, D]), ALU.mult).then_inc(c_gate, 1)
                        dve.wait_ge(c_gate, b + 1)
                        dve.tensor_tensor(x2s[:, batch, :], x2s[:, batch, :], rows[:, batch, :],
                                          ALU.add).then_inc(c_sum, 1)


_INS = ["x_in", "in_wT", "conv_w", "conv_b", "xp_wT", "dt_wT", "dt_b", "a_log", "d_skip", "out_wT",
        "wr", "br", "w1", "b12", "w2", "w3", "b3", "cT", "wmod"]


def kernel(L0_attn_hidden_states, L0_attn_in_proj_w, L0_attn_conv_w, L0_attn_conv_b, L0_attn_x_proj_w,
           L0_attn_dt_proj_w, L0_attn_dt_proj_b, L0_attn_A_log, L0_attn_Dskip, L0_attn_out_proj_w,
           L0_ffn_Wr, L0_ffn_br, L0_ffn_W1, L0_ffn_b1, L0_ffn_W2, L0_ffn_b2, L0_ffn_W3, L0_ffn_b3,
           L0_c, L0_wmod):
    import numpy as np
    import concourse.bacc as bacc
    from concourse.bass_utils import run_bass_kernel_spmd

    ac = lambda a: np.ascontiguousarray(np.asarray(a))
    H = 4
    ch = lambda a: ac(np.asarray(a).reshape(H, P, *np.asarray(a).shape[1:]).swapaxes(0, 1))
    b1 = np.asarray(L0_ffn_b1)
    b2 = np.asarray(L0_ffn_b2)
    E = b1.shape[0]
    data = dict(
        x_in=ac(L0_attn_hidden_states),
        in_wT=ac(np.asarray(L0_attn_in_proj_w).T),
        conv_w=ch(np.asarray(L0_attn_conv_w)[:, 0, :]),
        conv_b=ch(L0_attn_conv_b),
        xp_wT=ac(np.asarray(L0_attn_x_proj_w).reshape(H, -1, P).transpose(2, 0, 1)),
        dt_wT=ac(np.asarray(L0_attn_dt_proj_w).T),
        dt_b=ch(L0_attn_dt_proj_b),
        a_log=ch(L0_attn_A_log),
        d_skip=ch(L0_attn_Dskip),
        out_wT=ac(np.asarray(L0_attn_out_proj_w).T),
        wr=ac(np.asarray(L0_ffn_Wr).reshape(-1, P, E).swapaxes(0, 1)),
        br=ac(L0_ffn_br),
        w1=ac(L0_ffn_W1),
        b12=ac(np.concatenate([b1.reshape(E, -1, P), b2.reshape(E, -1, P)], axis=1).transpose(0, 2, 1)),
        w2=ac(L0_ffn_W2),
        w3=ac(L0_ffn_W3),
        b3=ac(L0_ffn_b3),
        cT=ac(np.asarray(L0_c).T.reshape(-1, P, L0_c.shape[0]).swapaxes(0, 1)),
        wmod=ac(L0_wmod),
    )
    nc = bacc.Bacc("TRN2", target_bir_lowering=False, num_devices=1)
    args = [nc.dram_tensor(f"in_{n}", data[n].shape, mybir.dt.from_np(data[n].dtype), kind="ExternalInput").ap()
            for n in _INS]
    o = nc.dram_tensor("out", data["x_in"].shape, F32, kind="ExternalOutput").ap()
    build(nc, *args, o)
    r = run_bass_kernel_spmd(nc, [{f"in_{n}": data[n] for n in _INS}], core_ids=[0])
    return r.results[0]["out"]
```

```python
from contextlib import ExitStack

import concourse.bass as bass
from concourse import mybir

F32 = mybir.dt.float32
F32R = mybir.dt.float32r
BF16 = mybir.dt.bfloat16
I32 = mybir.dt.int32
U32 = mybir.dt.uint32
ALU = mybir.AluOpType
ACT = mybir.ActivationFunctionType
AX_X = mybir.AxisListType.X

P = 128
EPS = 1e-5
EXP_LN = "natural_log_exp_and_others"


def build(nc, x_in, in_wT, conv_w, conv_b, xp_wT, dt_wT, dt_b, a_log, d_skip, out_wT,
          wr, br, w1, b12, w2, w3, b3, cT, wmod, out):
    B, L, D = x_in.shape
    H = 4
    NS = a_log.shape[2]
    TT = L // P
    DC = D // P
    KC = conv_w.shape[2]
    NP = NS // 2
    DTR = dt_wT.shape[0]
    E = wr.shape[2]
    DT0 = 32
    MID, LOW = 64, 96
    NT = B * TT
    BLK_BITS = 8
    BLK = 1 << BLK_BITS
    NB = (NT * P + E * (BLK - 1)) // BLK
    FULL = NT * P // BLK

    mod_d = nc.dram_tensor("mod_rows", (B, 4, D), F32).ap()
    x2_d = nc.dram_tensor("x2_gb_rows", (NT * P, 2 * D), F32).ap()
    h2_d = nc.dram_tensor("h2_rows", (NT * P, D), F32).ap()

    with ExitStack() as outer:
        def keep(name, shape, dt):
            return outer.enter_context(nc.sbuf_tensor(name, shape, dt))

        def sem(name):
            return outer.enter_context(nc.semaphore(name))

        def wait(eng, s, v):
            if not (isinstance(v, int) and v <= 0):
                eng.wait_ge(s, v)

        logits = keep("logits", [P, NT, E], F32)
        ident = keep("ident", [P, P], F32)

        with ExitStack() as ctx:
            def sb(name, shape, dt):
                return ctx.enter_context(nc.sbuf_tensor(name, shape, dt))

            def ps(name, shape, dt=F32):
                return ctx.enter_context(nc.psum_tensor(name, shape, dt))

            in_w = sb("in_w", [P, DC, 2 * H * P], F32)
            xp_w = sb("xp_w", [P, H, P], F32)
            dt_w = sb("dt_w", [P, H * P], F32)
            out_w = sb("out_w", [P, H, D], F32)
            cw = sb("cw", [P, H, KC], F32)
            cb = sb("cb", [P, H], F32)
            dtb = sb("dtb", [P, H], F32)
            dsk = sb("dsk", [P, H], F32)
            a_neg = sb("a_neg", [P, H, NS], F32)
            wr_sb = sb("wr_sb", [P, DC, E], F32)
            br_bc = sb("br_bc", [P, E], F32)
            sel = sb("sel", [P, 2 * NS, P], BF16)
            taps = sb("taps", [P, H, KC, P], F32)
            c_sb = sb("c_sb", [P, DC, B], F32)
            sh_pp = sb("sh_pp", [P, DC, B], F32)
            sc_pp = sb("sc_pp", [P, DC, B], F32)
            modr = sb("modr", [B, 4, D], F32)
            sgn = sb("sgn", [B, 2, D], F32)
            mag = sb("mag", [B, 2, D], F32)
            xa = sb("xa", [P, TT, D], F32)
            d_xa = sem("d_xa")
            x_v = x_in.rearrange("b (t p) d -> b p t d", p=P)

            def of_batch(view, b):
                return view[bass.ds(b, 1)].rearrange("a p t d -> (a p) t d")

            psB = ps("psB", [P, 2, L])
            psC = ps("psC", [P, 2, L])
            psY = ps("psY", [P, 2, L])
            psG = ps("psG", [P, 2, L])

            s_par = sem("s_par")
            s_small = sem("s_small")
            s_wload = sem("s_wload")
            s_zero = sem("s_zero")
            s_const = sem("s_const")
            s_cact = sem("s_cact")
            s_aexp = sem("s_aexp")
            s_aneg = sem("s_aneg")
            s_taps = sem("s_taps")
            s_modps = sem("s_modps")
            s_modrow = sem("s_modrow")
            s_guard = sem("s_guard")
            s_modst = sem("s_modst")

            with nc.sbuf_tensor("wm", [P, DC, 6 * D], F32) as wm, \
                    nc.sbuf_tensor("aex", [P, H, NS], F32) as aex, \
                    nc.Block() as block:
                small = [(c_sb[:], cT), (aex[:], a_log), (cw[:], conv_w), (cb[:], conv_b), (dtb[:], dt_b),
                         (dsk[:], d_skip), (wr_sb[:], wr), (br_bc[:], br.partition_broadcast(P))]

                @block.sync
                def _(sp):
                    for dst, src in small:
                        sp.dma_start(dst, src).then_inc(s_small, 16)
                    sp.dma_start(wm[:], wmod.rearrange("(c p) n -> p c n", p=P)).then_inc(s_wload, 16)
                    sp.dma_start(in_w[:], in_wT.rearrange("(c p) n -> p c n", p=P)).then_inc(s_par, 16)
                    sp.dma_start(dt_w[DT0:DT0 + DTR, :], dt_wT).then_inc(s_par, 16)
                    sp.dma_start(out_w[:], out_wT.rearrange("(h p) n -> p h n", p=P)).then_inc(s_par, 16)
                    sp.wait_ge(s_zero, 1)
                    for at in (0, MID, LOW):
                        sp.dma_start(xp_w[:, :, at:at + 2 * NS], xp_wT[:, :, DTR:]).then_inc(s_par, 16)
                    sp.dma_start(xp_w[:, :, DT0:DT0 + DTR], xp_wT[:, :, 0:DTR]).then_inc(s_par, 16)
                    sp.dma_start(xa[:], of_batch(x_v, 0)).then_inc(d_xa, 16)
                    sp.wait_ge(s_par, 16 * 7)
                    sp.wait_ge(s_small, 16 * len(small))

                @block.gpsimd
                def _(pool):
                    pool.memset(xp_w[:], 0.0).then_inc(s_zero, 1)
                    pool.memset(ident[:], 0.0).then_inc(s_const, 1)
                    pool.memset(sel[:], 0.0).then_inc(s_const, 1)
                    pool.wait_ge(s_const, 2)
                    pool.affine_select(out=ident[:], in_=ident[:], compare_op=ALU.not_equal, fill=1.0, base=0,
                                       pattern=[[-1, P]], channel_multiplier=1).then_inc(s_const, 1)
                    for k, at in enumerate((0, MID, LOW)):
                        pool.affine_select(out=sel[:], in_=sel[:], compare_op=ALU.not_equal, fill=1.0, base=-at,
                                           pattern=[[-1, 2 * NS], [0, P]], channel_multiplier=1).then_inc(s_const, 1)
                        pool.wait_ge(s_const, 4 + k)

                @block.scalar
                def _(act):
                    act.wait_ge(s_small, 16 * len(small))
                    act.activation(c_sb[:], c_sb[:], ACT.Silu).then_inc(s_cact, 1)
                    act.activation(aex[:], aex[:], ACT.Exp).then_inc(s_aexp, 1)

                @block.tensor
                def _(pe):
                    pe.wait_ge(s_wload, 16)
                    pe.wait_ge(s_cact, 1)
                    for j in range(2 * DC):
                        for c in range(DC):
                            mm = pe.matmul(psG[:, 0, j * B:(j + 1) * B], wm[:, c, j * P:(j + 1) * P], c_sb[:, c, :],
                                           start=(c == 0), stop=(c == DC - 1))
                    mm.then_inc(s_modps, 1)
                    for j in range(2):
                        for c in range(DC):
                            mm = pe.matmul(psY[0:B, j, :], c_sb[:, c, :], wm[:, c, (2 + 2 * j) * D:(4 + 2 * j) * D],
                                           start=(c == 0), stop=(c == DC - 1))
                    mm.then_inc(s_modps, 1)

                @block.vector
                def _(dve):
                    dve.wait_ge(s_aexp, 1)
                    dve.tensor_scalar(a_neg[:], aex[:], -1.0, None, ALU.mult).then_inc(s_aneg, 1)
                    dve.wait_ge(s_const, 3)
                    dve.wait_ge(s_small, 16 * len(small))
                    for h in range(H):
                        for k in range(KC):
                            dve.tensor_scalar(taps[:, h, k, :], ident[:], cw[:, h, k:k + 1], None,
                                              ALU.mult).then_inc(s_taps, 1)
                    dve.wait_ge(s_modps, 2)
                    pp = psG[:, 0, 0:2 * DC * B].rearrange("p (k c b) -> p k c b", k=2, c=DC)
                    dve.tensor_copy(sh_pp[:], pp[:, 0]).then_inc(s_modrow, 1)
                    dve.tensor_scalar(sc_pp[:], pp[:, 1], 1.0, None, ALU.add).then_inc(s_modrow, 1)

            xr = sb("xr", [P, TT, D], F32)
            mbc = sb("mbc", [P, 4, D], F32)
            xn = sb("xn", [P, TT, D], F32)
            x2b = sb("x2b", [P, TT, D], F32)
            h2n = sb("h2n", [P, TT, D], F32)
            st1 = sb("st1", [P, TT, 6], F32)
            mv1 = sb("mv1", [P, TT, 2], F32)
            rs1 = sb("rs1", [P, 4, TT], F32)
            st2 = sb("st2", [P, TT, 6], F32)
            mv2 = sb("mv2", [P, TT, 2], F32)
            rs2 = sb("rs2", [P, 4, TT], F32)
            hT = sb("hT", [P, DC, L], F32)
            h2T = sb("h2T", [P, DC, L], F32)
            xpad = sb("xpad", [P, KC - 1 + L], F32)
            u = sb("u", [P, 2, L], F32)
            ud = sb("ud", [P, L], F32)
            zs = sb("zs", [P, H, L], F32)
            xds = sb("xds", [P, L], F32)
            bc3 = sb("bc3", [P, 2, L], BF16)
            bcr = sb("bcr", [P, L], F32)
            sp_a = sb("sp_a", [P, L], F32)
            sp_r = sb("sp_r", [P, L], F32)
            sp_e = sb("sp_e", [P, L], F32)
            sp_l = sb("sp_l", [P, L], F32)
            sp_w = sb("sp_w", [P, L], F32)
            delta = sb("delta", [P, 2, L], F32)
            du = sb("du", [P, 2, L], F32)
            RA, RS, RC, RP = 4, 4, 4, 4
            LAG = 2
            dA = sb("dA", [P, RA, 2, L], F32)
            dBu = sb("dBu", [P, 2, 2, L], F32)
            st = sb("st", [P, RS, 2, L], F32)
            cbr = sb("cbr", [P, RC, 2, L], F32)
            sc = sb("sc", [P, RP, 2, L], F32)
            yg = sb("yg", [P, TT, P], F32)
            yT = sb("yT", [P, H, L], F32)
            y0 = sb("y0", [P, L], F32)

            d_xr = sem("d_xr")
            d_mbc = sem("d_mbc")
            d_x2 = sem("d_x2")
            d_h2 = sem("d_h2")
            s_st1 = sem("s_st1")
            s_mv1 = sem("s_mv1")
            s_ve1 = sem("s_ve1")
            s_rg1 = sem("s_rg1")
            s_rs1 = sem("s_rs1")
            s_xn1 = sem("s_xn1")
            s_t1 = sem("s_t1")
            s_hT = sem("s_hT")
            s_padz = sem("s_padz")
            s_xin = sem("s_xin")
            s_xpad = sem("s_xpad")
            s_conv = sem("s_conv")
            s_u = sem("s_u")
            s_zin = sem("s_zin")
            s_zs = sem("s_zs")
            s_xd = sem("s_xd")
            s_cast = sem("s_cast")
            s_xds = sem("s_xds")
            s_split = sem("s_split")
            s_dtp = sem("s_dtp")
            s_spa = sem("s_spa")
            s_spr = sem("s_spr")
            s_spe = sem("s_spe")
            s_spl = sem("s_spl")
            s_delta = sem("s_delta")
            s_w = sem("s_w")
            s_ln = sem("s_ln")
            s_du = sem("s_du")
            s_B = sem("s_B")
            s_C = sem("s_C")
            s_cev = sem("s_cev")
            s_mulB = sem("s_mulB")
            s_scan = sem("s_scan")
            s_prod = sem("s_prod")
            s_sum = sem("s_sum")
            s_dA = sem("s_dA")
            s_ud = sem("s_ud")
            s_udt = sem("s_udt")
            s_gate = sem("s_gate")
            s_back = sem("s_back")
            s_yT = sem("s_yT")
            s_y0 = sem("s_y0")
            s_out = sem("s_out")
            s_gated = sem("s_gated")
            s_x2 = sem("s_x2")
            s_st2 = sem("s_st2")
            s_mv2 = sem("s_mv2")
            s_ve2 = sem("s_ve2")
            s_rg2 = sem("s_rg2")
            s_rs2 = sem("s_rs2")
            s_xn2 = sem("s_xn2")
            s_mod2 = sem("s_mod2")
            s_h2 = sem("s_h2")
            s_t2 = sem("s_t2")
            s_h2T = sem("s_h2T")
            s_rt = sem("s_rt")
            s_lg = sem("s_lg")

            x2_v = x2_d.rearrange("(b t p) d -> b p t d", t=TT, p=P)
            h2_v = h2_d.rearrange("(b t p) d -> b p t d", t=TT, p=P)

            def batches(eng, body):
                body(0, True, False, False)
                body(1, False, True, False)
                with eng.Fori(2, B - 1) as b:
                    body(b, False, False, False)
                body(B - 1, False, False, True)

            with nc.Block() as block:
                @block.sync
                def _(sp):
                    def load_tokens(b):
                        wait(sp, s_xn1, b * TT)
                        sp.dma_start(xa[:], of_batch(x_v, b)).then_inc(d_xa, 16)

                    def load_tail(b):
                        wait(sp, s_x2, b * 2)
                        sp.dma_start(xr[:], of_batch(x_v, b)).then_inc(d_xr, 16)
                        wait(sp, d_x2, b * 32)
                        wait(sp, s_h2, b)
                        sp.dma_start(mbc[:].rearrange("p k d -> p (k d)"),
                                     mod_d[bass.ds(b, 1)].rearrange("a k d -> (a k d)").partition_broadcast(P)
                                     ).then_inc(d_mbc, 16)

                    def store_tail(b):
                        wait(sp, s_x2, (b + 1) * 2)
                        sp.dma_start(of_batch(x2_v, b)[:, :, 0:D], x2b[:]).then_inc(d_x2, 16)
                        sp.dma_start(of_batch(x2_v, b)[:, :, D:], mbc[:, 3:4, :].broadcast_to([P, TT, D])
                                     ).then_inc(d_x2, 16)
                        wait(sp, s_h2, b + 1)
                        sp.dma_start(of_batch(h2_v, b), h2n[:]).then_inc(d_h2, 16)

                    def body(b, first, second, last):
                        if not first:
                            load_tail(b - 1)
                        if not last:
                            load_tokens(b + 1)
                        if not first:
                            store_tail(b - 1)
                    sp.wait_ge(s_modrow, 6)
                    sp.dma_start(mod_d, modr[:]).then_inc(s_modst, 16)
                    sp.wait_ge(s_modst, 16)
                    batches(sp, body)
                    load_tail(B - 1)
                    store_tail(B - 1)
                    sp.wait_ge(d_x2, 32 * B)
                    sp.wait_ge(d_h2, 16 * B)

                @block.tensor
                def _(pe):
                    def xdbl_mm(v, h):
                        wait(pe, s_u, v + 1)
                        pe.matmul(psG[:, 0, :], xp_w[:, h, :], u[:, h % 2, :], start=True, stop=True).then_inc(s_xd, 1)

                    def dt_mm(v, h):
                        wait(pe, s_xds, v + 1)
                        pe.matmul(psG[:, 1, :], dt_w[DT0:DT0 + DTR, h * P:(h + 1) * P], xds[DT0:DT0 + DTR, :],
                                  start=True, stop=True).then_inc(s_dtp, 1)

                    def xin_mm(v, h):
                        for c in range(DC):
                            mm = pe.matmul(psG[:, 0, :], in_w[:, c, h * P:(h + 1) * P], hT[:, c, :],
                                           start=(c == 0), stop=(c == DC - 1))
                        mm.then_inc(s_xin, 1)

                    def zin_mm(v, h):
                        for t in range(TT):
                            for c in range(DC):
                                mm = pe.matmul(psG[:, 1, t * P:(t + 1) * P], hT[:, c, t * P:(t + 1) * P],
                                               in_w[:, c, (H + h) * P:(H + h + 1) * P],
                                               start=(c == 0), stop=(c == DC - 1))
                        mm.then_inc(s_zin, 1)

                    def conv_mm(v, h, part):
                        wait(pe, s_xpad, v + 1)
                        for k in range(part * KC // 2, (part + 1) * KC // 2):
                            mm = pe.matmul(psG[:, 0, :], taps[:, h, k, :], xpad[:, k:k + L],
                                           start=(k == 0), stop=(k == KC - 1))
                        if part == 1:
                            mm.then_inc(s_conv, 1)

                    def back(q):
                        wait(pe, s_gate, q + 1)
                        for t in range(TT):
                            mm = pe.transpose(psG[:, 1, t * P:(t + 1) * P], yg[:, t, :], ident[:])
                        mm.then_inc(s_back, 1)

                    def out_mm(t, bank):
                        for h in range(H):
                            mm = pe.matmul(psG[:, bank, (t % 2) * D:(t % 2 + 1) * D], yT[:, h, t * P:(t + 1) * P],
                                           out_w[:, h, :], start=(h == 0), stop=(h == H - 1))
                        if t % 2:
                            mm.then_inc(s_out, 1)

                    def turn(src, c, bank, done):
                        for t in range(TT):
                            mm = pe.transpose(psG[:, bank, t * P:(t + 1) * P], src[:, t, c * P:(c + 1) * P], ident[:])
                        mm.then_inc(done, 1)

                    def router_mm(b):
                        wait(pe, s_h2T, (b + 1) * DC)
                        for t in range(TT):
                            for c in range(DC):
                                mm = pe.matmul(psG[:, 1, t * E:(t + 1) * E], h2T[:, c, t * P:(t + 1) * P],
                                               wr_sb[:, c, :], start=(c == 0), stop=(c == DC - 1))
                        mm.then_inc(s_rt, 1)

                    def broadcast(q, h, g):
                        p = q * NP + g
                        if g == 0:
                            wait(pe, s_split, (q + 1) * 3)
                        wait(pe, s_mulB, p)
                        for i in range(2):
                            mm = pe.matmul(psB[:, i, :], sel[:, 2 * g + i, :], bc3[:, h % 2, :], start=True, stop=True)
                        mm.then_inc(s_B, 1)
                        wait(pe, s_cev, p)
                        for i in range(2):
                            mm = pe.matmul(psC[:, i, :], sel[:, NS + 2 * g + i, :], bc3[:, h % 2, :],
                                           start=True, stop=True)
                        mm.then_inc(s_C, 1)

                    def turn_add(h, src, first, last):
                        for t in range(TT):
                            mm = pe.matmul(psY[:, h % 2, t * P:(t + 1) * P], src[:, t * P:(t + 1) * P], ident[:],
                                           is_transpose=True, start=first and t == 0, stop=last and t == TT - 1,
                                           skip_group_check=True)
                        return mm

                    def skip_term(q, h):
                        wait(pe, s_gate, q - 1)
                        wait(pe, s_ud, q + 1)
                        turn_add(h, ud, True, False).then_inc(s_udt, 1)

                    def sums(q, h, g):
                        wait(pe, s_prod, q * NP + g + 1)
                        for i in range(2):
                            mm = turn_add(h, sc[:, g % RP, i, :], False, g == NP - 1 and i == 1)
                        mm.then_inc(s_sum, 1)

                    def guest(b, h, k, first, last):
                        if h == 0 and not first:
                            wait(pe, s_yT, b * H)
                            wait(pe, s_y0, b)
                            out_mm(k, 0)
                        if h == 1 and not last:
                            wait(pe, s_xn1, (b + 2) * TT)
                            if k == 1:
                                wait(pe, s_hT, (b + 1) * DC + 1)
                            else:
                                wait(pe, s_zs, b * H + 4)
                            turn(xn, k, 1, s_t1)
                        if h == 1 and not first:
                            out_mm(2 + k, 0)
                        if h == 3 and not first:
                            wait(pe, s_h2, b)
                            turn(h2n, k, k, s_t2)

                    def guest_left(b, h, k, first, last):
                        if h == 0 and k == 0 and not first:
                            wait(pe, s_gated, (b - 1) * 2 + 1)
                        if h == 1 and k == 0 and not first:
                            wait(pe, s_gated, b * 2)
                        if h == 1 and k == 1 and not last:
                            wait(pe, s_hT, (b + 2) * DC)
                        if h == 3 and not first:
                            wait(pe, s_h2T, (b - 1) * DC + k + 1)

                    def guest_before(b, h, k, first, second, last):
                        if h > 0:
                            guest_left(b, h - 1, k, first, last)
                        elif not (first or second):
                            guest_left(b - 1, H - 1, k, False, False)

                    def unit(b, h, first, second, last):
                        q = b * H + h
                        vb, hb = q + 1, (h + 1) % H
                        va, ha = q + 2, (h + 2) % H
                        prep_b = not (last and h == H - 1)
                        prep_a = not (last and h >= H - 2)
                        for g in range(NP):
                            broadcast(q, h, g)
                            if g >= LAG:
                                sums(q, h, g - LAG)
                            elif not (first and h == 0):
                                sums(q - 1, (h + 1) % 2, NP - LAG + g)
                            if g == LAG - 1:
                                skip_term(q, h)
                            if g == 0:
                                if prep_b:
                                    wait(pe, s_u, vb + 1)
                                    guest_before(b, h, 0, first, second, last)
                                    xdbl_mm(vb, hb)
                            if g == 1 and prep_b:
                                wait(pe, s_zs, vb + 1)
                                guest_before(b, h, 1, first, second, last)
                                if h == 0 and not (first or second):
                                    wait(pe, s_lg, b - 1)
                                dt_mm(vb, hb)
                            if g == 2 and prep_a:
                                wait(pe, s_xds, vb + 1)
                                if h == 2:
                                    wait(pe, s_hT, (b + 2) * DC)
                                xin_mm(va, ha)
                            if g == 3 and not (first and h == 0):
                                if prep_b:
                                    wait(pe, s_spr, vb + 1)
                                else:
                                    wait(pe, s_yT, q - 1)
                                back(q - 1)
                            if g in (3, 4) and prep_a:
                                conv_mm(va, ha, g - 3)
                            if g == 5 and prep_a:
                                wait(pe, s_spr, vb + 1)
                                wait(pe, s_yT, q)
                                zin_mm(va, ha)
                            if g in (6, 7):
                                if g == 6 and prep_a:
                                    wait(pe, s_u, va + 1)
                                elif g == 6:
                                    wait(pe, s_xds, vb + 1 if prep_b else vb)
                                elif prep_a:
                                    wait(pe, s_zs, va + 1)
                                else:
                                    wait(pe, s_yT, q)
                                guest(b, h, g - 6, first, last)
                            if g == 0 and h == 0 and not (first or second):
                                wait(pe, s_zs, vb + 1)
                                guest_before(b, h, 1, first, second, last)
                                router_mm(b - 2)

                    wait(pe, s_xn1, TT)
                    for c in range(DC):
                        turn(xn, c, c, s_t1)
                    wait(pe, s_hT, DC)
                    for v in range(2):
                        if v == 1:
                            wait(pe, s_xds, 1)
                        xin_mm(v, v)
                        if v == 1:
                            wait(pe, s_spr, 1)
                        zin_mm(v, v)
                        for k in range(2):
                            conv_mm(v, v, k)
                        if v == 0:
                            xdbl_mm(0, 0)
                            wait(pe, s_zs, 1)
                            dt_mm(0, 0)

                    def body(b, first, second, last):
                        for h in range(H):
                            unit(b, h, first, second, last)
                    wait(pe, s_modrow, 6)
                    batches(pe, body)
                    for g in range(NP - LAG, NP):
                        sums(B * H - 1, H - 1, g)
                    router_mm(B - 2)
                    wait(pe, s_lg, B - 1)
                    back(B * H - 1)
                    wait(pe, s_yT, B * H)
                    wait(pe, s_y0, B)
                    for t in range(TT):
                        out_mm(t, t // 2)
                    wait(pe, s_h2, B)
                    for k in range(2):
                        wait(pe, s_gated, (B - 1) * 2 + k + 1)
                        turn(h2n, k, k, s_t2)
                    router_mm(B - 1)

                @block.scalar
                def _(act):
                    def x_copy(v):
                        wait(act, s_xin, v + 1)
                        wait(act, s_conv, v)
                        act.activation(xpad[:, KC - 1:], psG[:, 0, :], ACT.Copy).then_inc(s_xpad, 1)

                    def silus(v, h):
                        wait(act, s_conv, v + 1)
                        wait(act, s_xd, v - 1)
                        wait(act, s_du, v - 1)
                        act.activation(u[:, h % 2, :], psG[:, 0, :], ACT.Silu, bias=cb[:, h:h + 1]).then_inc(s_u, 1)
                        wait(act, s_zin, v + 1)
                        wait(act, s_gate, v - 3)
                        act.activation(zs[:, h, :], psG[:, 1, :], ACT.Silu).then_inc(s_zs, 1)

                    def xd_copy(v, h):
                        wait(act, s_xd, v + 1)
                        wait(act, s_C, (v - 1) * NP)
                        act.activation(bc3[:, h % 2, :], psG[:, 0, :], ACT.Copy).then_inc(s_cast, 1)
                        wait(act, s_split, v * 3)
                        wait(act, s_dtp, v)
                        act.activation(xds[:], psG[:, 0, :], ACT.Copy).then_inc(s_xds, 1)

                    def y_copy(q, h):
                        wait(act, s_back, q + 1)
                        act.activation(yT[:, h, :] if h else y0[:], psG[:, 1, :], ACT.Copy).then_inc(s_yT, 1)

                    def put_y0(b):
                        wait(act, s_yT, b * H + 1)
                        wait(act, s_out, b * 2)
                        act.activation(yT[:, 0, :], y0[:], ACT.Copy).then_inc(s_y0, 1)

                    def softplus(v, h):
                        wait(act, s_dtp, v + 1)
                        wait(act, s_delta, v * 3)
                        act.activation(sp_a[:], psG[:, 1, :], ACT.Abs, bias=dtb[:, h:h + 1]).then_inc(s_spa, 1)
                        act.activation(sp_r[:], psG[:, 1, :], ACT.Relu, bias=dtb[:, h:h + 1]).then_inc(s_spr, 1)

                    def softplus_logs(v):
                        wait(act, s_spa, v + 1)
                        act.activation(sp_e[:], sp_a[:], ACT.Exp, scale=-1.0).then_inc(s_spe, 1)
                        wait(act, s_spe, v + 1)
                        act.activation(sp_l[:], sp_e[:], ACT.Ln, bias=1.0).then_inc(s_spl, 1)

                    def decays(q, h, g):
                        p = q * NP + g
                        if g == 0:
                            wait(act, s_delta, (q + 1) * 3)
                        wait(act, s_scan, p - RA + 1)
                        for i in range(2):
                            n = 2 * g + i
                            act.activation(dA[:, g % RA, i, :], delta[:, h % 2, :], ACT.Exp,
                                           scale=a_neg[:, h, n:n + 1]).then_inc(s_dA, 1)

                    def c_copy(q, g):
                        p = q * NP + g
                        wait(act, s_C, p + 1)
                        wait(act, s_prod, p - RC + 1)
                        act.activation(cbr[:, g % RC], psC[:], ACT.Copy).then_inc(s_cev, 1)

                    def modulated(b, c, bank):
                        wait(act, s_t1, b * DC + c + 1)
                        act.activation(hT[:, c, :], psG[:, bank, :], ACT.Identity, bias=sh_pp[:, c, bass.ds(b, 1)],
                                       scale=sc_pp[:, c, bass.ds(b, 1)]).then_inc(s_hT, 1)

                    def h2_copy(b, c):
                        wait(act, s_t2, b * DC + c + 1)
                        act.activation(h2T[:, c, :], psG[:, c, :], ACT.Copy).then_inc(s_h2T, 1)

                    def guess_rstd(b, rs, before, done):
                        wait(act, before, b + 1)
                        act.activation(rs[:, 1, :], rs[:, 0, :], ACT.Ln).then_inc(done, 1)
                        wait(act, done, b * 2 + 1)
                        act.activation(rs[:, 1, :], rs[:, 1, :], ACT.Exp, scale=-0.5).then_inc(done, 1)

                    def unit(b, h, first, second, last):
                        q = b * H + h
                        vb, hb = q + 1, (h + 1) % H
                        va, ha = q + 2, (h + 2) % H
                        prep_b = not (last and h == H - 1)
                        prep_a = not (last and h >= H - 2)
                        for g in range(NP):
                            back_to_exp = g == NP - 2 and prep_a
                            if back_to_exp:
                                c_copy(q, g)
                                act.preload_act_table_set(EXP_LN)
                            if g < NP - 1:
                                decays(q, h, g + 1)
                            elif prep_b:
                                decays(vb, hb, 0)
                            if not back_to_exp:
                                c_copy(q, g)
                            if g == 0 and prep_b:
                                xd_copy(vb, hb)
                            if g == 1 and prep_b:
                                softplus(vb, hb)
                            if g == 2 and prep_b:
                                softplus_logs(vb)
                            if g == 2 and prep_a:
                                x_copy(va)
                            if g == 3 and not (first and h == 0):
                                y_copy(q - 1, (h + H - 1) % H)
                            if h == 2 and g == 0:
                                put_y0(b)
                            if h == 2 and g == 2 and not first:
                                guess_rstd(b - 1, rs2, s_ve2, s_rg2)
                            if h == 0 and g == NP - 3 and not last:
                                guess_rstd(b + 1, rs1, s_ve1, s_rg1)
                            if g == NP - 3 and prep_a:
                                silus(va, ha)
                            if g in (6, 7):
                                if h == 1 and not last:
                                    modulated(b + 1, g - 6, 1)
                                if h == 3 and not first:
                                    h2_copy(b - 1, g - 6)

                    guess_rstd(0, rs1, s_ve1, s_rg1)
                    for c in range(DC):
                        modulated(0, c, c)
                    wait(act, s_padz, 1)
                    x_copy(0)
                    silus(0, 0)
                    xd_copy(0, 0)
                    softplus(0, 0)
                    x_copy(1)
                    silus(1, 1)
                    act.preload_act_table_set(EXP_LN)
                    softplus_logs(0)
                    decays(0, 0, 0)

                    def body(b, first, second, last):
                        for h in range(H):
                            unit(b, h, first, second, last)
                    batches(act, body)
                    y_copy(B * H - 1, H - 1)
                    guess_rstd(B - 1, rs2, s_ve2, s_rg2)
                    for c in range(DC):
                        h2_copy(B - 1, c)

                @block.gpsimd
                def _(pool):
                    pool.memset(xpad[:, 0:KC - 1], 0.0).then_inc(s_padz, 1)

                    def split(v, h, k):
                        wait(pool, s_cast, v + 1)
                        wait(pool, s_xds, v + 1)
                        wait(pool, s_split, v * 3 + k)
                        dst, a, b = ((bcr[MID:], xds[MID:], bc3[MID:, h % 2, :]),
                                           (bc3[MID:, h % 2, :], xds[MID:], bc3[MID:, h % 2, :]),
                                           (bc3[LOW:, h % 2, :], bcr[LOW:], bc3[LOW:, h % 2, :]))[k]
                        pool.tensor_tensor(dst, a, b, ALU.subtract).then_inc(s_split, 1)
                        wait(pool, s_split, v * 3 + k + 1)

                    def put_delta(v, h, k):
                        wait(pool, s_ln, v + 1)
                        wait(pool, s_delta, v * 3 + k)
                        if k == 0:
                            pool.tensor_tensor(sp_w[:], sp_e[:], sp_w[:], ALU.subtract).then_inc(s_delta, 1)
                        if k == 1:
                            pool.tensor_tensor(sp_w[:], sp_l[:], sp_w[:], ALU.add).then_inc(s_delta, 1)
                        if k == 2:
                            wait(pool, s_spr, v + 1)
                            wait(pool, s_dA, (v - 1) * NS)
                            wait(pool, s_du, v - 1)
                            pool.tensor_tensor(delta[:, h % 2, :], sp_w[:], sp_r[:], ALU.add).then_inc(s_delta, 1)

                    def product(q, g):
                        p = q * NP + g
                        wait(pool, s_cev, p + 1)
                        wait(pool, s_scan, p + 1)
                        wait(pool, s_sum, p - RP + 1)
                        pool.tensor_tensor(sc[:, g % RP], st[:, g % RS], cbr[:, g % RC], ALU.mult).then_inc(s_prod, 1)

                    wait(pool, s_padz, 1)
                    for k in range(3):
                        split(0, 0, k)
                    for k in range(3):
                        put_delta(0, 0, k)

                    def body(b, first, second, last):
                        for h in range(H):
                            q = b * H + h
                            v = q + 1
                            vh = (h + 1) % H
                            prep = not (last and h == H - 1)
                            for g in range(NP):
                                product(q, g)
                                if g in (0, 1, 2) and prep:
                                    wait(pool, s_prod, q * NP + g + 1)
                                    split(v, vh, g)
                                if g in (3, 4, 5) and prep:
                                    put_delta(v, vh, g - 3)
                    batches(pool, body)

                @block.vector
                def _(dve):
                    def stats(src, out, done):
                        for t in range(TT):
                            dve.bn_stats(out[:, t, :], src[:, t, :]).then_inc(done, 1)

                    def aggregate(b, stat, mv, rs, done_mv, done_ve):
                        for t in range(TT):
                            dve.bn_aggr(mv[:, t, :], stat[:, t, :]).then_inc(done_mv, 1)
                        plus_eps(b, mv, rs, done_mv, done_ve)

                    def plus_eps(b, mv, out, before, done):
                        wait(dve, before, (b + 1) * TT)
                        dve.tensor_scalar(out[:, 0, :], mv[:, :, 1], EPS, None, ALU.add).then_inc(done, 1)

                    def refine(b, rs, guess, done):
                        wait(dve, guess, (b + 1) * 2)
                        for k, (o, x, y) in enumerate(((2, 0, 1), (2, 2, 1))):
                            dve.tensor_tensor(rs[:, o, :], rs[:, x, :], rs[:, y, :], ALU.mult).then_inc(done, 1)
                            wait(dve, done, b * 4 + k + 1)
                        dve.tensor_scalar(rs[:, 2, :], rs[:, 2, :], -0.5, 1.5, ALU.mult, ALU.add).then_inc(done, 1)
                        wait(dve, done, b * 4 + 3)
                        dve.tensor_tensor(rs[:, 3, :], rs[:, 2, :], rs[:, 1, :], ALU.mult).then_inc(done, 1)

                    def centre(b, t, src, mv, rs, dst, before, done):
                        wait(dve, before, (b + 1) * 4)
                        dve.tensor_scalar(dst[:, t, :], src[:, t, :], mv[:, t, 0:1], rs[:, 3, t:t + 1],
                                          ALU.subtract, ALU.mult).then_inc(done, 1)

                    def norm1_stats(b):
                        wait(dve, d_xa, (b + 1) * 16)
                        stats(xa, st1, s_st1)

                    def norm1(b):
                        wait(dve, s_t1, b * DC)
                        for t in range(TT):
                            centre(b, t, xa, mv1, rs1, xn, s_rs1, s_xn1)

                    def residual(b, k, bank):
                        two = slice(2 * k, 2 * k + 2)
                        wait(dve, s_out, b * 2 + k + 1)
                        wait(dve, d_mbc, (b + 1) * 16)
                        wait(dve, d_xr, (b + 1) * 16)
                        wait(dve, d_x2, b * 32)
                        dve.tensor_tensor(x2b[:, two, :], psG[:, bank, :].rearrange("p (t d) -> p t d", t=2),
                                          mbc[:, 0:1, :].broadcast_to([P, 2, D]), ALU.mult).then_inc(s_gated, 1)
                        wait(dve, s_gated, b * 2 + k + 1)
                        dve.tensor_tensor(x2b[:, two, :], x2b[:, two, :], xr[:, two, :], ALU.add).then_inc(s_x2, 1)

                    def norm2_stats(b):
                        wait(dve, s_x2, (b + 1) * 2)
                        stats(x2b, st2, s_st2)

                    def norm2(b):
                        wait(dve, s_t2, b * DC)
                        wait(dve, d_h2, b * 16)
                        for t in range(TT):
                            centre(b, t, x2b, mv2, rs2, h2n, s_rs2, s_xn2)

                    def scale2(b):
                        wait(dve, s_xn2, (b + 1) * TT)
                        dve.tensor_tensor(h2n[:], h2n[:], mbc[:, 2:3, :].broadcast_to([P, TT, D]),
                                          ALU.mult).then_inc(s_mod2, 1)

                    def shift2(b):
                        wait(dve, s_mod2, b + 1)
                        dve.tensor_tensor(h2n[:], h2n[:], mbc[:, 1:2, :].broadcast_to([P, TT, D]),
                                          ALU.add).then_inc(s_h2, 1)

                    def logits_out(b):
                        wait(dve, s_rt, b + 1)
                        dve.tensor_tensor(logits[:, bass.ds(b * TT, TT), :],
                                          psG[:, 1, 0:TT * E].rearrange("p (t e) -> p t e", t=TT),
                                          br_bc[:].rearrange("p (a e) -> p a e", a=1).broadcast_to([P, TT, E]),
                                          ALU.add).then_inc(s_lg, 1)

                    def rounded(v):
                        wait(dve, s_spe, v + 1)
                        wait(dve, s_delta, v * 3)
                        dve.tensor_scalar(sp_w[:], sp_e[:], 1.0, 1.0, ALU.add, ALU.subtract).then_inc(s_w, 1)
                        wait(dve, s_w, v + 1)
                        wait(dve, s_spl, v + 1)
                        dve.scalar_tensor_tensor(out=sp_l[:], in0=sp_w[:], scalar=0.0, in1=sp_l[:],
                                                 op0=ALU.is_gt, op1=ALU.mult).then_inc(s_ln, 1)

                    def delta_u(v, h):
                        wait(dve, s_delta, (v + 1) * 3)
                        dve.tensor_tensor(du[:, h % 2, :], delta[:, h % 2, :], u[:, h % 2, :],
                                          ALU.mult).then_inc(s_du, 1)

                    def skip(v, h):
                        wait(dve, s_u, v + 1)
                        wait(dve, s_udt, v)
                        dve.tensor_scalar(ud[:], u[:, h % 2, :], dsk[:, h:h + 1], None, ALU.mult).then_inc(s_ud, 1)

                    def gate(q, h):
                        wait(dve, s_sum, (q + 1) * NP)
                        wait(dve, s_back, q)
                        dve.tensor_tensor(yg[:].rearrange("p t d -> p (t d)"), psY[:, h % 2, :], zs[:, h, :],
                                          ALU.mult).then_inc(s_gate, 1)

                    def scans(q, h, g):
                        p = q * NP + g
                        if g == 0:
                            wait(dve, s_du, q + 1)
                        wait(dve, s_B, p + 1)
                        dve.tensor_tensor(dBu[:, g % 2], psB[:], du[:, h % 2:h % 2 + 1, :].broadcast_to([P, 2, L]),
                                          ALU.mult).then_inc(s_mulB, 1)
                        wait(dve, s_mulB, p + 1)
                        wait(dve, s_prod, p - RS + 1)
                        for i in range(2):
                            wait(dve, s_dA, q * NS + 2 * g + i + 1)
                            last = dve.tensor_tensor_scan(out=st[:, g % RS, i, :], data0=dA[:, g % RA, i, :],
                                                          data1=dBu[:, g % 2, i, :], initial=0.0,
                                                          op0=ALU.mult, op1=ALU.add)
                        last.then_inc(s_scan, 1)

                    def guard_gates():
                        gates = [psY[0:B, 0, 0:D], psY[0:B, 1, D:2 * D]]
                        for k in range(2):
                            dve.tensor_copy(mag[:, k, :], gates[k]).then_inc(s_guard, 1)
                            dve.tensor_scalar(sgn[:, k, :], gates[k], 0.0, 2.0, ALU.is_ge, ALU.mult).then_inc(s_guard, 1)
                            dve.wait_ge(s_guard, 4 * k + 2)
                            dve.tensor_scalar(sgn[:, k, :], sgn[:, k, :], 1.0, None, ALU.subtract).then_inc(s_guard, 1)
                            dve.scalar_tensor_tensor(out=mag[:, k, :], in0=mag[:, k, :], scalar=-1.0, in1=mag[:, k, :],
                                                     op0=ALU.mult, op1=ALU.max).then_inc(s_guard, 1)
                            dve.wait_ge(s_guard, 4 * k + 4)
                            dve.scalar_tensor_tensor(out=modr[:, 3 * k, :], in0=mag[:, k, :], scalar=0.25,
                                                     in1=sgn[:, k, :], op0=ALU.max, op1=ALU.mult).then_inc(s_modrow, 1)
                        dve.tensor_copy(modr[:, 1, :], psY[0:B, 0, D:2 * D]).then_inc(s_modrow, 1)
                        dve.tensor_scalar(modr[:, 2, :], psY[0:B, 1, 0:D], 1.0, None, ALU.add).then_inc(s_modrow, 1)

                    norm1_stats(0)
                    wait(dve, s_st1, TT)
                    aggregate(0, st1, mv1, rs1, s_mv1, s_ve1)
                    refine(0, rs1, s_rg1, s_rs1)
                    norm1(0)
                    guard_gates()
                    rounded(0)
                    delta_u(0, 0)
                    skip(0, 0)

                    def body(b, first, second, last):
                        for h in range(H):
                            q = b * H + h
                            for g in range(NP):
                                if h == 2 and g == 1 and not first:
                                    wait(dve, s_st2, b * TT)
                                if h == 0 and g == 4 and not last:
                                    wait(dve, s_st1, (b + 2) * TT)
                                scans(q, h, g)
                                prep = not (last and h == H - 1)
                                if g == LAG and not (first and h == 0):
                                    gate(q - 1, (h + H - 1) % H)
                                if g == 2 and prep:
                                    rounded(q + 1)
                                if g == 4 and prep:
                                    skip(q + 1, (h + 1) % H)
                                if g == 7 and prep:
                                    delta_u(q + 1, (h + 1) % H)
                                if h == 0 and not last:
                                    if g == 3:
                                        norm1_stats(b + 1)
                                    if g == 4:
                                        aggregate(b + 1, st1, mv1, rs1, s_mv1, s_ve1)
                                    if g == 6:
                                        refine(b + 1, rs1, s_rg1, s_rs1)
                                if h == 1 and g == 1 and not last:
                                    norm1(b + 1)
                                if first:
                                    continue
                                if h in (0, 1) and g == 7:
                                    residual(b - 1, h, 0)
                                if h == 2 and g == 0:
                                    norm2_stats(b - 1)
                                if h == 2 and g == 1:
                                    aggregate(b - 1, st2, mv2, rs2, s_mv2, s_ve2)
                                if h == 2 and g == 5:
                                    refine(b - 1, rs2, s_rg2, s_rs2)
                                if h == 2 and g == 6:
                                    norm2(b - 1)
                                if h == 3 and g == 0:
                                    scale2(b - 1)
                                if h == 3 and g == 1:
                                    shift2(b - 1)
                                if h == 0 and g == 0 and not second:
                                    logits_out(b - 2)
                    batches(dve, body)
                    logits_out(B - 2)
                    gate(B * H - 1, H - 1)
                    for k in range(2):
                        residual(B - 1, k, k)
                    norm2_stats(B - 1)
                    wait(dve, s_st2, B * TT)
                    aggregate(B - 1, st2, mv2, rs2, s_mv2, s_ve2)
                    refine(B - 1, rs2, s_rg2, s_rs2)
                    norm2(B - 1)
                    scale2(B - 1)
                    shift2(B - 1)
                    logits_out(B - 1)

        with ExitStack() as ctx:
            def sb(name, shape, dt):
                return ctx.enter_context(nc.sbuf_tensor(name, shape, dt))

            def ps(name, shape, dt=F32):
                return ctx.enter_context(nc.psum_tensor(name, shape, dt))

            NS_T = NB * BLK // P
            QT = NT // 4
            P_BITS = P.bit_length() - 1
            NOWHERE = float(4 * NT * P)
            mx = sb("mx", [P, NT], F32)
            eq = sb("eq", [P, NT, E], F32)
            hot = sb("hot", [P, NT, E], F32)
            hotb = sb("hotb", [P, NT, E], BF16)
            rank = sb("rank", [P, E], F32)
            before = sb("before", [P, P], BF16)
            ones = sb("ones", [P, P], BF16)
            onesf = sb("onesf", [P, NT], F32)
            run = sb("run", [P, NT, E], F32)
            slot = sb("slot", [P, NT, E], F32)
            padi = sb("padi", [P, E], I32)
            padf = sb("padf", [P, E], F32)
            ends = sb("ends", [P, E], F32)
            offs = sb("offs", [P, E], F32)
            posf = sb("posf", [P, NT], F32)
            posi = sb("posi", [P, NT], I32)
            tilef = sb("tilef", [P, NT], F32)
            inf = sb("inf", [P, NT], F32)
            cols = sb("cols", [P, max(P, NS_T)], F32)
            rowf = sb("rowf", [P, 1], F32)
            in_tile = sb("in_tile", [P, NT, NS_T], BF16)
            token = sb("token", [P, NT, 2, NS_T], BF16)
            in_row = sb("in_row", [P, NT, P], BF16)
            holder = sb("holder", [P, NS_T], F32)
            fetch = sb("fetch", [P, NS_T + 2 * BLK // P], F32)
            target = sb("target", [P, NS_T], F32)
            starts = sb("starts", [1, NB], F32)
            past = sb("past", [1, NB, E], F32)
            expf = sb("expf", [1, NB], F32)
            block_expert = sb("block_expert", [1, NB], I32)
            used = sb("used", [1, 1], I32)
            psR = ps("psR", [P, 2, NT, E])

            r_const = sem("r_const")
            r_hot = sem("r_hot")
            r_count = sem("r_count")
            r_step = sem("r_step")
            r_tok = sem("r_tok")
            r_holder = sem("r_holder")
            r_table = sem("r_table")
            r_blocks = sem("r_blocks")

            F1, F2 = w1.shape[2], w2.shape[2]
            M1, M2 = F1 // P, F2 // P
            RT = BLK // P
            KG = 2
            G2 = M1 // KG
            NG = M1 + M2
            RG = 4
            stage = sb("stage", [P, DC * F1 + M1 * F2 + M2 * D], F32)
            at2, at3, end = DC * F1, DC * F1 + M1 * F2, DC * F1 + M1 * F2 + M2 * D
            w1s = stage[:, 0:at2].rearrange("p (c n) -> p c n", c=DC)
            w2s = stage[:, at2:at3].rearrange("p (c n) -> p c n", c=M1)
            w3s = stage[:, at3:end].rearrange("p (c n) -> p c n", c=M2)
            w1h, w1l = sb("w1h", [P, DC, F1], F32R), sb("w1l", [P, DC, F1], F32R)
            w2h, w2l = sb("w2h", [P, M1, F2], F32R), sb("w2l", [P, M1, F2], F32R)
            w3h, w3l = sb("w3h", [P, M2, D], F32R), sb("w3l", [P, M2, D], F32R)
            b12s = sb("b12s", [P, E, NG], F32)
            b3s = sb("b3s", [P, E, D], F32)
            hrow = sb("hrow", [P, RT, D], F32)
            hh, hl = sb("hh", [P, DC, BLK], F32R), sb("hl", [P, DC, BLK], F32R)
            gr = sb("gr", [P, RG, BLK], F32)
            g1h, g1l = sb("g1h", [P, M1, BLK], F32R), sb("g1l", [P, M1, BLK], F32R)
            g2h, g2l = sb("g2h", [P, M2, BLK], F32R), sb("g2l", [P, M2, BLK], F32R)
            xg = sb("xg", [P, RT, 2 * D], F32)
            yrow = sb("yrow", [P, RT, D], F32)
            gap = sb("gap", [P, 1], F32)
            ih = sb("ih", [P, RT], U32)
            ix = sb("ix", [P, RT], U32)
            io = sb("io", [P, RT], U32)
            psT = ps("psT", [P, DC, BLK])
            ps1 = ps("ps1", [P, 2, 2, BLK])
            ps2 = ps("ps2", [P, M2, L])
            ps3 = psR[:].rearrange("p k t e -> p (k t e)").rearrange("p (r d) -> p r d", r=RT)

            f_b12 = sem("f_b12")
            f_b3 = sem("f_b3")
            f_h = sem("f_h")
            f_w1 = sem("f_w1")
            f_w2 = [sem(f"f_w2_{c}") for c in range(G2)]
            f_w3 = sem("f_w3")
            f_w1h = sem("f_w1h")
            f_w1l = sem("f_w1l")
            f_w2h = sem("f_w2h")
            f_w2l = sem("f_w2l")
            f_w3h = sem("f_w3h")
            f_w3l = sem("f_w3l")
            f_t = sem("f_t")
            f_hh = sem("f_hh")
            f_hl = sem("f_hl")
            f_l1 = sem("f_l1")
            f_k2 = sem("f_k2")
            f_l2 = sem("f_l2")
            f_l3 = sem("f_l3")
            f_gelu = sem("f_gelu")
            f_gh = sem("f_gh")
            f_gl = sem("f_gl")
            f_y = sem("f_y")
            f_st = sem("f_st")
            f_ih = sem("f_ih")
            f_ix = sem("f_ix")
            f_io = sem("f_io")
            f_gap = sem("f_gap")
            f_x = sem("f_x")
            f_ys = sem("f_ys")

            w1_v = w1.rearrange("e (c p) n -> e p c n", p=P)
            w2_v = w2.rearrange("e (c p) n -> e p c n", p=P)
            w3_v = w3.rearrange("e (c p) n -> e p c n", p=P)
            out_rows = out.rearrange("b l d -> (b l) d")

            def one(view, i):
                return view[bass.ds(i, 1)].rearrange("a p c n -> (a p) c n")

            def blocks(eng, body):
                body(0, False)
                with eng.Fori(1, FULL) as j:
                    body(j, False)
                n = eng.value_load(used[0:1, 0:1], min_val=FULL, max_val=NB)
                with eng.Fori(FULL, NB - 1) as j:
                    with eng.If(j < n):
                        body(j, False)
                with eng.If(NB - 1 < n):
                    body(NB - 1, True)
                return n

            def for_expert(eng, j, work, kept):
                if isinstance(j, int) and j == 0:
                    work(j)
                    return
                e = eng.value_load(block_expert[0:1, bass.ds(j, 1)], min_val=0, max_val=E - 1)
                old = eng.value_load(block_expert[0:1, bass.ds(j - 1, 1)], min_val=0, max_val=E - 1)
                with eng.If(e != old):
                    work(j)
                with eng.If(e == old):
                    for s_kept, n in kept:
                        eng.wait_ge(s_kept, j * n)
                        eng.sem_inc(s_kept, n)

            with nc.Block() as block:
                @block.sync
                def _(sp):
                    def load_weights(j):
                        e = sp.value_load(block_expert[0:1, bass.ds(j, 1)], min_val=0, max_val=E - 1)
                        wait(sp, f_w1l, j * DC)
                        sp.dma_start(w1s, one(w1_v, e)).then_inc(f_w1, 16)
                        for c in range(G2):
                            wait(sp, f_w2l, (j - 1) * G2 + c + 1)
                            group = slice(c * KG, (c + 1) * KG)
                            sp.dma_start(w2s[:, group, :], one(w2_v, e)[:, group, :]).then_inc(f_w2[c], 16)
                        wait(sp, f_w3l, j)
                        sp.dma_start(w3s, one(w3_v, e)).then_inc(f_w3, 16)

                    def load_expert(j):
                        for_expert(sp, j, load_weights, [(s_w, 16) for s_w in [f_w1, f_w3] + f_w2])

                    sp.dma_start(b12s[:], b12.rearrange("e p n -> p e n")).then_inc(f_b12, 16)
                    sp.dma_start(b3s[:].rearrange("p e d -> p (e d)"),
                                 b3.rearrange("e d -> (e d)").partition_broadcast(P)).then_inc(f_b3, 16)
                    sp.wait_ge(r_blocks, 2)
                    load_expert(0)
                    sp.wait_ge(f_h, RT * 16)

                    def body(j, last):
                        if not last:
                            load_expert(j + 1)
                    blocks(sp, body)

                @block.gpsimd
                def _(pool):
                    pool.memset(before[:], 1.0).then_inc(r_const, 1)
                    pool.memset(ones[:], 1.0).then_inc(r_const, 1)
                    pool.memset(onesf[:], 1.0).then_inc(r_const, 1)
                    pool.memset(fetch[:], 0.0).then_inc(r_const, 1)
                    pool.iota(rank[:], pattern=[[-1, E]], base=E, channel_multiplier=0,
                              allow_small_or_imprecise_dtypes=True).then_inc(r_const, 1)
                    pool.iota(cols[:], pattern=[[1, max(P, NS_T)]], base=0, channel_multiplier=0,
                              allow_small_or_imprecise_dtypes=True).then_inc(r_const, 1)
                    pool.iota(rowf[:], pattern=[[1, 1]], base=1, channel_multiplier=1,
                              allow_small_or_imprecise_dtypes=True).then_inc(r_const, 1)
                    pool.iota(starts[:], pattern=[[BLK, NB]], base=0, channel_multiplier=0,
                              allow_small_or_imprecise_dtypes=True).then_inc(r_const, 1)
                    pool.wait_ge(r_const, 8)
                    pool.affine_select(out=before[:], in_=before[:], compare_op=ALU.is_gt, fill=0.0, base=0,
                                       pattern=[[1, P]], channel_multiplier=-1).then_inc(r_const, 1)

                    def gather(dst, src, index, done):
                        for r in range(RT):
                            pool.indirect_dma_start(dst[:, r, :], None, src,
                                                    bass.IndirectOffsetOnAxis(ap=index[:, r:r + 1], axis=0)
                                                    ).then_inc(done, 16)

                    def scatter():
                        for r in range(RT):
                            pool.indirect_dma_start(out_rows, bass.IndirectOffsetOnAxis(ap=io[:, r:r + 1], axis=0),
                                                    yrow[:, r, :], None, bounds_check=NT * P - 1,
                                                    oob_is_err=False).then_inc(f_st, 16)

                    def w2_low(j, groups=range(G2)):
                        for c in groups:
                            group = slice(c * KG, (c + 1) * KG)
                            wait(pool, f_w2h, j * G2 + c + 1)
                            pool.tensor_tensor(w2l[:, group, :], w2s[:, group, :], w2h[:, group, :],
                                               ALU.subtract).then_inc(f_w2l, 1)

                    pool.wait_ge(r_blocks, 2)
                    w2_low(0, range(2))
                    pool.wait_ge(f_ih, 1)
                    gather(hrow, h2_d, ih, f_h)
                    w2_low(0, range(2, G2))
                    pool.wait_ge(f_ih, 2)
                    pool.wait_ge(f_t, 1)
                    gather(hrow, h2_d, ih, f_h)

                    def step_aside(done):
                        wait(pool, f_gap, done)
                        pool.tensor_tensor(gap[0:1, :], ones[0:1, 0:1], ones[0:1, 0:1],
                                           ALU.subtract).then_inc(f_gap, 1)

                    def body(j, last):
                        wait(pool, f_y, j)
                        wait(pool, f_ix, j + 1)
                        step_aside(3 * j)
                        gather(xg, x2_d, ix, f_x)
                        if not last:
                            for_expert(pool, j + 1, w2_low, [(f_w2l, G2)])
                        wait(pool, f_t, j + 1 if last else j + 2)
                        wait(pool, f_ih, j + 3)
                        step_aside(3 * j + 1)
                        gather(hrow, h2_d, ih, f_h)
                        wait(pool, f_io, j + 1)
                        wait(pool, f_y, j + 1)
                        step_aside(3 * j + 2)
                        scatter()
                    n = blocks(pool, body)
                    pool.wait_ge(f_st, n * RT * 16)
                    pool.wait_ge(f_h, (n + 2) * RT * 16)

                @block.tensor
                def _(pe):
                    pe.wait_ge(r_const, 9)
                    pe.wait_ge(r_hot, 1)
                    flat = hotb[:].rearrange("p t e -> p (t e)")
                    pe.matmul(psR[:, 0].rearrange("p t e -> p (t e)"), before[:], flat, start=True, stop=True)
                    pe.matmul(psR[:, 1].rearrange("p t e -> p (t e)"), ones[:], flat, start=True,
                              stop=True).then_inc(r_count, 1)
                    for t in range(NT):
                        if t % QT == 0:
                            pe.wait_ge(r_tok, 2 + t // QT + 1)
                        mm = pe.matmul(psT[:, 0, 0:2 * NS_T], in_row[:, t, :],
                                       token[:, t].rearrange("p k s -> p (k s)"), start=(t == 0), stop=(t == NT - 1))
                    mm.then_inc(r_holder, 1)

                    def product(dst, lhs, rhs, first, last):
                        (lhi, llo), (rhi, rlo) = lhs, rhs
                        pe.matmul(dst, lhi, rhi, start=first, stop=False)
                        pe.matmul(dst, lhi, rlo, start=False, stop=False)
                        return pe.matmul(dst, llo, rhi, start=False, stop=last)

                    def turn_rows(j):
                        wait(pe, f_h, (j + 1) * RT * 16)
                        wait(pe, f_hl, j)
                        for c in range(DC):
                            for r in range(RT):
                                mm = pe.transpose(psT[:, c, r * P:(r + 1) * P], hrow[:, r, c * P:(c + 1) * P], ident[:])
                        mm.then_inc(f_t, 1)

                    def layer1(j):
                        wait(pe, f_w1l, (j + 1) * DC)
                        wait(pe, f_hl, j + 1)
                        for m in range(M1):
                            if m % 2 == 0:
                                wait(pe, f_gelu, j * NG + m - 2 if m >= 4 else (j - 1) * NG + m + M1 - 2)
                            cols = slice(m * P, (m + 1) * P)
                            for c in range(DC):
                                mm = product(ps1[:, m // 2 % 2, m % 2, :], (w1h[:, c, cols], w1l[:, c, cols]),
                                             (hh[:, c, :], hl[:, c, :]), c == 0, c == DC - 1)
                            if m % 2:
                                mm.then_inc(f_l1, 1)

                    def layer2(j, last):
                        wait(pe, f_gelu, j * NG)
                        for k in range(M1):
                            if k == M1 // 2 and not last:
                                turn_rows(j + 1)
                            if k % KG == 0:
                                wait(pe, f_w2l, j * G2 + k // KG + 1)
                            wait(pe, f_gl, j * NG + k + 1)
                            for m in range(M2):
                                cols = slice(m * P, (m + 1) * P)
                                mm = product(ps2[:, m, 0:BLK], (w2h[:, k, cols], w2l[:, k, cols]),
                                             (g1h[:, k, :], g1l[:, k, :]), k == 0, k == M1 - 1)
                                if k == M1 - 1:
                                    mm.then_inc(f_l2, 1)
                            if k % KG == KG - 1 and k < M1 - 1:
                                mm.then_inc(f_k2, 1)

                    def layer3(j):
                        wait(pe, f_w3l, j + 1)
                        wait(pe, f_y, j)
                        wait(pe, f_gl, (j + 1) * NG)
                        for r in range(RT):
                            rows = slice(r * P, (r + 1) * P)
                            for k in range(M2):
                                mm = product(ps3[:, r, :], (g2h[:, k, rows], g2l[:, k, rows]),
                                             (w3h[:, k, :], w3l[:, k, :]), k == 0, k == M2 - 1)
                        mm.then_inc(f_l3, 1)

                    pe.wait_ge(r_blocks, 2)
                    pe.wait_ge(r_table, 2)
                    turn_rows(0)
                    layer1(0)

                    def body(j, last):
                        layer2(j, last)
                        if not last:
                            layer1(j + 1)
                        layer3(j)
                    blocks(pe, body)

                @block.scalar
                def _(act):
                    def w1_high(j):
                        wait(act, f_l1, j * (M1 // 2))
                        wait(act, f_w1, (j + 1) * 16)
                        for c in range(DC):
                            act.activation(w1h[:, c, :], w1s[:, c, :], ACT.Copy).then_inc(f_w1h, 1)

                    def w2_high(j, groups):
                        for c in groups:
                            if c < G2 - 1:
                                wait(act, f_k2, (j - 1) * (G2 - 1) + c + 1)
                            else:
                                wait(act, f_l2, j * M2)
                            wait(act, f_w2[c], (j + 1) * 16)
                            group = slice(c * KG, (c + 1) * KG)
                            act.activation(w2h[:, group, :], w2s[:, group, :], ACT.Copy).then_inc(f_w2h, 1)

                    def high(j):
                        w1_high(j)
                        w2_high(j, range(G2 - 1))

                    def expert(j):
                        return act.value_load(block_expert[0:1, bass.ds(j, 1)], min_val=0, max_val=E - 1)

                    def bias(e, m):
                        return b12s[:].rearrange("p e n -> p (e n)")[:, bass.ds(e * NG + m, 1)]

                    def rest_high(j):
                        w2_high(j, [G2 - 1])

                    def gelu1(j, e):
                        for m in range(M1):
                            wait(act, f_l1, j * (M1 // 2) + m // 2 + 1)
                            wait(act, f_gl, j * NG + m - RG + 1)
                            act.activation(gr[:, m % RG, :], ps1[:, m // 2 % 2, m % 2, :], ACT.Gelu,
                                           bias=bias(e, m)).then_inc(f_gelu, 1)

                    def gelu2(j, e):
                        for m in range(M2):
                            wait(act, f_l2, j * M2 + m + 1)
                            wait(act, f_gl, j * NG + M1 + m - RG + 1)
                            act.activation(gr[:, (M1 + m) % RG, :], ps2[:, m, 0:BLK], ACT.Gelu,
                                           bias=bias(e, M1 + m)).then_inc(f_gelu, 1)

                    act.wait_ge(r_blocks, 2)
                    high(0)
                    rest_high(0)
                    act.wait_ge(f_b12, 16)
                    gelu1(0, expert(0))

                    def body(j, last):
                        e = expert(j)
                        if not last:
                            e_next = expert(j + 1)
                        if not last:
                            for_expert(act, j + 1, high, [(f_w1h, DC)])
                        gelu2(j, e)
                        if not last:
                            for_expert(act, j + 1, rest_high, [(f_w2h, G2)])
                            gelu1(j + 1, e_next)
                    blocks(act, body)

                @block.vector
                def _(dve):
                    def w1_low(j):
                        for c in range(DC):
                            wait(dve, f_w1h, j * DC + c + 1)
                            dve.tensor_tensor(w1l[:, c, :], w1s[:, c, :], w1h[:, c, :], ALU.subtract).then_inc(f_w1l, 1)

                    def split_w3(j):
                        wait(dve, f_w3, (j + 1) * 16)
                        wait(dve, f_l3, j)
                        dve.tensor_copy(w3h[:], w3s).then_inc(f_w3h, 1)
                        wait(dve, f_w3h, j + 1)
                        dve.tensor_tensor(w3l[:], w3s, w3h[:], ALU.subtract).then_inc(f_w3l, 1)

                    steps = [0]

                    def step(ins):
                        steps[0] += 1
                        ins.then_inc(r_step, 1)
                        dve.wait_ge(r_step, steps[0])

                    def along(ap, n=NT):
                        return ap.rearrange("p (a s) -> p a s", a=1).broadcast_to([P, n, ap.shape[1]])

                    def over(ap, m, n=NT):
                        return ap.rearrange("p (t a) -> p t a", a=1).broadcast_to([P, n, m])

                    def per_tile(ap):
                        return ap[:].rearrange("p (t a) -> p t a", a=1).broadcast_to([P, NT, E])

                    def per_expert(ap):
                        return ap[:].rearrange("p (a e) -> p a e", a=1).broadcast_to([P, NT, E])

                    dve.wait_ge(r_const, 8)
                    step(dve.tensor_reduce(mx[:], logits[:], AX_X, ALU.max))
                    step(dve.tensor_tensor(eq[:], logits[:], per_tile(mx), ALU.is_equal))
                    step(dve.tensor_tensor(eq[:], eq[:], per_expert(rank), ALU.mult))
                    step(dve.tensor_reduce(mx[:], eq[:], AX_X, ALU.max))
                    step(dve.tensor_tensor(hot[:], eq[:], per_tile(mx), ALU.is_equal))
                    dve.tensor_copy(hotb[:], hot[:]).then_inc(r_hot, 1)
                    dve.wait_ge(r_count, 1)
                    for e in range(E):
                        last = dve.tensor_tensor_scan(out=run[:, :, e], data0=onesf[:], data1=psR[:, 1, :, e],
                                                      initial=0.0, op0=ALU.mult, op1=ALU.add)
                    step(last)
                    step(dve.tensor_scalar(padi[:], run[:, NT - 1, :], float(BLK - 1), None, ALU.add))
                    step(dve.tensor_scalar(padi[:], padi[:], BLK_BITS, BLK_BITS, ALU.arith_shift_right,
                                           ALU.arith_shift_left))
                    step(dve.tensor_copy(padf[:], padi[:]))
                    step(dve.tensor_tensor_scan(out=ends[:], data0=onesf[:, 0:E], data1=padf[:], initial=0.0,
                                                op0=ALU.mult, op1=ALU.add))
                    step(dve.tensor_tensor(past[:], starts[:].rearrange("p (b a) -> p b a", a=1).broadcast_to([1, NB, E]),
                                           ends[0:1, :].rearrange("p (a e) -> p a e", a=1).broadcast_to([1, NB, E]),
                                           ALU.is_ge))
                    step(dve.tensor_reduce(expf[:], past[:], AX_X, ALU.add))
                    dve.tensor_scalar(block_expert[:], expf[:], float(E - 1), None, ALU.min).then_inc(r_blocks, 1)
                    dve.tensor_scalar(used[:], ends[0:1, E - 1:E], 1.0 / BLK, None, ALU.mult).then_inc(r_blocks, 1)
                    step(dve.tensor_tensor(offs[:], ends[:], padf[:], ALU.subtract))
                    step(dve.tensor_tensor(slot[:], run[:], psR[:, 1], ALU.subtract))
                    step(dve.tensor_tensor(slot[:], slot[:], psR[:, 0], ALU.add))
                    step(dve.tensor_tensor(slot[:], slot[:], per_expert(offs), ALU.add))
                    step(dve.tensor_tensor(slot[:], slot[:], hot[:], ALU.mult))
                    step(dve.tensor_reduce(posf[:], slot[:], AX_X, ALU.add))
                    step(dve.tensor_copy(posi[:], posf[:]))
                    step(dve.tensor_scalar(posi[:], posi[:], P_BITS, None, ALU.arith_shift_right))
                    step(dve.tensor_copy(tilef[:], posi[:]))
                    step(dve.scalar_tensor_tensor(out=inf[:], in0=tilef[:], scalar=-float(P), in1=posf[:],
                                                  op0=ALU.mult, op1=ALU.add))
                    step(dve.tensor_tensor(in_tile[:], along(cols[:, 0:NS_T]), over(tilef[:], NS_T), ALU.is_equal))
                    dve.tensor_tensor(token[:, :, 0, :], in_tile[:], over(cols[:, 0:NT], NS_T),
                                      ALU.mult).then_inc(r_tok, 1)
                    dve.tensor_scalar(token[:, :, 1, :], in_tile[:], rowf[:, 0:1], None, ALU.mult).then_inc(r_tok, 1)
                    for k in range(NT // QT):
                        part = slice(k * QT, (k + 1) * QT)
                        dve.tensor_tensor(in_row[:, part, :], along(cols[:, 0:P], QT), over(inf[:, part], P, QT),
                                          ALU.is_equal).then_inc(r_tok, 1)
                    w1_low(0)
                    dve.wait_ge(r_holder, 1)
                    held = psT[:, 0, 0:2 * NS_T].rearrange("p (k s) -> p k s", k=2)
                    step(dve.tensor_copy(holder[:], held[:, 1, :]))
                    step(dve.scalar_tensor_tensor(out=holder[:], in0=held[:, 0, :], scalar=float(P), in1=holder[:],
                                                  op0=ALU.mult, op1=ALU.add))
                    dve.tensor_scalar(fetch[:, 0:NS_T], holder[:], 1.0, 0.0, ALU.subtract, ALU.max).then_inc(r_table, 1)
                    step(dve.tensor_scalar(target[:], holder[:], 0.0, NOWHERE, ALU.is_equal, ALU.mult))
                    step(dve.tensor_tensor(target[:], target[:], holder[:], ALU.add))
                    dve.tensor_scalar(target[:], target[:], 1.0, None, ALU.subtract).then_inc(r_table, 1)
                    dve.wait_ge(r_table, 2)

                    def split_rows(j):
                        wait(dve, f_t, j + 1)
                        wait(dve, f_l1, j * (M1 // 2))
                        dve.tensor_copy(hh[:], psT[:]).then_inc(f_hh, 1)
                        wait(dve, f_hh, j + 1)
                        dve.tensor_tensor(hl[:], psT[:], hh[:], ALU.subtract).then_inc(f_hl, 1)

                    def split_gelus(j, at, hi, lo, n):
                        for m in range(n):
                            wait(dve, f_gelu, j * NG + at + m + 1)
                            dve.tensor_copy(hi[:, m, :], gr[:, (at + m) % RG, :]).then_inc(f_gh, 1)
                            wait(dve, f_gh, j * NG + at + m + 1)
                            dve.tensor_tensor(lo[:, m, :], gr[:, (at + m) % RG, :], hi[:, m, :],
                                              ALU.subtract).then_inc(f_gl, 1)

                    def indices(j, dst, src, done):
                        dve.tensor_copy(dst[:], src[:, bass.ds(j * RT, RT)]).then_inc(done, 1)

                    def result(j, e):
                        wait(dve, f_st, j * RT * 16)
                        indices(j, io, target, f_io)
                        wait(dve, f_l3, j + 1)
                        dve.tensor_tensor(yrow[:], ps3, b3s[:, bass.ds(e, 1), :].broadcast_to([P, RT, D]),
                                          ALU.add).then_inc(f_ys, 1)
                        wait(dve, f_x, (j + 1) * RT * 16)
                        wait(dve, f_ys, 2 * j + 1)
                        dve.tensor_tensor(yrow[:], yrow[:], xg[:, :, D:], ALU.mult).then_inc(f_ys, 1)
                        wait(dve, f_ys, 2 * j + 2)
                        dve.tensor_tensor(yrow[:], yrow[:], xg[:, :, 0:D], ALU.add).then_inc(f_y, 1)

                    dve.wait_ge(f_b3, 16)
                    indices(0, ih, fetch, f_ih)
                    dve.wait_ge(r_blocks, 2)
                    split_w3(0)
                    wait(dve, f_h, RT * 16)
                    indices(1, ih, fetch, f_ih)
                    split_rows(0)
                    split_gelus(0, 0, g1h, g1l, M1)

                    def body(j, last):
                        e = dve.value_load(block_expert[0:1, bass.ds(j, 1)], min_val=0, max_val=E - 1)
                        wait(dve, f_h, (j + 2) * RT * 16)
                        indices(j + 2, ih, fetch, f_ih)
                        wait(dve, f_x, j * RT * 16)
                        indices(j, ix, fetch, f_ix)
                        if not last:
                            for_expert(dve, j + 1, w1_low, [(f_w1l, DC)])
                            split_rows(j + 1)
                        split_gelus(j, M1, g2h, g2l, M2)
                        if not last:
                            split_gelus(j + 1, 0, g1h, g1l, M1)
                        result(j, e)
                        if not last:
                            for_expert(dve, j + 1, split_w3, [(f_w3h, 1), (f_w3l, 1)])
                    blocks(dve, body)


_INS = ["x_in", "in_wT", "conv_w", "conv_b", "xp_wT", "dt_wT", "dt_b", "a_log", "d_skip", "out_wT",
        "wr", "br", "w1", "b12", "w2", "w3", "b3", "cT", "wmod"]


def kernel(L0_attn_hidden_states, L0_attn_in_proj_w, L0_attn_conv_w, L0_attn_conv_b, L0_attn_x_proj_w,
           L0_attn_dt_proj_w, L0_attn_dt_proj_b, L0_attn_A_log, L0_attn_Dskip, L0_attn_out_proj_w,
           L0_ffn_Wr, L0_ffn_br, L0_ffn_W1, L0_ffn_b1, L0_ffn_W2, L0_ffn_b2, L0_ffn_W3, L0_ffn_b3,
           L0_c, L0_wmod):
    import numpy as np
    import concourse.bacc as bacc
    from concourse.bass_utils import run_bass_kernel_spmd

    ac = lambda a: np.ascontiguousarray(np.asarray(a))
    H = 4
    ch = lambda a: ac(np.asarray(a).reshape(H, P, *np.asarray(a).shape[1:]).swapaxes(0, 1))
    b1 = np.asarray(L0_ffn_b1)
    b2 = np.asarray(L0_ffn_b2)
    E = b1.shape[0]
    data = dict(
        x_in=ac(L0_attn_hidden_states),
        in_wT=ac(np.asarray(L0_attn_in_proj_w).T),
        conv_w=ch(np.asarray(L0_attn_conv_w)[:, 0, :]),
        conv_b=ch(L0_attn_conv_b),
        xp_wT=ac(np.asarray(L0_attn_x_proj_w).reshape(H, -1, P).transpose(2, 0, 1)),
        dt_wT=ac(np.asarray(L0_attn_dt_proj_w).T),
        dt_b=ch(L0_attn_dt_proj_b),
        a_log=ch(L0_attn_A_log),
        d_skip=ch(L0_attn_Dskip),
        out_wT=ac(np.asarray(L0_attn_out_proj_w).T),
        wr=ac(np.asarray(L0_ffn_Wr).reshape(-1, P, E).swapaxes(0, 1)),
        br=ac(L0_ffn_br),
        w1=ac(L0_ffn_W1),
        b12=ac(np.concatenate([b1.reshape(E, -1, P), b2.reshape(E, -1, P)], axis=1).transpose(0, 2, 1)),
        w2=ac(L0_ffn_W2),
        w3=ac(L0_ffn_W3),
        b3=ac(L0_ffn_b3),
        cT=ac(np.asarray(L0_c).T.reshape(-1, P, L0_c.shape[0]).swapaxes(0, 1)),
        wmod=ac(L0_wmod),
    )
    nc = bacc.Bacc("TRN2", target_bir_lowering=False, num_devices=1)
    args = [nc.dram_tensor(f"in_{n}", data[n].shape, mybir.dt.from_np(data[n].dtype), kind="ExternalInput").ap()
            for n in _INS]
    o = nc.dram_tensor("out", data["x_in"].shape, F32, kind="ExternalOutput").ap()
    build(nc, *args, o)
    r = run_bass_kernel_spmd(nc, [{f"in_{n}": data[n] for n in _INS}], core_ids=[0])
    return r.results[0]["out"]
```
